# Optimizing a Trainium2 kernel written in Bass

```python
import numpy as np
import jax
import jax.numpy as jnp

def _softmax(x, axis=-1):
    return jax.nn.softmax(x, axis=axis)

def _gelu(x):
    return jax.nn.gelu(x, approximate=True)

def _silu(x):
    return jax.nn.silu(x)

def _sigmoid(x):
    return jax.nn.sigmoid(x)

def _layernorm(x, axis=-1, eps=1e-05):
    m = jnp.mean(x, axis=axis, keepdims=True)
    v = jnp.var(x, axis=axis, keepdims=True)
    return (x - m) / jnp.sqrt(v + eps)

def _scatter_add(tgt, idx, src, axis=0):
    return tgt.at[idx].add(src)

def _segment_sum(src, seg, n):
    return jax.ops.segment_sum(src, seg, n)
kernel_name = 'mk_gnn_resnorm_d2_gnn_r8_02f851'

def setup_inputs(seed: int=0):
    np.random.seed(seed)
    _w = jnp.asarray

    def _rec_inputs():
        import jax
        import jax.numpy as jnp
        _gk = jax.random.key(seed)
        x = -8.776e-05 + 1 * jax.random.normal(jax.random.fold_in(_gk, 1), (6250, 128), jnp.float32)
        _s = jax.random.randint(jax.random.fold_in(_gk, 2), (100000,), 0, 6250, jnp.int32)
        _d = jax.random.randint(jax.random.fold_in(_gk, 3), (100000,), 0, 6250, jnp.int32)
        _loop = jnp.arange(6250, dtype=jnp.int32)
        src = jnp.concatenate([_s, _d, _loop])
        dst = jnp.concatenate([_d, _s, _loop])
        _o = jnp.argsort(dst, stable=True)
        src = src[_o]
        dst = dst[_o]
        edge_type_4 = jax.random.randint(jax.random.fold_in(_gk, 12), (206250,), 0, 4, jnp.int32)
        node_type_3 = jax.random.randint(jax.random.fold_in(_gk, 13), (6250,), 0, 3, jnp.int32)
        return (x, src, dst, edge_type_4, node_type_3)
    x, src, dst, edge_type_4, node_type_3 = _rec_inputs()

    def _L0_gnn_setup():
        import jax, jax.numpy as jnp
        import numpy as np
        import math
        N, E, D, T, R, H = (5000, 80000, 128, 3, 4, 8)
        DK = D // H

        def _hgt_forward(node_inp, node_type, edge_index, edge_type, Wk, bk, Wq, bq, Wv, bv, Wa, ba, rel_pri, rel_att, rel_msg, skip, ln_g, ln_b):
            n = node_inp.shape[0]
            out_dim = Wk.shape[2]
            n_heads, d_k = (rel_att.shape[1], rel_att.shape[2])
            sqrt_dk = math.sqrt(d_k)
            rng = jnp.arange(n)

            def type_proj(W, b):
                all_t = jnp.einsum('ni,tio->tno', node_inp, W) + b[:, None, :]
                return all_t[node_type, rng]
            k = type_proj(Wk, bk)
            q = type_proj(Wq, bq)
            v = type_proj(Wv, bv)
            src, dst = (edge_index[0], edge_index[1])
            q_e = q[dst].reshape(-1, n_heads, d_k)
            k_e = k[src].reshape(-1, n_heads, d_k)
            v_e = v[src].reshape(-1, n_heads, d_k)
            k_rot = jnp.zeros_like(k_e)
            msg = jnp.zeros_like(v_e)
            n_rel = rel_att.shape[0]
            for r in range(n_rel):
                m = (edge_type == r)[:, None, None]
                k_rot = k_rot + jnp.where(m, jnp.einsum('ehd,hdf->ehf', k_e, rel_att[r]), 0.0)
                msg = msg + jnp.where(m, jnp.einsum('ehd,hdf->ehf', v_e, rel_msg[r]), 0.0)
            att = (q_e * k_rot).sum(-1) * rel_pri[edge_type] / sqrt_dk
            seg_max = jax.ops.segment_max(att, dst, num_segments=n)
            seg_max = jnp.where(jnp.isfinite(seg_max), seg_max, 0.0)
            ex = jnp.exp(att - seg_max[dst])
            denom = jax.ops.segment_sum(ex, dst, num_segments=n)[dst] + 1e-16
            alpha = ex / denom
            out_e = (msg * alpha[:, :, None]).reshape(-1, out_dim)
            aggr = jax.ops.segment_sum(out_e, dst, num_segments=n)
            h = jax.nn.gelu(aggr, approximate=False)
            trans_all = jnp.einsum('no,top->tnp', h, Wa) + ba[:, None, :]
            trans = trans_all[node_type, rng]
            a = jax.nn.sigmoid(skip)[node_type][:, None]
            res = trans * a + node_inp * (1.0 - a)
            mu = res.mean(-1, keepdims=True)
            var = ((res - mu) ** 2).mean(-1, keepdims=True)
            normed = (res - mu) * jax.lax.rsqrt(var + 1e-05)
            return normed * ln_g[node_type] + ln_b[node_type]
        key = jax.random.key(seed)
        ks = jax.random.split(key, 16)
        glorot = lambda k, shape, fan: jax.random.normal(k, shape, jnp.float32) * math.sqrt(2.0 / fan)
        inp = {'node_inp': jax.random.normal(ks[0], (N, D), jnp.float32), 'node_type': jax.random.randint(ks[1], (N,), 0, T), 'edge_index': jax.random.randint(ks[2], (2, E), 0, N), 'edge_type': jax.random.randint(ks[3], (E,), 0, R), 'Wk': glorot(ks[4], (T, D, D), 2 * D), 'bk': jnp.zeros((T, D), jnp.float32), 'Wq': glorot(ks[5], (T, D, D), 2 * D), 'bq': jnp.zeros((T, D), jnp.float32), 'Wv': glorot(ks[6], (T, D, D), 2 * D), 'bv': jnp.zeros((T, D), jnp.float32), 'Wa': glorot(ks[7], (T, D, D), 2 * D), 'ba': jnp.zeros((T, D), jnp.float32), 'rel_pri': jnp.ones((R, H), jnp.float32), 'rel_att': glorot(ks[8], (R, H, DK, DK), 2 * DK), 'rel_msg': glorot(ks[9], (R, H, DK, DK), 2 * DK), 'skip': jnp.ones((T,), jnp.float32), 'ln_g': jnp.ones((T, D), jnp.float32), 'ln_b': jnp.zeros((T, D), jnp.float32)}
        return inp
    _L0_gnn_all = _L0_gnn_setup()
    _L0_gnn_in = {k: v for k, v in _L0_gnn_all.items() if k in ('Wk', 'bk', 'Wq', 'bq', 'Wv', 'bv', 'Wa', 'ba', 'rel_pri', 'rel_att', 'rel_msg', 'skip', 'ln_g', 'ln_b')}
    del _L0_gnn_all

    def _L1_gnn_setup():
        import jax, jax.numpy as jnp
        import numpy as np
        BN_EPS = 1e-05

        def _batchnorm(h, gamma, beta):
            mean = jnp.mean(h, axis=0)
            var = jnp.mean(jnp.square(h - mean), axis=0)
            return (h - mean) * jax.lax.rsqrt(var + BN_EPS) * gamma + beta
        key = jax.random.key(seed)
        ks = jax.random.split(key, 8)
        N, E, D, H = (12500, 200000, 128, 128)
        x = jax.random.normal(ks[0], (N, D), dtype=jnp.float32)
        edge_index = jax.random.randint(ks[1], (2, E), 0, N, dtype=jnp.int64)
        s = 1.0 / np.sqrt(D)
        return {'x': x, 'edge_index': edge_index, 'eps': jnp.zeros((), dtype=jnp.float32), 'W1': jax.random.uniform(ks[2], (D, H), jnp.float32, -s, s), 'b1': jax.random.uniform(ks[3], (H,), jnp.float32, -s, s), 'g1': jnp.ones((H,), jnp.float32), 'be1': jnp.zeros((H,), jnp.float32), 'W2': jax.random.uniform(ks[4], (H, H), jnp.float32, -s, s), 'b2': jax.random.uniform(ks[5], (H,), jnp.float32, -s, s), 'g2': jnp.ones((H,), jnp.float32), 'be2': jnp.zeros((H,), jnp.float32)}
    _L1_gnn_all = _L1_gnn_setup()
    _L1_gnn_in = {k: v for k, v in _L1_gnn_all.items() if k in ('eps', 'W1', 'b1', 'g1', 'be1', 'W2', 'b2', 'g2', 'be2')}
    del _L1_gnn_all
    return {'x': x, 'src': src, 'dst': dst, 'edge_type_4': edge_type_4, 'node_type_3': node_type_3, 'L0_gnn_Wk': _L0_gnn_in['Wk'], 'L0_gnn_bk': _L0_gnn_in['bk'], 'L0_gnn_Wq': _L0_gnn_in['Wq'], 'L0_gnn_bq': _L0_gnn_in['bq'], 'L0_gnn_Wv': _L0_gnn_in['Wv'], 'L0_gnn_bv': _L0_gnn_in['bv'], 'L0_gnn_Wa': _L0_gnn_in['Wa'], 'L0_gnn_ba': _L0_gnn_in['ba'], 'L0_gnn_rel_pri': _L0_gnn_in['rel_pri'], 'L0_gnn_rel_att': _L0_gnn_in['rel_att'], 'L0_gnn_rel_msg': _L0_gnn_in['rel_msg'], 'L0_gnn_skip': _L0_gnn_in['skip'], 'L0_gnn_ln_g': _L0_gnn_in['ln_g'], 'L0_gnn_ln_b': _L0_gnn_in['ln_b'], 'L1_gnn_eps': _L1_gnn_in['eps'], 'L1_gnn_W1': _L1_gnn_in['W1'], 'L1_gnn_b1': _L1_gnn_in['b1'], 'L1_gnn_g1': _L1_gnn_in['g1'], 'L1_gnn_be1': _L1_gnn_in['be1'], 'L1_gnn_W2': _L1_gnn_in['W2'], 'L1_gnn_b2': _L1_gnn_in['b2'], 'L1_gnn_g2': _L1_gnn_in['g2'], 'L1_gnn_be2': _L1_gnn_in['be2']}

def reference(x, src, dst, edge_type_4, node_type_3, L0_gnn_Wk, L0_gnn_bk, L0_gnn_Wq, L0_gnn_bq, L0_gnn_Wv, L0_gnn_bv, L0_gnn_Wa, L0_gnn_ba, L0_gnn_rel_pri, L0_gnn_rel_att, L0_gnn_rel_msg, L0_gnn_skip, L0_gnn_ln_g, L0_gnn_ln_b, L1_gnn_eps, L1_gnn_W1, L1_gnn_b1, L1_gnn_g1, L1_gnn_be1, L1_gnn_W2, L1_gnn_b2, L1_gnn_g2, L1_gnn_be2):
    import jax
    import jax.numpy as jnp

    def _L0_gnn_ref(node_inp, node_type, edge_index, edge_type, Wk, bk, Wq, bq, Wv, bv, Wa, ba, rel_pri, rel_att, rel_msg, skip, ln_g, ln_b):
        import jax, jax.numpy as jnp
        import numpy as np
        import math
        N, E, D, T, R, H = (5000, 80000, 128, 3, 4, 8)
        DK = D // H

        def _hgt_forward(node_inp, node_type, edge_index, edge_type, Wk, bk, Wq, bq, Wv, bv, Wa, ba, rel_pri, rel_att, rel_msg, skip, ln_g, ln_b):
            n = node_inp.shape[0]
            out_dim = Wk.shape[2]
            n_heads, d_k = (rel_att.shape[1], rel_att.shape[2])
            sqrt_dk = math.sqrt(d_k)
            rng = jnp.arange(n)

            def type_proj(W, b):
                all_t = jnp.einsum('ni,tio->tno', node_inp, W) + b[:, None, :]
                return all_t[node_type, rng]
            k = type_proj(Wk, bk)
            q = type_proj(Wq, bq)
            v = type_proj(Wv, bv)
            src, dst = (edge_index[0], edge_index[1])
            q_e = q[dst].reshape(-1, n_heads, d_k)
            k_e = k[src].reshape(-1, n_heads, d_k)
            v_e = v[src].reshape(-1, n_heads, d_k)
            k_rot = jnp.zeros_like(k_e)
            msg = jnp.zeros_like(v_e)
            n_rel = rel_att.shape[0]
            for r in range(n_rel):
                m = (edge_type == r)[:, None, None]
                k_rot = k_rot + jnp.where(m, jnp.einsum('ehd,hdf->ehf', k_e, rel_att[r]), 0.0)
                msg = msg + jnp.where(m, jnp.einsum('ehd,hdf->ehf', v_e, rel_msg[r]), 0.0)
            att = (q_e * k_rot).sum(-1) * rel_pri[edge_type] / sqrt_dk
            seg_max = jax.ops.segment_max(att, dst, num_segments=n)
            seg_max = jnp.where(jnp.isfinite(seg_max), seg_max, 0.0)
            ex = jnp.exp(att - seg_max[dst])
            denom = jax.ops.segment_sum(ex, dst, num_segments=n)[dst] + 1e-16
            alpha = ex / denom
            out_e = (msg * alpha[:, :, None]).reshape(-1, out_dim)
            aggr = jax.ops.segment_sum(out_e, dst, num_segments=n)
            h = jax.nn.gelu(aggr, approximate=False)
            trans_all = jnp.einsum('no,top->tnp', h, Wa) + ba[:, None, :]
            trans = trans_all[node_type, rng]
            a = jax.nn.sigmoid(skip)[node_type][:, None]
            res = trans * a + node_inp * (1.0 - a)
            mu = res.mean(-1, keepdims=True)
            var = ((res - mu) ** 2).mean(-1, keepdims=True)
            normed = (res - mu) * jax.lax.rsqrt(var + 1e-05)
            return normed * ln_g[node_type] + ln_b[node_type]
        return _hgt_forward(node_inp, node_type, edge_index, edge_type, Wk, bk, Wq, bq, Wv, bv, Wa, ba, rel_pri, rel_att, rel_msg, skip, ln_g, ln_b)

    def _L1_gnn_ref(x, edge_index, eps, W1, b1, g1, be1, W2, b2, g2, be2):
        import jax, jax.numpy as jnp
        import numpy as np
        BN_EPS = 1e-05

        def _batchnorm(h, gamma, beta):
            mean = jnp.mean(h, axis=0)
            var = jnp.mean(jnp.square(h - mean), axis=0)
            return (h - mean) * jax.lax.rsqrt(var + BN_EPS) * gamma + beta
        N = x.shape[0]
        src, dst = (edge_index[0], edge_index[1])
        agg = jax.ops.segment_sum(x[src], dst, num_segments=N)
        h = (1.0 + eps) * x + agg
        h = jax.nn.relu(_batchnorm(h @ W1 + b1, g1, be1))
        h = jax.nn.relu(_batchnorm(h @ W2 + b2, g2, be2))
        return h + x
    edge_index = jnp.stack([src, dst])
    x = _layernorm(x + _L0_gnn_ref(x, node_type_3, edge_index, edge_type_4, L0_gnn_Wk, L0_gnn_bk, L0_gnn_Wq, L0_gnn_bq, L0_gnn_Wv, L0_gnn_bv, L0_gnn_Wa, L0_gnn_ba, L0_gnn_rel_pri, L0_gnn_rel_att, L0_gnn_rel_msg, L0_gnn_skip, L0_gnn_ln_g, L0_gnn_ln_b), axis=-1)
    x = _layernorm(x + _L1_gnn_ref(x, edge_index, L1_gnn_eps, L1_gnn_W1, L1_gnn_b1, L1_gnn_g1, L1_gnn_be1, L1_gnn_W2, L1_gnn_b2, L1_gnn_g2, L1_gnn_be2), axis=-1)
    return x

_drawn_inputs = setup_inputs


def setup_inputs(seed=0):
    import zlib

    import numpy as np

    out = dict(_drawn_inputs(seed))
    spreads = {'L0_gnn_bk': (0.0, 0.354),
     'L0_gnn_bq': (0.0, 0.327),
     'L0_gnn_bv': (0.0, 0.1),
     'L0_gnn_ba': (0.0, 0.1),
     'L0_gnn_rel_pri': (1.0, 0.2),
     'L0_gnn_skip': (1.0, 0.2),
     'L0_gnn_ln_g': (1.0, 0.2),
     'L0_gnn_ln_b': (0.0, 0.1),
     'L1_gnn_g1': (1.0, 0.2),
     'L1_gnn_be1': (0.0, 0.278),
     'L1_gnn_g2': (1.0, 0.2),
     'L1_gnn_be2': (0.0, 0.1)}
    factors = {'L1_gnn_b1': 8.0, 'L1_gnn_b2': 8.0}
    for name, (base, spread) in spreads.items():
        noise = np.random.default_rng([zlib.crc32(name.encode()), seed]).standard_normal(out[name].shape)
        drawn = base * np.exp(spread * noise) if base else spread * noise
        out[name] = jnp.asarray(drawn.astype(out[name].dtype))
    for name, factor in factors.items():
        out[name] = (out[name] * factor).astype(out[name].dtype)
    return out
```

```python
from contextlib import ExitStack

import concourse.bass as bass
from concourse import mybir

F32 = mybir.dt.float32
BF16 = mybir.dt.bfloat16
I32 = mybir.dt.int32
ALU = mybir.AluOpType
ACT = mybir.ActivationFunctionType
AX = mybir.AxisListType

P = 128
HEADS = 8
DK = 16
RELS = 4
TYPES = 3
STEPS = 16
SLOTS = 4
BIG = 1.0e30
LN_EPS = 1e-5
BN_EPS = 1e-5
C_KVROW, C_KEY, C_FIRST, C_LAST, C_HEAD, C_HEADKEY, C_SRC = range(7)
REC = 7 * STEPS
M_EXP, M_MAX, M_KEY = P, P + HEADS, P + 2 * HEADS
SUMW = P + HEADS
ROWW = P + 2 * HEADS + 1


class Chain:

    def __init__(self, eng, sem):
        self.eng, self.sem, self.base, self.n = eng, sem, 0, 0

    def then(self, ins):
        ins.then_inc(self.sem, 1)
        self.n += 1
        self.eng.wait_ge(self.sem, self.base + self.n)

    def enter(self, i, per):
        self.start, self.per = self.base + self.n, per
        self.base, self.n = self.start + i * per, 0

    def leave(self, rounds):
        assert self.n == self.per, (self.n, self.per)
        self.base, self.n = self.start + rounds * self.per, 0


def gnn_kernel(nc, x, src, dst, edge_type, node_type, Wk, bk, Wq, bq, Wv, bv, Wa, ba, rel_pri, rel_att,
               rel_msg, skip, ln_g, ln_b, eps, W1, b1, g1, be1, W2, b2, g2, be2, out):
    N = x.shape[0]
    E = src.shape[0]
    NB = -(-N // P)
    LASTN = N - (NB - 1) * P
    NT = -(-E // P)
    TAIL = NT * P - E
    SG = -(-(NT + NB - 1) // P)
    S = SG * P
    ROUNDS = S // STEPS
    ENTRIES = 2 * S
    LG = ENTRIES // P
    MERGES = 5
    MR = -(-(LG + NB - 1) // MERGES)
    PADNODE = NB * P - 1
    EC = 7
    assert NB % EC == 0 and NB % 2 == 1 and PADNODE >= N and TAIL > 0 and ROUNDS % SLOTS == 0
    NPAD = NB * P
    NCONST = 49
    FULLE = [d for d in range(64, 4000) if E % d == 0][0]

    dram = nc.dram_tensor
    dst_p = dram("dst_p", (NT, P), I32).ap()
    src_p = dram("src_p", (NT, P), I32).ap()
    typ_p = dram("typ_p", (NT, P), I32).ap()
    kvtab = dram("kvtab", (NPAD * RELS, 2 * P), F32).ap()
    rec_d = dram("rec_d", (ROUNDS + 1, P, REC), F32).ap()
    reset_d = dram("reset_d", (S, P), F32).ap()
    blk_d = dram("blk_d", (ROUNDS + 1, STEPS), I32).ap()
    list_d = dram("list_d", (ENTRIES, ROWW), F32).ap()
    x1_d = dram("x1_d", (NPAD, P), F32).ap()

    with ExitStack() as ctx:
        def sb(name, shape, dt=F32):
            return ctx.enter_context(nc.sbuf_tensor(name, shape, dt))[:, :]

        sems = {}

        def sem(name):
            if name not in sems:
                sems[name] = ctx.enter_context(nc.semaphore(name))
            return sems[name]

        bank = [ctx.enter_context(nc.psum_tensor(f"bank{i}", [P, 512], F32))[:, :] for i in range(8)]

        A2 = LG * ROWW
        A3 = A2 + NB * (SUMW + 1)
        AR = max(10 * S, SLOTS * STEPS * 2 * P, A3 + ENTRIES, A3 + EC * (SUMW + P))
        QW = max(NB * 3 * P, 2 * NPAD + 6 * EC * P, 4 * ENTRIES)
        arena = sb("arena", [P, AR])
        X = sb("X", [P, NB * P])
        acc_s = sb("acc", [P, max(NB * SUMW, NPAD + TYPES * P)])
        Qsplit = sb("Qsplit", [P, QW], BF16)
        blks = sb("blks", [1, SLOTS * STEPS], I32)
        hot = sb("hot", [P, 2 * STEPS * P])
        rows = sb("rows", [P, STEPS * ROWW])
        rec = sb("rec", [P, SLOTS * REC])
        resets = sb("resets", [P, SLOTS * (P + 1)])
        prod = sb("prod", [P, 2 * 4 * P])
        att = sb("att", [P, P])
        fwd = sb("fwd", [P, P])
        seg = sb("seg", [P, P])
        shifted = sb("shifted", [P, P])
        hotT = sb("hotT", [P, 16 * P], BF16)
        ends = sb("ends", [P, STEPS * 2 * STEPS])
        listed = sb("listed", [P, SLOTS * ROWW])
        iota_f = sb("iota_f", [P, P])
        iota_i = sb("iota_i", [P, P], I32)
        ident = sb("ident", [P, P])
        identb = sb("identb", [P, P], BF16)
        ones1 = sb("ones1", [1, P])
        Wa_s = sb("Wa_s", [P, TYPES * P])
        pri = sb("pri", [P, RELS])
        W12 = sb("W12", [P, 2 * P])
        bias3 = sb("bias3", [TYPES, 6 * P])
        cols = sb("cols", [P, 8])
        skip_s = sb("skip_s", [P, TYPES])
        ntype_i = sb("ntype_i", [P, NB], I32)
        ntype_f = sb("ntype_f", [P, NB])
        tmask = sb("tmask", [P, TYPES * NB])
        gate = sb("gate", [P, NB])
        tcol = sb("tcol", [TYPES, 1])
        small = sb("small", [P, 3 * SG])
        misc_i = sb("misc_i", [P, SG + 1], I32)
        tile_i = sb("tile_i", [P, SG], I32)
        step_f = sb("step_f", [P, SG])
        stat = sb("stat", [P, 8 * EC + EC * HEADS])
        pcol = sb("pcol", [P, 1])
        ungate = sb("ungate", [P, NB])

        def W(i):
            return arena[:, i * S:(i + 1) * S]

        last_i = W(0)[0:1, 0:NT].bitcast(I32)
        last_b = W(1)[0:1, 0:NT].bitcast(I32)
        start_row = W(2)[0:1, 0:NT]
        tcount = W(3)[0:1, 0:NT]
        tcount_i = W(4)[0:1, 0:NT].bitcast(I32)
        starts = W(5)[:, 0:NT]
        tail_d = W(9)[0:1, 0:P].bitcast(I32)
        tail_z = W(8)[0:1, 0:P].bitcast(I32)
        blkT = prod[0:SG, P:2 * P].bitcast(I32)
        started = W(6)[:, 0:NT]

        types_i = acc_s[0:TYPES, 0:NPAD].bitcast(I32)
        onehot3 = acc_s[0:TYPES, 0:NPAD]
        acc = acc_s[:, 0:NB * SUMW]
        NK = NB - 1

        xm = [hot[:, u * 384:(u + 1) * 384] for u in range(2)]
        xmT = [hot[:, 768 + u * 384:768 + (u + 1) * 384] for u in range(2)]
        kvT = [hot[:, 1536 + u * 256:1536 + (u + 1) * 256] for u in range(2)]
        tab_s = [rows[:, u * 1024:(u + 1) * 1024] for u in range(2)]
        rest = prod[:, 0:P]
        relk, relv = hot[:, 2048:2048 + 512], hot[:, 2560:2560 + 512]
        Wk_s, Wv_s = hot[:, 3072:3072 + 384], hot[:, 3456:3456 + 384]
        Wq_s = acc_s[:, NPAD:NPAD + TYPES * P]
        types_s = hotT.bitcast(F32)[0:TYPES, 0:EC * P]

        rec_s = [hot[:, u * 8 * REC:(u + 1) * 8 * REC] for u in range(2)]
        pad_s = prod[:, 0:REC]

        RING = 4
        rec_slot = [rec[:, u * REC:(u + 1) * REC] for u in range(SLOTS)]
        reset_slot = [resets[:, u * (P + 1):(u + 1) * (P + 1)] for u in range(SLOTS)]
        blk_slot = [blks[:, u * STEPS:(u + 1) * STEPS] for u in range(SLOTS)]
        kv_slot = [arena[:, u * STEPS * 2 * P:(u + 1) * STEPS * 2 * P] for u in range(SLOTS)]
        xg_slot = [arena[:, u * STEPS * P:(u + 1) * STEPS * P] for u in range(SLOTS)]
        rows3 = rows.rearrange("e (t c) -> e t c", c=ROWW)
        hotb = hot.bitcast(BF16)

        def rec_col(u, c):
            return rec_slot[u][:, c * STEPS:(c + 1) * STEPS]

        def hot_step(par, t):
            o = (par * STEPS + t) * P
            return hot[:, o:o + P]

        def hot_step_bf16(par, t):
            o = (par * STEPS + t) * P * 2
            return hotb[:, o + 1:o + 2 * P:2]

        AW = SUMW + 1
        plist = arena[:, 0:A2]
        pl = plist.rearrange("p (g c) -> p g c", c=ROWW)
        acc2 = arena[:, A2:A3]
        Qf = Qsplit.bitcast(F32)
        mT = Qf[0:HEADS, 0:ENTRIES]
        keyT = Qf[0:HEADS, ENTRIES:2 * ENTRIES]
        resets2 = hot[0:HEADS, 0:ENTRIES + 1]
        seg2 = arena[0:HEADS, A3:A3 + ENTRIES]
        G8 = LG * HEADS
        mval, key8, factor, keyf = (rows[:, 0:G8], rows[:, G8:2 * G8], rows[:, 2 * G8:3 * G8],
                                    rows[:, 3 * G8:3 * G8 + LG])
        MS = MR * MERGES
        merge_i = prod[0:1, 512:512 + 2 * MS + LG].bitcast(I32)
        merge_f = prod[:, 0:4 * MS + LG]
        assert 4 * MS + LG <= 512
        mtile_i, mblk_i = merge_i[:, 0:MS], merge_i[:, MS:2 * MS]
        mlast_i = merge_i[:, 2 * MS:2 * MS + LG - 1]
        mstep_f, mtile_f, mblk_f = (merge_f[0:1, j * MS:(j + 1) * MS] for j in range(3))
        mbase = merge_f[:, 3 * MS:4 * MS]
        mstart_f = merge_f[0:1, 4 * MS:4 * MS + LG - 1]
        mcount = arena[0:1, A3:A3 + MS * (LG - 1)]
        assert A3 + max(ENTRIES, MS * (LG - 1)) <= AR and ENTRIES + 1 <= 2 * STEPS * P and 2 * ENTRIES <= Qf.shape[1]

        EW = EC * P
        types2_i = Qf[0:TYPES, 0:NPAD].bitcast(I32)
        onehot3b = Qf[0:TYPES, 0:NPAD]
        hmT = Qf[:, NPAD:NPAD + 3 * EW]
        hm = hot[:, 0:3 * EW]
        square = hot[:, 3 * EW:4 * EW]
        hbuf, res = rows[:, 0:EW], rows[:, EW:2 * EW]
        fin = arena[:, A3:A3 + EC * SUMW]
        kept = arena[:, A3 + EC * SUMW:A3 + EC * SUMW + EW]
        aggT = acc_s[:, 0:NPAD]
        y1 = Qf[:, 0:NPAD]
        y2 = arena[:, SLOTS * STEPS * P:SLOTS * STEPS * P + NPAD]
        CH = [(c, min(c + 512, NPAD)) for c in range(0, NPAD, 512)]
        assert NPAD + 3 * EW <= Qf.shape[1] and SLOTS * STEPS * P + NPAD <= AR

        def blocks(a, i, w=P):
            return a.rearrange("p (b c) -> p b c", c=w)[:, bass.ds(i * EC, EC), :]

        def by_block(a, w=P):
            return a.rearrange("p (b c) -> p b c", c=w)

        def spread(a, n):
            return a.unsqueeze(2).to_broadcast([a.shape[0], a.shape[1], n])

        def load_regs(engine, row, top):
            return nc.values_load_multi_w_load_instructions(
                row, engines=(engine,), min_val=0, max_val=top,
                skip_runtime_bounds_check_because="the schedule is clamped")[1]

        ctx.enter_context(nc.allow_non_contiguous_dma(reason="a few columns of the inputs, once"))
        block = ctx.enter_context(nc.Block())

        @block.sync
        def _(sp):
            cst = sem("consts_loaded")
            for name, a, p in (("dst", dst, dst_p), ("src", src, src_p), ("typ", edge_type, typ_p)):
                flat = p.rearrange("t e -> (t e)")
                sp.dma_start(flat[0:E].rearrange("(a b) -> a b", a=FULLE),
                             a.rearrange("(a b) -> a b", a=FULLE)).then_inc(sem("edges_copied"), 16)
            sp.wait_ge(sem("tails_set"), 2)
            for p, t in ((dst_p, tail_d), (src_p, tail_z), (typ_p, tail_z)):
                flat = p.rearrange("t e -> (t e)")
                sp.dma_start(flat[E:NT * P].unsqueeze(0), t[:, 0:TAIL]).then_inc(sem("edges_copied"), 16)
            sp.dma_start(blk_d[ROUNDS:ROUNDS + 1], tail_z[:, 0:STEPS]).then_inc(sem("edges_copied"), 16)
            sp.wait_ge(sem("edges_copied"), 112)
            sp.dma_start(last_i, dst_p[:, P - 1:P].rearrange("t o -> o t")).then_inc(sem("last_loaded"), 16)
            for s_, w in ((Wk_s, Wk), (Wq_s, Wq), (Wv_s, Wv), (Wa_s, Wa)):
                sp.dma_start(s_.rearrange("i (t o) -> i t o", t=TYPES), w.rearrange("t i o -> i t o")).then_inc(cst, 16)
            for j, b in enumerate((bk, bv, bq, ba, ln_g, ln_b)):
                sp.dma_start(bias3[:, j * P:(j + 1) * P], b).then_inc(cst, 16)
            sp.dma_start(W12[:, 0:P], W1).then_inc(cst, 16)
            sp.dma_start(W12[:, P:2 * P], W2).then_inc(cst, 16)
            for j, b in enumerate((b1, g1, be1, b2, g2, be2)):
                sp.dma_start(cols[:, j:j + 1], b.unsqueeze(1)).then_inc(cst, 16)
            sp.dma_start(cols[:, 6:7], eps.partition_broadcast(P)).then_inc(cst, 16)
            sp.dma_start(skip_s, skip.partition_broadcast(P)).then_inc(cst, 16)
            sp.wait_ge(sem("rels_zeroed"), 1)
            for h in range(HEADS):
                for s_, r in ((relk, rel_att), (relv, rel_msg)):
                    sp.dma_start(s_.rearrange("p (r f) -> p r f", r=RELS)[h * DK:(h + 1) * DK, :, h * DK:(h + 1) * DK],
                                 r[:, h].rearrange("r d f -> d r f")).then_inc(cst, 16)
                sp.dma_start(pri[h * DK:(h + 1) * DK, :], rel_pri[:, h].partition_broadcast(DK)).then_inc(cst, 16)
            sp.wait_ge(sem("nodes_zeroed"), 1)
            sp.dma_start(X[:, 0:NK * P].rearrange("p (b f) -> p b f", f=P),
                         x[0:NK * P, :].rearrange("(b p) f -> p b f", p=P)).then_inc(cst, 16)
            sp.dma_start(X[0:LASTN, NK * P:NB * P], x[NK * P:N, :]).then_inc(cst, 16)
            sp.dma_start(ntype_i[:, 0:NK], node_type[0:NK * P].rearrange("(b p) -> p b", p=P)).then_inc(cst, 16)
            sp.dma_start(ntype_i[0:LASTN, NK:NB], node_type[NK * P:N].unsqueeze(1)).then_inc(cst, 16)
            sp.dma_start(types_i[:, 0:N], node_type.partition_broadcast(TYPES)).then_inc(cst, 16)

            def store_table(b, u, count):
                sp.wait_ge(sem("tabk_copied"), b + 1)
                sp.wait_ge(sem("tabv_copied"), b + 1)
                sp.dma_start(kvtab.rearrange("(n r) f -> n (r f)", r=RELS)[bass.ds(b * P, P), :],
                             tab_s[u]).then_inc(sem(f"tab_stored{u}"), 16)
                sp.wait_ge(sem(f"tab_stored{u}"), 16 * count)
                sp.sem_inc(sem("tab_free"), 1)

            sp.sem_inc(sem("tab_free"), 2)
            with sp.Fori(0, NK // 2) as i:
                for u in range(2):
                    store_table(2 * i + u, u, i + 1)
            store_table(NK, 0, NK // 2 + 1)

            sp.wait_ge(sem("blk_made"), 1)
            sp.dma_start(blk_d[0:ROUNDS].rearrange("(g k) s -> g (k s)", g=SG), blkT[:, :]).then_inc(sem("blk_stored"), 16)
            sp.wait_ge(sem("blk_stored"), 16)
            sp.wait_ge(sem("resets_made"), 1)
            sp.dma_start(reset_d.rearrange("(g s) e -> s g e", s=P),
                         W(4).rearrange("s (g e) -> s g e", g=SG)).then_inc(sem("rec_stored"), 16)
            sp.sem_inc(sem("recs_free"), 2)
            for g in range(SG):
                sp.wait_ge(sem("reca_copied"), g + 1)
                sp.wait_ge(sem("recb_copied"), g + 1)
                sp.dma_start(rec_d[g * 8:(g + 1) * 8].rearrange("k e c -> e k c"),
                             rec_s[g % 2].rearrange("e (k c) -> e k c", c=REC)).then_inc(sem(f"rec_stored{g % 2}"), 16)
                sp.wait_ge(sem(f"rec_stored{g % 2}"), 16 * (g // 2 + 1))
                sp.sem_inc(sem("recs_free"), 1)
            sp.wait_ge(sem("pad_set"), 1)
            sp.dma_start(rec_d[ROUNDS], pad_s).then_inc(sem("rec_stored"), 16)
            sp.wait_ge(sem("rec_stored"), 32)

            def load_blks(k, u, loaded):
                sp.dma_start(blk_slot[u], blk_d[bass.ds(k, 1), :]).then_inc(sem(f"{loaded}{u}"), 16)

            def load_round(k, u):
                load_blks(k, u, "blk_loaded")
                sp.dma_start(rec_slot[u], rec_d[bass.ds(k, 1)].rearrange("o e c -> (o e) c")).then_inc(sem(f"rec_loaded{u}"), 16)
                sp.dma_start(reset_slot[u][:, 0:P], reset_d[bass.ds(k * STEPS, STEPS), :].unsqueeze(1)
                             .to_broadcast([STEPS, HEADS, P])).then_inc(sem(f"reset_loaded{u}"), 16)

            def store_list(k, u):
                sp.wait_ge(sem("list_copied"), k + 1)
                sp.dma_start(list_d[bass.ds(k * 2 * STEPS, 2 * STEPS), :],
                             listed[0:2 * STEPS, u * ROWW:(u + 1) * ROWW]).then_inc(sem("list_stored"), 16)
                sp.wait_ge(sem("list_stored"), 16 * (k + 1))

            sp.wait_ge(sem("resets_zeroed"), 1)
            for u in range(SLOTS):
                load_round(u, u)
            with sp.Fori(0, ROUNDS // SLOTS - 1) as i:
                for u in range(SLOTS):
                    k = SLOTS * i + u
                    sp.wait_ge(sem("acc_done"), RING + STEPS * (k + 1))
                    store_list(k, u)
                    load_round(k + SLOTS, u)
            for u in range(SLOTS):
                k = ROUNDS - SLOTS + u
                sp.wait_ge(sem("acc_done"), RING + STEPS * (k + 1))
                store_list(k, u)
                if u == 0:
                    load_blks(ROUNDS, 0, "blk_loaded")
                    sp.dma_start(rec_slot[0], rec_d[ROUNDS]).then_inc(sem("rec_loaded0"), 16)
            sp.dma_start(plist.rearrange("p (g c) -> p g c", g=LG),
                         list_d.rearrange("(g p) c -> p g c", p=P)).then_inc(sem("list_loaded"), 16)
            sp.wait_ge(sem("keys_merged"), 1)
            sp.dma_start(types2_i[:, 0:N], node_type.partition_broadcast(TYPES)).then_inc(sem("types_loaded"), 16)

            with sp.Fori(0, NB // EC) as i:
                sp.wait_ge(sem("x1_made"), i + 1)
                sp.dma_start(x1_d.rearrange("(b p) f -> p b f", p=P)[:, bass.ds(i * EC, EC), :],
                             X.rearrange("p (b f) -> p b f", f=P)[:, bass.ds(i * EC, EC), :]).then_inc(sem("x1_stored"), 16)
            sp.wait_ge(sem("x1_stored"), 16 * (NB // EC))
            sp.sem_inc(sem("x1_ready"), 1)

            def load_round2(k, u):
                load_blks(k, u, "blk2_loaded")
                sp.dma_start(rec_slot[u], rec_d[bass.ds(k, 1)].rearrange("o e c -> (o e) c")).then_inc(sem(f"rec2_loaded{u}"), 16)

            for u in range(SLOTS):
                load_round2(u, u)
            with sp.Fori(0, ROUNDS // SLOTS - 1) as i:
                for u in range(SLOTS):
                    k = SLOTS * i + u
                    sp.wait_ge(sem("agg_done"), STEPS * (k + 2))
                    load_round2(k + SLOTS, u)
            sp.wait_ge(sem("agg_done"), STEPS * (ROUNDS - SLOTS + 2))
            sp.dma_start(rec_slot[0], rec_d[ROUNDS]).then_inc(sem("rec2_loaded0"), 16)

            def store_out(lo, n, cnt):
                sp.dma_start(out[lo * P:(lo + n) * P, :].rearrange("(b p) f -> p b f", p=P),
                             X.rearrange("p (b f) -> p b f", f=P)[:, lo:lo + n, :]).then_inc(sem("out_stored"), 16)

            for c in range(NB // EC):
                sp.wait_ge(sem("out_made"), c + 1)
                store_out(c * EC, EC if c < NB // EC - 1 else EC - 1, c)
            sp.dma_start(out[NK * P:N, :], X[0:LASTN, NK * P:NB * P]).then_inc(sem("out_stored"), 16)
            sp.wait_ge(sem("out_stored"), 16 * (NB // EC + 1))

        @block.gpsimd
        def _(pool):
            made = sem("patterns_made")
            pool.iota(iota_i, [[1, P]], base=0, channel_multiplier=0).then_inc(made, 1)
            pool.iota(misc_i[:, 0:SG], [[P, SG]], base=0, channel_multiplier=1).then_inc(made, 1)
            pool.iota(misc_i[:, SG:SG + 1], [[0, 1]], base=0, channel_multiplier=1).then_inc(made, 1)
            pool.iota(tcount_i, [[1, NT]], base=1, channel_multiplier=0).then_inc(made, 1)

            def gather(to, table, idx):
                return pool.indirect_dma_start(to, None, table, bass.IndirectOffsetOnAxis(ap=idx, axis=0))

            pool.wait_ge(sem("tiles_made"), 1)
            for g in range(SG):
                for w, table in ((2, dst_p), (3, src_p), (4, typ_p)):
                    gather(W(w)[:, g * P:(g + 1) * P].bitcast(I32), table,
                           tile_i[:, g:g + 1]).then_inc(sem("rows_gathered"), 16)

            pool.wait_ge(sem("tab_free"), NB + 2)

            def gather_kv(u):
                for t in range(STEPS):
                    gather(kv_slot[u][:, t * 2 * P:(t + 1) * 2 * P], kvtab,
                           rec_col(u, C_KVROW).bitcast(I32)[:, t:t + 1]).then_inc(sem(f"kv_loaded{u}"), 16)

            for u in range(SLOTS):
                pool.wait_ge(sem(f"rec_loaded{u}"), 16)
                gather_kv(u)
            with pool.Fori(1, ROUNDS // SLOTS) as i:
                for u in range(SLOTS):
                    pool.wait_ge(sem("msg_ready"), 4 * (SLOTS * (i - 1) + u + 1))
                    pool.wait_ge(sem(f"rec_loaded{u}"), 16 * (i + 1))
                    pool.sem_inc(sem("pool_rounds"), 1)
                    gather_kv(u)

            pool.wait_ge(sem("msg_ready"), 4 * ROUNDS)
            pool.iota(mtile_i, [[1, MS]], base=0, channel_multiplier=0).then_inc(made, 1)
            pool.iota(mlast_i, [[1, LG - 1]], base=1, channel_multiplier=0).then_inc(made, 1)

            pool.wait_ge(sem("x1_ready"), 1)

            def gather_x(u):
                for t in range(STEPS):
                    gather(xg_slot[u][:, t * P:(t + 1) * P], x1_d,
                           rec_col(u, C_SRC).bitcast(I32)[:, t:t + 1]).then_inc(sem(f"xg_loaded{u}"), 16)

            for u in range(SLOTS):
                pool.wait_ge(sem(f"rec2_loaded{u}"), 16)
                gather_x(u)
            with pool.Fori(1, ROUNDS // SLOTS) as i:
                for u in range(SLOTS):
                    pool.wait_ge(sem(f"rec2_loaded{u}"), 16 * (i + 1))
                    pool.sem_inc(sem("pool_rounds"), 1)
                    gather_x(u)

        @block.scalar
        def _(act):
            link = Chain(act, sem("act_chain"))

            def copy(to, of, **kw):
                return act.activation(to, of, ACT.Copy, **kw)

            for c in range(-(-NT // 512)):
                n = min(NT - c * 512, 512)
                act.wait_ge(sem("starts_spread"), c + 1)
                copy(starts[:, c * 512:c * 512 + n], bank[c][:, 0:n]).then_inc(sem("starts_copied"), 1)
            act.wait_ge(sem("consts_loaded"), 16 * NCONST)
            act.activation(skip_s, skip_s, ACT.Sigmoid).then_inc(sem("skip_gated"), 1)

            def copy_xmT(b, u):
                act.wait_ge(sem("xm_turned"), b + 1)
                copy(xmT[u], bank[u][:, 0:384]).then_inc(sem("xmT_copied"), 1)

            def copy_kvT(b, u):
                act.wait_ge(sem("qkv_made"), b + 1)
                copy(kvT[u], bank[2 + u][:, 0:256]).then_inc(sem("kvT_copied"), 1)

            def copy_tabk(b, u):
                act.wait_ge(sem("tab_made"), b + 1)
                act.wait_ge(sem("tab_free"), b + 1)
                copy(tab_s[u].rearrange("p (r c) -> p r c", r=RELS)[:, :, 0:P],
                     bank[4 + u].rearrange("p (r c) -> p r c", r=RELS)).then_inc(sem("tabk_copied"), 1)

            copy_xmT(0, 0)
            with act.Fori(0, NK // 2) as i:
                for u in range(2):
                    b = 2 * i + u
                    copy_kvT(b, u)
                    copy_xmT(b + 1, 1 - u)
                    copy_tabk(b, u)
            copy_kvT(NK, 0)
            copy_tabk(NK, 0)

            for g in range(SG):
                act.wait_ge(sem("reca_turned"), g + 1)
                act.wait_ge(sem("recs_free"), g + 1)
                copy(rec_s[g % 2].rearrange("e (k c s) -> e c k s", c=7, s=STEPS)[:, C_KEY:C_HEAD + 1],
                     bank[g % 2 * 2].rearrange("e (c k s) -> e c k s", c=4, s=STEPS)).then_inc(sem("reca_copied"), 1)

            def copy_hotT(k):
                for q in range(4):
                    act.wait_ge(sem("hot_turned"), 4 * k + q + 1)
                    copy(hotT[:, q * 512:(q + 1) * 512],
                         bank[3 + q % 2].bitcast(BF16)[:, 0:512]).then_inc(sem("hotT_copied"), 1)

            copy_hotT(0)
            with act.Fori(0, ROUNDS // SLOTS) as i:
                for u in range(SLOTS):
                    k = SLOTS * i + u
                    act.wait_ge(sem("shift_turned"), k + 1)
                    act.activation(rows3[:, :, M_EXP:M_EXP + HEADS],
                                   bank[2][:, P:2 * P].rearrange("e (t h) -> e t h", h=HEADS),
                                   ACT.Exp).then_inc(sem("exp_done"), 1)
                    copy_hotT(k + 1)
                    act.wait_ge(sem("ends_summed"), k + 1)
                    copy(listed[0:2 * STEPS, u * ROWW:(u + 1) * ROWW],
                         bank[7][0:2 * STEPS, u % 2 * 256:u % 2 * 256 + ROWW]).then_inc(sem("list_copied"), 1)

            for w, to in ((0, mT), (1, keyT)):
                for c in range(-(-LG // 4)):
                    n = min(LG - 4 * c, 4) * P
                    act.wait_ge(sem("list_turned"), w * (-(-LG // 4)) + c + 1)
                    copy(to[:, c * 512:c * 512 + n], bank[c][0:HEADS, 0:n]).then_inc(sem("list_taken"), 1)
            act.wait_ge(sem("mshift_made"), 1)
            act.activation(mT, mT, ACT.Exp).then_inc(sem("mexp_done"), 1)

            with act.Fori(0, NB // EC) as i:
                act.wait_ge(sem("aggr_made"), i + 1)
                act.activation(hbuf, res, ACT.Gelu).then_inc(sem("gelu_done"), 1)
                for j in range(EC):
                    act.wait_ge(sem("hm_turned"), EC * i + j + 1)
                    copy(hmT[:, j * 384:(j + 1) * 384], bank[j][:, 0:384]).then_inc(sem("hmT_copied"), 1)
                for n in range(2):
                    act.wait_ge(sem("var_made"), 2 * i + n + 1)
                    act.activation(stat[:, 0:EC], stat[:, EC:2 * EC], ACT.Sqrt).then_inc(sem("root_made"), 1)

            for c, (lo, hi) in enumerate(CH):
                act.wait_ge(sem("x1_turned"), c + 1)
                copy(aggT[:, lo:hi], bank[c % 8][:, 0:hi - lo], scale=cols[:, 7:8]).then_inc(sem("agg_begun"), 1)

            for m, y in ((0, y1), (1, y2)):
                for c, (lo, hi) in enumerate(CH):
                    act.wait_ge(sem("lin_made"), m * len(CH) + c + 1)
                    act.activation(y[:, lo:hi], bank[c % 8][:, 0:hi - lo], ACT.Identity,
                                   bias=cols[:, 3 * m:3 * m + 1]).then_inc(sem("lin_copied"), 1)
                act.wait_ge(sem("bvar_made"), m + 1)
                act.activation(stat[:, 0:1], stat[:, 1:2], ACT.Sqrt).then_inc(sem("broot_made"), 1)
                act.wait_ge(sem("bscale_made"), m + 1)
                for lo, hi in CH:
                    act.activation(y[:, lo:hi], y[:, lo:hi], ACT.Relu, bias=stat[:, 3:4],
                                   scale=stat[:, 2:3]).then_inc(sem("relu_done"), 1)
            for c in range(NB // EC):
                act.wait_ge(sem("ovar_made"), c + 1)
                act.activation(stat[:, 0:EC], stat[:, EC:2 * EC], ACT.Sqrt).then_inc(sem("oroot_made"), 1)

        @block.tensor
        def _(pe):
            mm, turn = nc.tensor.matmul, nc.tensor.transpose
            PE_ = mybir.EngineType.PE

            pe.wait_ge(sem("start_made"), 1)
            for c in range(-(-NT // 512)):
                n = min(NT - c * 512, 512)
                mm(bank[c][:, 0:n], ones1, start_row[:, c * 512:c * 512 + n],
                   start=True, stop=True).then_inc(sem("starts_spread"), 1)

            def turn_xm(b, u):
                pe.wait_ge(sem("xm_made"), b + 1)
                for t in range(TYPES):
                    last = turn(bank[u][:, t * P:(t + 1) * P], xm[u][:, t * P:(t + 1) * P], ident)
                last.then_inc(sem("xm_turned"), 1)

            def make_qkv(b, u):
                pe.wait_ge(sem("xmT_copied"), b + 1)
                hot3 = types_s[:, u * P:(u + 1) * P]
                for j, w in enumerate((Wk_s, Wv_s)):
                    o = bank[2 + u][:, j * P:(j + 1) * P]
                    for t in range(TYPES):
                        mm(o, w[:, t * P:(t + 1) * P], xmT[u][:, t * P:(t + 1) * P], start=(t == 0), stop=False)
                    mm(o, bias3[:, j * P:(j + 1) * P], hot3, start=False, stop=True)
                o = bank[2 + u][:, 2 * P:3 * P]
                for t in range(TYPES):
                    mm(o, xmT[u][:, t * P:(t + 1) * P], Wq_s[:, t * P:(t + 1) * P], start=(t == 0), stop=False)
                mm(o, hot3, bias3[:, 2 * P:3 * P], start=False, stop=True).then_inc(sem("qkv_made"), 1)

            def make_tab(b, u):
                pe.wait_ge(sem("kvT_copied"), b + 1)
                mm(bank[4 + u], kvT[u][:, 0:P], relk, start=True, stop=True)
                mm(bank[6 + u], kvT[u][:, P:2 * P], relv, start=True, stop=True).then_inc(sem("tab_made"), 1)

            pe.wait_ge(sem("consts_loaded"), 16 * NCONST)
            pe.wait_ge(sem("masks_made"), 1)
            pe.wait_ge(sem("starts_copied"), -(-NT // 512))
            turn_xm(0, 0)
            with pe.Fori(0, NK // 2) as i:
                for u in range(2):
                    b = 2 * i + u
                    pe.wait_ge(sem("bank_free"), b + 1)
                    make_qkv(b, u)
                    turn_xm(b + 1, 1 - u)
                    make_tab(b, u)
            pe.wait_ge(sem("bank_free"), NK + 1)
            make_qkv(NK, 0)
            make_tab(NK, 0)

            pe.wait_ge(sem("arrays_made"), 1)
            pe.wait_ge(sem("tabk_copied"), NB)
            turn(bank[4][0:SG, 0:P], small[:, SG:2 * SG], ident).then_inc(sem("blk_turned"), 1)
            for g in range(SG):
                if g >= 2:
                    pe.wait_ge(sem("reca_copied"), g - 1)
                    pe.wait_ge(sem("recb_copied"), g - 1)
                for j, w in enumerate((7, 1, 2, 9)):
                    last = turn(bank[g % 2 * 2][:, j * P:(j + 1) * P], W(w)[:, g * P:(g + 1) * P], ident)
                last.then_inc(sem("reca_turned"), 1)
                for j, w in enumerate((3, 8, 6)):
                    last = turn(bank[g % 2 * 2 + 1][:, j * P:(j + 1) * P], W(w)[:, g * P:(g + 1) * P], ident)
                last.then_inc(sem("recb_turned"), 1)

            def turn_hot(k, par):
                for q in range(4):
                    pe.wait_ge(sem("hot_made"), 4 * k + q + 1)
                    if q >= 2:
                        pe.wait_ge(sem("hotT_copied"), 4 * k + q - 1)
                    for t in range(4):
                        last = turn(bank[3 + q % 2].bitcast(BF16)[:, t * P:(t + 1) * P],
                                    hot_step_bf16(par, 4 * q + t), identb)
                    last.then_inc(sem("hot_turned"), 1)

            def spread_q(k, q, regs):
                pe.wait_ge(sem("hotT_copied"), 4 * k + q + 1)
                for t in range(4):
                    for part in range(3):
                        last = mm(bank[q % 2][:, t * P:(t + 1) * P], hotT[:, (4 * q + t) * P:(4 * q + t + 1) * P],
                                  Qsplit[:, bass.ds(regs[4 * q + t] * (3 * P) + part * P, P)],
                                  start=(part == 0), stop=(part == 2))
                last.then_inc(sem("q_spread"), 1)

            pe.wait_ge(sem("blk_loaded0"), 16)
            pe.wait_ge(sem("reca_copied"), SG)
            pe.wait_ge(sem("recb_copied"), SG)
            regs = load_regs(PE_, blk_slot[0][:, 0:STEPS], NB - 1)
            turn_hot(0, 0)
            for q in range(2):
                spread_q(0, q, regs)
            with pe.Fori(0, ROUNDS // SLOTS) as i:
                for u in range(SLOTS):
                    k = SLOTS * i + u
                    regs = load_regs(PE_, blk_slot[u][:, 8:16], NB - 1)
                    for q in (2, 3):
                        pe.wait_ge(sem("q_used"), 4 * k + q - 1)
                        spread_q(k, q, [None] * 8 + list(regs))
                    pe.wait_ge(sem("att_made"), k + 1)
                    turn(bank[2][:, 0:P], att, ident).then_inc(sem("att_turned"), 1)
                    pe.wait_ge(sem("shift_made"), k + 1)
                    turn(bank[2][:, P:2 * P], shifted, ident)
                    turn(bank[2][:, 2 * P:3 * P], seg, ident).then_inc(sem("shift_turned"), 1)
                    pe.wait_ge(sem(f"blk_loaded{(u + 1) % SLOTS}"), 16 * (i + 1 + (u + 1) // SLOTS))
                    turn_hot(k + 1, (u + 1) % 2)
                    regs = load_regs(PE_, blk_slot[(u + 1) % SLOTS][:, 0:8], NB - 1)
                    for q in range(2):
                        pe.wait_ge(sem("q_used"), 4 * k + q + 3)
                        spread_q(k + 1, q, regs)
                    for t in range(STEPS):
                        if t % 4 == 0:
                            pe.wait_ge(sem("msg_ready"), 4 * k + t // 4 + 1)
                        if t % 2 == 0:
                            pe.wait_ge(sem("acc_done"), STEPS * k + t + 2)
                        mm(bank[5 + t % RING // 2][:, t % 2 * 256:t % 2 * 256 + SUMW], hot_step(u % 2, t),
                           rows3[:, t, 0:SUMW], start=True, stop=True).then_inc(sem("sum_made"), 1)
                        last = mm(bank[7][0:2 * STEPS, u % 2 * 256:u % 2 * 256 + ROWW],
                                  ends[:, t * 2 * STEPS:(t + 1) * 2 * STEPS], rows3[:, t, :],
                                  start=(t == 0), stop=(t == STEPS - 1))
                    last.then_inc(sem("ends_summed"), 1)

            pe.wait_ge(sem("mval_made"), 1)
            pe.wait_ge(sem("list_copied"), ROUNDS)
            nc4 = -(-LG // 4)
            for w, of in ((0, mval), (1, key8)):
                for c in range(nc4):
                    if w:
                        pe.wait_ge(sem("list_taken"), c + 1)
                    for g in range(4 * c, min(4 * c + 4, LG)):
                        last = turn(bank[c][0:HEADS, g % 4 * P:(g % 4 + 1) * P], of[:, g * HEADS:(g + 1) * HEADS], ident)
                    last.then_inc(sem("list_turned"), 1)
            pe.wait_ge(sem("keys_filled"), 1)
            pe.wait_ge(sem("list_taken"), 2 * nc4)
            for g in range(LG):
                last = turn(bank[1][:, g * HEADS:(g + 1) * HEADS], keyT[:, g * P:(g + 1) * P], ident[0:HEADS, 0:HEADS])
            last.then_inc(sem("keys_back"), 1)
            pe.wait_ge(sem("mexp_done"), 1)
            for g in range(LG):
                last = turn(bank[0][:, g * HEADS:(g + 1) * HEADS], mT[:, g * P:(g + 1) * P], ident[0:HEADS, 0:HEADS])
            last.then_inc(sem("factors_back"), 1)
            pe.wait_ge(sem("mblk_made"), 1)
            mm(bank[4][:, 0:MS], ones1, mblk_f, start=True, stop=True).then_inc(sem("mbase_spread"), 1)
            with pe.Fori(0, MR) as i:
                regs = load_regs(PE_, mtile_i[:, bass.ds(i * MERGES, MERGES)], LG - 1)
                for j in range(MERGES):
                    pe.wait_ge(sem("mhot_made"), MERGES * i + j + 1)
                    mm(bank[2 + j // 3][:, j % 3 * AW:(j % 3 + 1) * AW], hot[:, j * P:(j + 1) * P],
                       plist[:, bass.ds(regs[j] * ROWW, AW)], start=True, stop=True).then_inc(sem("msum_made"), 1)

            with pe.Fori(0, NB // EC) as i:
                pe.wait_ge(sem("hm_made"), i + 1)
                for j in range(EC):
                    for t in range(TYPES):
                        last = turn(bank[j][:, t * P:(t + 1) * P], hm[:, (t * EC + j) * P:(t * EC + j + 1) * P], ident)
                    last.then_inc(sem("hm_turned"), 1)
                for j in range(EC):
                    pe.wait_ge(sem("hmT_copied"), EC * (i + 1))
                    hot3 = types_s[:, j * P:(j + 1) * P]
                    o = bank[j // 4][:, j % 4 * P:(j % 4 + 1) * P]
                    for t in range(TYPES):
                        mm(o, hmT[:, (j * TYPES + t) * P:(j * TYPES + t + 1) * P], Wa_s[:, t * P:(t + 1) * P],
                           start=(t == 0), stop=False)
                    mm(o, hot3, bias3[:, 3 * P:4 * P], start=False, stop=True)
                    last = mm(bank[2 + j // 2][:, j % 2 * 256:j % 2 * 256 + 256], hot3, bias3[:, 4 * P:6 * P],
                              start=True, stop=True)
                last.then_inc(sem("trans_made"), 1)

            pe.wait_ge(sem("x1_made"), NB // EC)
            for c, (lo, hi) in enumerate(CH):
                if c >= 8:
                    pe.wait_ge(sem("agg_begun"), c - 7)
                for b in range(lo // P, hi // P):
                    last = turn(bank[c % 8][:, b * P - lo:b * P - lo + P], X[:, b * P:(b + 1) * P], ident)
                last.then_inc(sem("x1_turned"), 1)

            pe.wait_ge(sem("agg_begun"), len(CH))
            with pe.Fori(0, ROUNDS // SLOTS) as i:
                for u in range(SLOTS):
                    k = SLOTS * i + u
                    pe.wait_ge(sem(f"xg_loaded{u}"), 16 * STEPS * (i + 1))
                    for t in range(STEPS):
                        if t % 4 == 0:
                            pe.wait_ge(sem("hot2_made"), 4 * k + t // 4 + 1)
                            pe.wait_ge(sem("agg_done"), STEPS * k + t + 4)
                        mm(bank[t // 4][:, t % 4 * P:(t % 4 + 1) * P], xg_slot[u][:, t * P:(t + 1) * P],
                           hot_step(u % 2, t), start=True, stop=True).then_inc(sem("agg_made"), 1)

            pe.wait_ge(sem("agg_done"), STEPS * (ROUNDS + 1))
            for m, of in ((0, aggT), (1, y1)):
                if m:
                    pe.wait_ge(sem("relu_done"), len(CH))
                for c, (lo, hi) in enumerate(CH):
                    if m * len(CH) + c >= 8:
                        pe.wait_ge(sem("lin_copied"), m * len(CH) + c - 7)
                    mm(bank[c % 8][:, 0:hi - lo], W12[:, m * P:(m + 1) * P], of[:, lo:hi],
                       start=True, stop=True).then_inc(sem("lin_made"), 1)
            pe.wait_ge(sem("relu_done"), 2 * len(CH))
            for c in range(NB // EC):
                if c >= 4:
                    pe.wait_ge(sem("h2_used"), c - 3)
                for j in range(EC):
                    last = turn(bank[c % 4 * 2 + j // 4][:, j % 4 * P:(j % 4 + 1) * P],
                                y2[:, (c * EC + j) * P:(c * EC + j + 1) * P], ident)
                last.then_inc(sem("h2_turned"), 1)

        @block.vector
        def _(dve):
            v = nc.vector
            link = Chain(dve, sem("dve_chain"))
            then = link.then
            DVE_ = mybir.EngineType.DVE

            v.memset(tail_d, PADNODE).then_inc(sem("tails_set"), 1)
            v.memset(tail_z, 0).then_inc(sem("tails_set"), 1)
            v.memset(relk, 0.0)
            v.memset(relv, 0.0).then_inc(sem("rels_zeroed"), 1)
            v.memset(X[:, NK * P:NB * P], 0.0)
            v.memset(ntype_i, 0)
            v.memset(types_i, 0).then_inc(sem("nodes_zeroed"), 1)
            v.memset(resets, 0.0).then_inc(sem("resets_zeroed"), 1)
            v.memset(ends, 0.0)
            v.memset(ones1, 1.0)
            dve.wait_ge(sem("patterns_made"), 4)
            v.tensor_copy(iota_f, iota_i)
            v.tensor_copy(step_f, misc_i[:, 0:SG])
            v.tensor_copy(tcol, misc_i[0:TYPES, SG:SG + 1])
            v.tensor_copy(tcount, tcount_i)
            then(v.tensor_copy(pcol, misc_i[:, SG:SG + 1]))
            v.tensor_scalar(identb, iota_f, pcol, None, ALU.is_equal)
            then(v.tensor_scalar(ident, iota_f, pcol, None, ALU.is_equal))

            dve.wait_ge(sem("last_loaded"), 16)
            then(v.tensor_scalar(last_b, last_i, 7, None, ALU.arith_shift_right))
            then(v.tensor_copy(start_row, last_b))
            v.tensor_tensor(start_row, start_row, tcount, ALU.add).then_inc(sem("start_made"), 1)
            dve.wait_ge(sem("starts_copied"), -(-NT // 512))
            for g in range(SG):
                then(v.tensor_scalar(started[:, 0:NT - 1], starts[:, 0:NT - 1], step_f[:, g:g + 1], None, ALU.is_le))
                then(v.tensor_reduce(small[:, g:g + 1], started[:, 0:NT - 1], AX.X, ALU.add))
            v.tensor_copy(tile_i, small[:, 0:SG]).then_inc(sem("tiles_made"), 1)
            then(v.tensor_tensor(small[:, SG:2 * SG], step_f, small[:, 0:SG], ALU.subtract))
            then(v.tensor_scalar(small[:, 2 * SG:3 * SG], small[:, SG:2 * SG], float(P), None, ALU.mult))

            dve.wait_ge(sem("consts_loaded"), 16 * NCONST)
            then(v.tensor_copy(ntype_f, ntype_i))
            for t in range(TYPES):
                then(v.tensor_scalar(tmask[:, t * NB:(t + 1) * NB], ntype_f, float(t), None, ALU.is_equal))
            then(v.tensor_scalar(onehot3, types_i, tcol, None, ALU.is_equal))
            for r in range(RELS):
                v.tensor_scalar(relk[:, r * P:(r + 1) * P], relk[:, r * P:(r + 1) * P], pri[:, r:r + 1],
                                DK ** -0.5, ALU.mult, ALU.mult)
            then(v.tensor_scalar(cols[:, 7:8], cols[:, 6:7], 1.0, None, ALU.add))
            dve.sem_inc(sem("masks_made"), 1)
            dve.wait_ge(sem("skip_gated"), 1)
            then(v.tensor_scalar(gate, tmask[:, 0:NB], skip_s[:, 0:1], None, ALU.mult))
            for t in range(1, TYPES):
                then(v.scalar_tensor_tensor(gate, tmask[:, t * NB:(t + 1) * NB], skip_s[:, t:t + 1], gate,
                                            ALU.mult, ALU.add))
            then(v.tensor_scalar(ungate, gate, -1.0, 1.0, ALU.mult, ALU.add))

            def mask_x(b, u):
                v.tensor_scalar(types_s[:, u * P:(u + 1) * P], onehot3[:, bass.ds(b * P, P)], 0.0, None, ALU.add)
                for t in range(TYPES):
                    last = v.tensor_scalar(xm[u][:, t * P:(t + 1) * P], X[:, bass.ds(b * P, P)],
                                           tmask[:, bass.ds(t * NB + b, 1)], None, ALU.mult)
                last.then_inc(sem("xm_made"), 1)

            def split_q(b, u):
                dve.wait_ge(sem("kvT_copied"), b + 1)
                q = bank[2 + u][:, 2 * P:3 * P]
                parts = [Qsplit[:, bass.ds(b * (3 * P) + j * P, P)] for j in range(3)]
                then(v.tensor_scalar(parts[0], q, 0.0, None, ALU.add))
                then(v.tensor_tensor(rest, q, parts[0], ALU.subtract))
                then(v.tensor_scalar(parts[1], rest, 0.0, None, ALU.add))
                then(v.tensor_tensor(parts[2], rest, parts[1], ALU.subtract))

            def copy_tabv(b, u):
                dve.wait_ge(sem("tab_made"), b + 1)
                dve.wait_ge(sem("tab_free"), b + 1)
                then(v.tensor_copy(tab_s[u].rearrange("p (r c) -> p r c", r=RELS)[:, :, P:2 * P],
                                   bank[6 + u].rearrange("p (r c) -> p r c", r=RELS)))
                dve.sem_inc(sem("tabv_copied"), 1)
                dve.sem_inc(sem("bank_free"), 1)

            dve.sem_inc(sem("bank_free"), 2)
            mask_x(0, 0)
            with dve.Fori(0, NK // 2) as i:
                link.enter(i, 10)
                for u in range(2):
                    b = 2 * i + u
                    split_q(b, u)
                    mask_x(b + 1, 1 - u)
                    copy_tabv(b, u)
            link.leave(NK // 2)
            split_q(NK, 0)
            copy_tabv(NK, 0)

            dve.wait_ge(sem("rows_gathered"), 16 * 3 * SG)
            W3 = [W(j).rearrange("s (g e) -> s g e", e=P) for j in range(10)]
            v.tensor_copy(W(5), W(2).bitcast(I32))
            v.tensor_copy(W(6), W(3).bitcast(I32))
            then(v.tensor_copy(W(7), W(4).bitcast(I32)))
            then(v.scalar_tensor_tensor(W(8), W(6), float(RELS), W(7), ALU.mult, ALU.add))
            then(v.tensor_tensor(W3[7], W3[5], spread(small[:, 2 * SG:3 * SG], P), ALU.subtract))
            then(v.tensor_scalar(W(0), W(7), 0.0, None, ALU.is_ge))
            then(v.scalar_tensor_tensor(W(0), W(7), float(P - 1), W(0), ALU.is_le, ALU.mult))
            v.memset(W3[9][:, :, 0:1], 1.0)
            then(v.tensor_tensor(W3[9][:, :, 1:P], W3[5][:, :, 1:P], W3[5][:, :, 0:P - 1], ALU.not_equal))
            v.tensor_scalar(W(4), W(9), -BIG, None, ALU.mult).then_inc(sem("resets_made"), 1)
            v.tensor_tensor(W(3), W(5), W(9), ALU.mult)
            v.tensor_tensor(W3[1], W3[5], W3[5][:, :, 0:1].to_broadcast([P, SG, P]), ALU.is_equal)
            then(v.tensor_tensor(W3[2], W3[5], W3[5][:, :, P - 1:P].to_broadcast([P, SG, P]), ALU.is_equal))
            then(v.scalar_tensor_tensor(W(2), W(1), 0.0, W(2), ALU.is_equal, ALU.mult))
            v.tensor_tensor(W(2), W(2), W(0), ALU.mult)
            then(v.tensor_tensor(W(1), W(1), W(0), ALU.mult))
            dve.sem_inc(sem("arrays_made"), 1)
            then(v.memset(pad_s, -1.0))
            dve.sem_inc(sem("pad_set"), 1)
            dve.wait_ge(sem("blk_turned"), 1)
            v.tensor_scalar(blkT, bank[4][0:SG, 0:P], float(NB - 1), None, ALU.min).then_inc(sem("blk_made"), 1)
            for g in range(SG):
                dve.wait_ge(sem("recb_turned"), g + 1)
                dve.wait_ge(sem("recs_free"), g + 1)
                to = rec_s[g % 2].rearrange("e (k c s) -> e c k s", c=7, s=STEPS)
                of = bank[g % 2 * 2 + 1][:, 0:3 * P].rearrange("e (c k s) -> e c k s", c=3, s=STEPS)
                v.tensor_copy(to[:, C_HEADKEY], of[:, 0])
                v.tensor_copy(to[:, C_KVROW].bitcast(I32), of[:, 1])
                v.tensor_copy(to[:, C_SRC].bitcast(I32), of[:, 2]).then_inc(sem("recb_copied"), 1)

            def one_hot(par, u, made):
                for q in range(4):
                    key = rec_col(u, C_KEY)[:, 4 * q:4 * q + 4]
                    v.tensor_tensor(hot[:, (par * STEPS + 4 * q) * P:(par * STEPS + 4 * q + 4) * P]
                                    .rearrange("e (t n) -> e t n", n=P),
                                    iota_f.unsqueeze(1).to_broadcast([P, 4, P]), spread(key, P),
                                    ALU.is_equal).then_inc(made, 1)

            v.memset(acc, 0.0).then_inc(sem("acc_done"), RING)
            dve.wait_ge(sem("rec_loaded0"), 16)
            dve.wait_ge(sem("rec_stored0"), 16 * ((SG + 1) // 2))
            dve.wait_ge(sem("rec_stored1"), 16 * (SG // 2))
            dve.wait_ge(sem("acc_done"), RING)
            one_hot(0, 0, sem("hot_made"))
            with dve.Fori(0, ROUNDS // SLOTS) as i:
                link.enter(i, 2 * SLOTS)
                for u in range(SLOTS):
                    k = SLOTS * i + u
                    dve.wait_ge(sem(f"kv_loaded{u}"), 16 * STEPS * (i + 1))
                    kv3 = kv_slot[u].rearrange("e (t c) -> e t c", c=2 * P)
                    for q in range(4):
                        pr = prod[:, q % 2 * 512:q % 2 * 512 + 512]
                        dve.wait_ge(sem("q_spread"), 4 * k + q + 1)
                        v.tensor_tensor(pr.rearrange("e (t c) -> e t c", c=P), kv3[:, 4 * q:4 * q + 4, 0:P],
                                        bank[q % 2].rearrange("e (t c) -> e t c", c=P),
                                        ALU.mult).then_inc(sem("q_used"), 1)
                        dve.wait_ge(sem("q_used"), 4 * k + q + 1)
                        last = v.tensor_reduce(att[:, q * 32:q * 32 + 32], pr.rearrange("e (a d) -> e a d", d=DK),
                                               AX.X, ALU.add)
                    last.then_inc(sem("att_made"), 1)
                    dve.wait_ge(sem("att_turned"), k + 1)
                    dve.wait_ge(sem(f"reset_loaded{u}"), 16 * (i + 1))
                    rs = reset_slot[u]
                    then(v.tensor_tensor_scan(fwd, rs[:, 0:P], bank[2][:, 0:P], -BIG, ALU.add, ALU.max))
                    then(v.tensor_tensor_scan(seg[:, ::-1], rs[:, P:0:-1], fwd[:, ::-1], -BIG, ALU.add, ALU.max))
                    v.tensor_tensor(shifted, bank[2][:, 0:P], seg, ALU.subtract).then_inc(sem("shift_made"), 1)
                    if u + 1 < SLOTS:
                        dve.wait_ge(sem(f"rec_loaded{u + 1}"), 16 * (i + 1))
                    else:
                        dve.wait_ge(sem("rec_loaded0"), 16 * (i + 2))
                    one_hot((u + 1) % 2, (u + 1) % SLOTS, sem("hot_made"))
                    dve.wait_ge(sem(f"blk_loaded{u}"), 16 * (i + 1))
                    v.tensor_copy(ends[:, 0:511:34], rec_col(u, C_FIRST))
                    v.tensor_copy(ends[:, 1:512:34], rec_col(u, C_LAST))
                    v.tensor_copy(rows3[:, :, M_KEY], rec_col(u, C_HEADKEY))
                    dve.wait_ge(sem("exp_done"), k + 1)
                    v.tensor_tensor(rows3[:, :, M_MAX:M_MAX + HEADS],
                                    bank[2][:, 2 * P:3 * P].rearrange("e (t h) -> e t h", h=HEADS),
                                    spread(rec_col(u, C_HEAD), HEADS), ALU.mult)
                    for q in range(4):
                        tt = slice(4 * q, 4 * q + 4)
                        v.tensor_tensor(rows3[:, tt, 0:P].rearrange("e t (h d) -> e t h d", d=DK),
                                        kv3[:, tt, P:2 * P].rearrange("e t (h d) -> e t h d", d=DK),
                                        rows3[:, tt, M_EXP:M_EXP + HEADS].unsqueeze(3).to_broadcast([P, 4, HEADS, DK]),
                                        ALU.mult).then_inc(sem("msg_ready"), 1)
                    regs = load_regs(DVE_, blk_slot[u], NB - 1)
                    for t in range(STEPS):
                        dve.wait_ge(sem("acc_done"), RING + STEPS * k + t)
                        if t % 2 == 0:
                            dve.wait_ge(sem("sum_made"), STEPS * k + t + 2)
                        a = acc[:, bass.ds(regs[t] * SUMW, SUMW)]
                        v.tensor_tensor(a, bank[5 + t % RING // 2][:, t % 2 * 256:t % 2 * 256 + SUMW], a,
                                        ALU.add).then_inc(sem("acc_done"), 1)
            link.leave(ROUNDS // SLOTS)

            dve.wait_ge(sem("list_loaded"), 16)
            g8 = lambda a: a.rearrange("p (g h) -> p g h", h=HEADS)
            den = pl[:, :, M_EXP:M_EXP + HEADS]
            v.tensor_copy(g8(key8), pl[:, :, M_KEY:M_KEY + 1].to_broadcast([P, LG, HEADS]))
            then(v.tensor_scalar(g8(mval), den, 0.0, -BIG, ALU.is_equal, ALU.mult))
            then(v.tensor_tensor(g8(mval), g8(mval), pl[:, :, M_MAX:M_MAX + HEADS], ALU.add))
            dve.sem_inc(sem("mval_made"), 1)
            v.tensor_scalar(pl[:, :, M_MAX:M_MAX + 1], pl[:, :, M_EXP:M_EXP + 1], 0.0, None, ALU.is_gt)
            dve.wait_ge(sem("list_taken"), 2 * -(-LG // 4))
            then(v.tensor_tensor_scan(keyT, keyT, keyT, 0.0, ALU.max, ALU.max))
            dve.sem_inc(sem("keys_filled"), 1)
            v.memset(resets2[:, 0:1], 1.0)
            v.memset(resets2[:, ENTRIES:ENTRIES + 1], 0.0)
            then(v.tensor_tensor(resets2[:, 1:ENTRIES], keyT[:, 1:ENTRIES], keyT[:, 0:ENTRIES - 1], ALU.not_equal))
            then(v.tensor_scalar(resets2, resets2, -BIG, None, ALU.mult))
            then(v.tensor_tensor_scan(seg2, resets2[:, 0:ENTRIES], mT, -BIG, ALU.add, ALU.max))
            then(v.tensor_tensor_scan(seg2[:, ::-1], resets2[:, ENTRIES:0:-1], seg2[:, ::-1], -BIG, ALU.add, ALU.max))
            v.tensor_tensor(mT, mT, seg2, ALU.subtract).then_inc(sem("mshift_made"), 1)
            dve.wait_ge(sem("patterns_made"), 6)
            v.tensor_copy(mstep_f, mtile_i)
            then(v.tensor_copy(mstart_f, mlast_i))
            mkeys = keyT[0:1, P - 1:(LG - 1) * P:P]
            then(v.tensor_copy(mlast_i, mkeys))
            then(v.tensor_scalar(mlast_i, mlast_i, 7, None, ALU.arith_shift_right))
            mc = mcount.rearrange("o (s g) -> o s g", g=LG - 1)
            then(v.tensor_copy(mblk_f[:, 0:LG - 1], mlast_i))
            then(v.tensor_tensor(mstart_f, mstart_f, mblk_f[:, 0:LG - 1], ALU.add))
            then(v.tensor_tensor(mc, mstart_f.unsqueeze(1).to_broadcast([1, MS, LG - 1]), spread(mstep_f, LG - 1), ALU.is_le))
            then(v.tensor_reduce(mtile_f, mc, AX.X, ALU.add))
            v.tensor_copy(mtile_i, mtile_f)
            then(v.tensor_tensor(mblk_f, mstep_f, mtile_f, ALU.subtract))
            v.tensor_scalar(mblk_i, mblk_f, float(NB - 1), None, ALU.min)
            then(v.tensor_scalar(mblk_f, mblk_f, float(P), None, ALU.mult))
            dve.sem_inc(sem("mblk_made"), 1)
            dve.wait_ge(sem("keys_back"), 1)
            then(v.tensor_copy(keyf, bank[1][:, 0:G8:HEADS]))
            dve.wait_ge(sem("mbase_spread"), 1)
            then(v.tensor_copy(mbase, bank[4][:, 0:MS]))
            dve.wait_ge(sem("factors_back"), 1)
            dve.sem_inc(sem("keys_merged"), 1)
            then(v.tensor_copy(factor, bank[0][:, 0:G8]))
            v.tensor_tensor(pl[:, :, 0:P].rearrange("p g (h d) -> p g h d", d=DK),
                            pl[:, :, 0:P].rearrange("p g (h d) -> p g h d", d=DK),
                            g8(factor).unsqueeze(3).to_broadcast([P, LG, HEADS, DK]), ALU.mult)
            then(v.tensor_tensor(den, den, g8(factor), ALU.mult))
            then(v.memset(acc2, 0.0))
            dve.sem_inc(sem("macc_done"), 1)
            with dve.Fori(0, MR) as i:
                rt = load_regs(DVE_, mtile_i[:, bass.ds(i * MERGES, MERGES)], LG - 1)
                rb = load_regs(DVE_, mblk_i[:, bass.ds(i * MERGES, MERGES)], NB - 1)
                for j in range(MERGES):
                    v.tensor_scalar(hot[:, j * P:(j + 1) * P], iota_f, mbase[:, bass.ds(i * MERGES + j, 1)],
                                    keyf[:, bass.ds(rt[j], 1)], ALU.add, ALU.is_equal).then_inc(sem("mhot_made"), 1)
                for j in range(MERGES):
                    dve.wait_ge(sem("macc_done"), MERGES * i + j + 1)
                    dve.wait_ge(sem("msum_made"), MERGES * (i + 1))
                    a = acc2[:, bass.ds(rb[j] * AW, AW)]
                    v.tensor_tensor(a, bank[2 + j // 3][:, j % 3 * AW:(j % 3 + 1) * AW], a,
                                    ALU.add).then_inc(sem("macc_done"), 1)

            dve.wait_ge(sem("macc_done"), MS + 1)
            dve.wait_ge(sem("types_loaded"), 16)
            if NPAD > N:
                then(v.memset(types2_i[:, N:NPAD], 0))
            then(v.tensor_scalar(onehot3b, types2_i, tcol, None, ALU.is_equal))

            def layer_norm(to, a, var_made, root_made, count):
                mean, var = stat[:, 2 * EC:3 * EC], stat[:, EC:2 * EC]
                then(v.tensor_reduce(mean, a, AX.X, ALU.add))
                then(v.tensor_scalar(mean, mean, 1.0 / P, None, ALU.mult))
                then(v.tensor_tensor(a, a, spread(mean, P), ALU.subtract))
                then(v.tensor_tensor(by_block(square), a, a, ALU.mult))
                then(v.tensor_reduce(var, by_block(square), AX.X, ALU.add))
                v.tensor_scalar(var, var, 1.0 / P, LN_EPS, ALU.mult, ALU.add).then_inc(var_made, 1)
                dve.wait_ge(root_made, count)
                then(v.reciprocal(stat[:, 0:EC], stat[:, 0:EC]))
                then(v.tensor_tensor(to, a, spread(stat[:, 0:EC], P), ALU.mult))

            with dve.Fori(0, NB // EC) as i:
                link.enter(i, 33)
                a2 = blocks(acc2, i, AW)
                f3, h3, r3, k3 = by_block(fin, SUMW), by_block(hbuf), by_block(res), by_block(kept)
                keep = stat[:, 3 * EC:4 * EC]
                then(v.tensor_scalar(keep, a2[:, :, SUMW], 0.0, None, ALU.is_equal))
                then(v.tensor_tensor(f3, blocks(acc, i, SUMW), spread(keep, SUMW), ALU.mult))
                then(v.tensor_tensor(f3, f3, a2[:, :, 0:SUMW], ALU.add))
                rd = stat[:, 8 * EC:8 * EC + EC * HEADS]
                rd3 = rd.rearrange("p (b h) -> p b h", h=HEADS)
                then(v.tensor_scalar(rd3, f3[:, :, P:SUMW], 1e-16, None, ALU.add))
                then(v.reciprocal(rd, rd))
                then(v.tensor_tensor(r3.rearrange("p b (h d) -> p b h d", d=DK),
                                     f3[:, :, 0:P].rearrange("p b (h d) -> p b h d", d=DK),
                                     rd3.unsqueeze(3).to_broadcast([P, EC, HEADS, DK]), ALU.mult))
                dve.sem_inc(sem("aggr_made"), 1)
                then(v.tensor_scalar(types_s, onehot3b[:, bass.ds(i * EW, EW)], 0.0, None, ALU.add))
                dve.wait_ge(sem("gelu_done"), i + 1)
                for t in range(TYPES):
                    then(v.tensor_tensor(by_block(hm[:, t * EW:(t + 1) * EW]), h3,
                                         spread(tmask[:, bass.ds(i * EC + t * NB, EC)], P), ALU.mult))
                dve.sem_inc(sem("hm_made"), 1)
                then(v.tensor_tensor(k3, blocks(X, i), spread(ungate[:, bass.ds(i * EC, EC)], P), ALU.mult))
                dve.wait_ge(sem("trans_made"), i + 1)
                for n in range(2):
                    m = min(4, EC - 4 * n)
                    then(v.tensor_tensor(r3[:, 4 * n:4 * n + m], bank[n][:, 0:m * P].rearrange("p (b c) -> p b c", c=P),
                                         spread(gate[:, bass.ds(i * EC + 4 * n, m)], P), ALU.mult))
                then(v.tensor_tensor(r3, r3, k3, ALU.add))
                layer_norm(k3, r3, sem("var_made"), sem("root_made"), 2 * i + 1)
                for n in range(4):
                    m = min(2, EC - 2 * n)
                    gains = bank[2 + n][:, 0:m * 256].rearrange("p (b c) -> p b c", c=256)
                    v.tensor_tensor(k3[:, 2 * n:2 * n + m], k3[:, 2 * n:2 * n + m], gains[:, :, 0:P], ALU.mult)
                    then(v.tensor_tensor(r3[:, 2 * n:2 * n + m], blocks(X, i)[:, 2 * n:2 * n + m], gains[:, :, P:2 * P], ALU.add))
                then(v.tensor_tensor(r3, r3, k3, ALU.add))
                layer_norm(blocks(X, i), r3, sem("var_made"), sem("root_made"), 2 * i + 2)
                dve.sem_inc(sem("x1_made"), 1)
            link.leave(NB // EC)

            dve.wait_ge(sem("agg_begun"), len(CH))
            dve.sem_inc(sem("agg_done"), STEPS)
            dve.wait_ge(sem("rec2_loaded0"), 16)
            one_hot(0, 0, sem("hot2_made"))
            with dve.Fori(0, ROUNDS // SLOTS) as i:
                for u in range(SLOTS):
                    k = SLOTS * i + u
                    if u + 1 < SLOTS:
                        dve.wait_ge(sem(f"rec2_loaded{u + 1}"), 16 * (i + 1))
                    else:
                        dve.wait_ge(sem("rec2_loaded0"), 16 * (i + 2))
                    dve.wait_ge(sem(f"blk2_loaded{u}"), 16 * (i + 1))
                    one_hot((u + 1) % 2, (u + 1) % SLOTS, sem("hot2_made"))
                    regs = load_regs(DVE_, blk_slot[u], NB - 1)
                    for t in range(STEPS):
                        dve.wait_ge(sem("agg_done"), STEPS * (k + 1) + t)
                        if t % 4 == 0:
                            dve.wait_ge(sem("agg_made"), STEPS * k + t + 4)
                        a = aggT[:, bass.ds(regs[t] * P, P)]
                        v.tensor_tensor(a, bank[t // 4][:, t % 4 * P:(t % 4 + 1) * P], a,
                                        ALU.add).then_inc(sem("agg_done"), 1)

            for m, y in ((0, y1), (1, y2)):
                for c, (lo, hi) in enumerate(CH):
                    dve.wait_ge(sem("lin_copied"), m * len(CH) + c + 1)
                    last = v.bn_stats(stat[:, 8 + 6 * c:14 + 6 * c], y[:, lo:min(hi, N)])
                then(last)
                then(v.bn_aggr(stat[:, 4:6], stat[:, 8:8 + 6 * len(CH)]))
                v.tensor_scalar(stat[:, 1:2], stat[:, 5:6], BN_EPS, None, ALU.add).then_inc(sem("bvar_made"), 1)
                dve.wait_ge(sem("broot_made"), m + 1)
                then(v.reciprocal(stat[:, 0:1], stat[:, 0:1]))
                then(v.tensor_tensor(stat[:, 2:3], stat[:, 0:1], cols[:, 3 * m + 1:3 * m + 2], ALU.mult))
                then(v.tensor_tensor(stat[:, 6:7], stat[:, 4:5], stat[:, 2:3], ALU.mult))
                v.tensor_tensor(stat[:, 3:4], cols[:, 3 * m + 2:3 * m + 3], stat[:, 6:7],
                                ALU.subtract).then_inc(sem("bscale_made"), 1)
                dve.wait_ge(sem("relu_done"), (m + 1) * len(CH))
            for c in range(NB // EC):
                xc = blocks(X, c)
                r3 = by_block(res)
                dve.wait_ge(sem("h2_turned"), c + 1)
                for n in range(2):
                    m = min(4, EC - 4 * n)
                    then(v.tensor_tensor(r3[:, 4 * n:4 * n + m],
                                         bank[c % 4 * 2 + n][:, 0:m * P].rearrange("p (b c) -> p b c", c=P),
                                         xc[:, 4 * n:4 * n + m], ALU.add))
                dve.sem_inc(sem("h2_used"), 1)
                then(v.tensor_tensor(r3, r3, xc, ALU.add))
                layer_norm(xc, r3, sem("ovar_made"), sem("oroot_made"), c + 1)
                dve.sem_inc(sem("out_made"), 1)


_INS = ["x", "src", "dst", "edge_type_4", "node_type_3"] + ["L0_gnn_" + n for n in (
    "Wk", "bk", "Wq", "bq", "Wv", "bv", "Wa", "ba", "rel_pri", "rel_att", "rel_msg", "skip", "ln_g", "ln_b")] + [
    "L1_gnn_" + n for n in ("eps", "W1", "b1", "g1", "be1", "W2", "b2", "g2", "be2")]


def kernel(**inputs):
    import numpy as np
    import concourse.bacc as bacc
    from concourse.bass_utils import run_bass_kernel_spmd as run

    nc = bacc.Bacc("TRN2", target_bir_lowering=False, num_devices=1)
    arrays, args = {}, []
    for name in _INS:
        a = np.ascontiguousarray(inputs[name])
        if a.ndim == 0:
            a = a.reshape(1)
        arrays[f"in_{name}"] = a
        args.append(nc.dram_tensor(f"in_{name}", a.shape, mybir.dt.from_np(a.dtype), kind="ExternalInput").ap())
    out = nc.dram_tensor("out_x", tuple(inputs["x"].shape), F32, kind="ExternalOutput").ap()
    gnn_kernel(nc, *args, out)
    r = run(nc, [arrays], core_ids=[0])
    return r.results[0]["out_x"]
```

```python
from contextlib import ExitStack

import concourse.bass as bass
from concourse import mybir

F32 = mybir.dt.float32
BF16 = mybir.dt.bfloat16
I32 = mybir.dt.int32
ALU = mybir.AluOpType
ACT = mybir.ActivationFunctionType
AX = mybir.AxisListType

P = 128
HEADS = 8
DK = 16
RELS = 4
TYPES = 3
STEPS = 16
SLOTS = 4
BIG = 1.0e30
LN_EPS = 1e-5
BN_EPS = 1e-5
C_KVROW, C_KEY, C_FIRST, C_LAST, C_HEAD, C_HEADKEY, C_SRC = range(7)
REC = 7 * STEPS
M_EXP, M_MAX, M_KEY = P, P + HEADS, P + 2 * HEADS
SUMW = P + HEADS
ROWW = P + 2 * HEADS + 1


class Chain:

    def __init__(self, eng, sem):
        self.eng, self.sem, self.base, self.n = eng, sem, 0, 0

    def then(self, ins):
        ins.then_inc(self.sem, 1)
        self.n += 1
        self.eng.wait_ge(self.sem, self.base + self.n)

    def mark(self, ins):
        ins.then_inc(self.sem, 1)
        self.n += 1

    def reach(self):
        self.eng.wait_ge(self.sem, self.base + self.n)

    def enter(self, i, per):
        self.start, self.per = self.base + self.n, per
        self.base, self.n = self.start + i * per, 0

    def leave(self, rounds):
        assert self.n == self.per, (self.n, self.per)
        self.base, self.n = self.start + rounds * self.per, 0


def gnn_kernel(nc, x, src, dst, edge_type, node_type, Wk, bk, Wq, bq, Wv, bv, Wa, ba, rel_pri, rel_att,
               rel_msg, skip, ln_g, ln_b, eps, W1, b1, g1, be1, W2, b2, g2, be2, out):
    N = x.shape[0]
    E = src.shape[0]
    NB = -(-N // P)
    LASTN = N - (NB - 1) * P
    NT = -(-E // P)
    TAIL = NT * P - E
    SG = -(-(NT + NB - 1) // P)
    S = SG * P
    ROUNDS = S // STEPS
    ENTRIES = 2 * S
    LG = ENTRIES // P
    MERGES = 5
    MR = -(-(LG + NB - 1) // MERGES)
    PADNODE = NB * P - 1
    EC = 7
    assert NB % EC == 0 and NB % 2 == 1 and PADNODE >= N and TAIL > 0 and ROUNDS % SLOTS == 0
    NPAD = NB * P
    NCONST = 49
    FULLE = [d for d in range(64, 4000) if E % d == 0][0]

    dram = nc.dram_tensor
    dst_p = dram("dst_p", (NT, P), I32).ap()
    src_p = dram("src_p", (NT, P), I32).ap()
    typ_p = dram("typ_p", (NT, P), I32).ap()
    sorted_d = dram("sorted_d", (NT * P, 3), I32).ap()
    kvtab = dram("kvtab", (NPAD * RELS, 2 * P), F32).ap()
    rec_d = dram("rec_d", (ROUNDS + 1, P, REC), F32).ap()
    reset_d = dram("reset_d", (S, P), F32).ap()
    blk_d = dram("blk_d", (ROUNDS + 1, STEPS), I32).ap()
    list_d = dram("list_d", (2 * STEPS + ENTRIES, ROWW), F32).ap()
    x1_d = dram("x1_d", (NPAD, P), F32).ap()

    with ExitStack() as ctx:
        def sb(name, shape, dt=F32):
            return ctx.enter_context(nc.sbuf_tensor(name, shape, dt))[:, :]

        sems = {}

        def sem(name):
            if name not in sems:
                sems[name] = ctx.enter_context(nc.semaphore(name))
            return sems[name]

        bank = [ctx.enter_context(nc.psum_tensor(f"bank{i}", [P, 512], F32))[:, :] for i in range(8)]

        A2 = LG * ROWW
        A3 = A2 + NB * (SUMW + 1)
        AR = max(10 * S, SLOTS * STEPS * 2 * P, A3 + ENTRIES, A3 + EC * (SUMW + P))
        QW = max(NB * 3 * P, 2 * NPAD + 6 * EC * P, 4 * ENTRIES)
        arena = sb("arena", [P, AR])
        X = sb("X", [P, NB * P])
        acc_s = sb("acc", [P, max(NB * SUMW, NPAD + TYPES * P)])
        Qsplit = sb("Qsplit", [P, QW], BF16)
        blks = sb("blks", [1, SLOTS * STEPS], I32)
        hot = sb("hot", [P, 2 * STEPS * P])
        rows = sb("rows", [P, STEPS * ROWW])
        rec = sb("rec", [P, SLOTS * REC])
        resets = sb("resets", [P, SLOTS * (P + 1)])
        prod = sb("prod", [P, 2 * 4 * P])
        att = sb("att", [P, P])
        fwd = sb("fwd", [P, P])
        seg = sb("seg", [P, P])
        shifted = sb("shifted", [P, P])
        weight = sb("weight", [P, P])
        hotT = sb("hotT", [P, 16 * P], BF16)
        ends = sb("ends", [P, STEPS * 2 * STEPS])
        listed = sb("listed", [P, SLOTS * ROWW])
        iota_f = sb("iota_f", [P, P])
        unsorted_i = sb("unsorted_i", [1, 1], I32)
        iota_i = sb("iota_i", [P, P], I32)
        ident = sb("ident", [P, P])
        identb = sb("identb", [P, P], BF16)
        ones1 = sb("ones1", [1, P])
        Wa_s = sb("Wa_s", [P, TYPES * P])
        pri = sb("pri", [P, RELS])
        W12 = sb("W12", [P, 2 * P])
        bias3 = sb("bias3", [TYPES, 6 * P])
        cols = sb("cols", [P, 8])
        skip_s = sb("skip_s", [P, TYPES])
        ntype_i = sb("ntype_i", [P, NB], I32)
        ntype_f = sb("ntype_f", [P, NB])
        tmask = sb("tmask", [P, TYPES * NB])
        gate = sb("gate", [P, NB])
        tcol = sb("tcol", [TYPES, 1])
        small = sb("small", [P, 3 * SG])
        misc_i = sb("misc_i", [P, SG + 1], I32)
        tile_i = sb("tile_i", [P, SG], I32)
        step_f = sb("step_f", [P, SG])
        stat = sb("stat", [P, 8 * EC + EC * HEADS])
        pcol = sb("pcol", [P, 1])
        ungate = sb("ungate", [P, NB])

        def W(i):
            return arena[:, i * S:(i + 1) * S]

        last_i = W(0)[0:1, 0:NT].bitcast(I32)
        last_b = W(1)[0:1, 0:NT].bitcast(I32)
        start_row = W(2)[0:1, 0:NT]
        tcount = W(3)[0:1, 0:NT]
        tcount_i = W(4)[0:1, 0:NT].bitcast(I32)
        starts = W(5)[:, 0:NT]
        order_a, order_b = (W(j)[:, 0:NT].bitcast(I32) for j in (0, 1))
        descents = W(2)[:, 0:NT]
        srt = W(8)
        edge3 = srt[:, 0:3].bitcast(I32)
        digits_i, digits_f, dst_f = srt[:, 3:5].bitcast(I32), srt[:, 5:7], srt[:, 7:8]
        rank, base_f, place_i = srt[:, 8:9], srt[:, 9:10], srt[:, 10:11].bitcast(I32)
        nextp, counts, before_f = W(4)[:, 0:NB], W(5)[:, 0:NB], W(6)[:, 0:NB]
        one_lo, one_hi, one_loT = W(7)[:, 0:P], acc_s[:, 0:NB], acc_s[:, P:2 * P]
        row_i, row_f = acc_s[:, 2 * P:3 * P].bitcast(I32), acc_s[:, 3 * P:4 * P]
        earlier, later, ones_f = hot[:, 0:P], hot[:, P:2 * P], hot[:, 2 * P:3 * P]
        tail_d = W(9)[0:1, 0:P].bitcast(I32)
        tail_z = W(8)[0:1, 0:P].bitcast(I32)
        blkT = prod[0:SG, P:2 * P].bitcast(I32)
        started = W(6)[:, 0:NT]

        types_i = acc_s[0:TYPES, 0:NPAD].bitcast(I32)
        onehot3 = acc_s[0:TYPES, 0:NPAD]
        acc = acc_s[:, 0:NB * SUMW]
        NK = NB - 1

        xm = [hot[:, u * 384:(u + 1) * 384] for u in range(2)]
        xmT = [hot[:, 768 + u * 384:768 + (u + 1) * 384] for u in range(2)]
        kvT = [hot[:, 1536 + u * 256:1536 + (u + 1) * 256] for u in range(2)]
        tab_s = [rows[:, u * 1024:(u + 1) * 1024] for u in range(2)]
        rest = prod[:, 0:P]
        relk, relv = hot[:, 2048:2048 + 512], hot[:, 2560:2560 + 512]
        Wk_s, Wv_s = hot[:, 3072:3072 + 384], hot[:, 3456:3456 + 384]
        Wq_s = acc_s[:, NPAD:NPAD + TYPES * P]
        types_s = hotT.bitcast(F32)[0:TYPES, 0:EC * P]

        rec_s = [hot[:, u * 8 * REC:(u + 1) * 8 * REC] for u in range(2)]
        pad_s = prod[:, 0:REC]

        RING = 4
        Q_BANK = (0, 1, 4, 0)
        rec_slot = [rec[:, u * REC:(u + 1) * REC] for u in range(SLOTS)]
        reset_slot = [resets[:, u * (P + 1):(u + 1) * (P + 1)] for u in range(SLOTS)]
        blk_slot = [blks[:, u * STEPS:(u + 1) * STEPS] for u in range(SLOTS)]
        kv_slot = [arena[:, u * STEPS * 2 * P:(u + 1) * STEPS * 2 * P] for u in range(SLOTS)]
        xg_slot = [arena[:, u * STEPS * P:(u + 1) * STEPS * P] for u in range(SLOTS)]
        rows3 = rows.rearrange("e (t c) -> e t c", c=ROWW)
        hotb = hot.bitcast(BF16)

        def rec_col(u, c):
            return rec_slot[u][:, c * STEPS:(c + 1) * STEPS]

        def hot_step(par, t):
            o = (par * STEPS + t) * P
            return hot[:, o:o + P]

        def hot_step_bf16(par, t):
            o = (par * STEPS + t) * P * 2
            return hotb[:, o + 1:o + 2 * P:2]

        AW = SUMW + 1
        plist = arena[:, 0:A2]
        pl = plist.rearrange("p (g c) -> p g c", c=ROWW)
        acc2 = arena[:, A2:A3]
        Qf = Qsplit.bitcast(F32)
        mT = Qf[0:HEADS, 0:ENTRIES]
        keyT = Qf[0:HEADS, ENTRIES:2 * ENTRIES]
        resets2 = hot[0:HEADS, 0:ENTRIES + 1]
        seg2 = arena[0:HEADS, A3:A3 + ENTRIES]
        G8 = LG * HEADS
        mval, key8, factor, keyf = (rows[:, 0:G8], rows[:, G8:2 * G8], rows[:, 2 * G8:3 * G8],
                                    rows[:, 3 * G8:3 * G8 + LG])
        MS = MR * MERGES
        merge_i = prod[0:1, 512:512 + 2 * MS + LG].bitcast(I32)
        merge_f = prod[:, 0:4 * MS + LG]
        assert 4 * MS + LG <= 512
        mtile_i, mblk_i = merge_i[:, 0:MS], merge_i[:, MS:2 * MS]
        mlast_i = merge_i[:, 2 * MS:2 * MS + LG - 1]
        mstep_f, mtile_f, mblk_f = (merge_f[0:1, j * MS:(j + 1) * MS] for j in range(3))
        mbase = merge_f[:, 3 * MS:4 * MS]
        mstart_f = merge_f[0:1, 4 * MS:4 * MS + LG - 1]
        mcount = arena[0:1, A3:A3 + MS * (LG - 1)]
        assert A3 + max(ENTRIES, MS * (LG - 1)) <= AR and ENTRIES + 1 <= 2 * STEPS * P and 2 * ENTRIES <= Qf.shape[1]

        EW = EC * P
        types2_i = Qf[0:TYPES, 0:NPAD].bitcast(I32)
        onehot3b = Qf[0:TYPES, 0:NPAD]
        hmT = Qf[:, NPAD:NPAD + 3 * EW]
        hm = hot[:, 0:3 * EW]
        square = hot[:, 3 * EW:4 * EW]
        hbuf, res = rows[:, 0:EW], rows[:, EW:2 * EW]
        fin = arena[:, A3:A3 + EC * SUMW]
        kept = arena[:, A3 + EC * SUMW:A3 + EC * SUMW + EW]
        aggT = acc_s[:, 0:NPAD]
        y1 = Qf[:, 0:NPAD]
        y2 = arena[:, SLOTS * STEPS * P:SLOTS * STEPS * P + NPAD]
        CH = [(c, min(c + 512, NPAD)) for c in range(0, NPAD, 512)]
        assert NPAD + 3 * EW <= Qf.shape[1] and SLOTS * STEPS * P + NPAD <= AR

        def blocks(a, i, w=P):
            return a.rearrange("p (b c) -> p b c", c=w)[:, bass.ds(i * EC, EC), :]

        def by_block(a, w=P):
            return a.rearrange("p (b c) -> p b c", c=w)

        def spread(a, n):
            return a.unsqueeze(2).to_broadcast([a.shape[0], a.shape[1], n])

        def load_regs(engine, row, top):
            return nc.values_load_multi_w_load_instructions(
                row, engines=(engine,), min_val=0, max_val=top,
                skip_runtime_bounds_check_because="the schedule is clamped")[1]

        ctx.enter_context(nc.allow_non_contiguous_dma(reason="a few columns of the inputs, once"))
        block = ctx.enter_context(nc.Block())

        @block.sync
        def _(sp):
            cst = sem("consts_loaded")
            for name, a, p in (("dst", dst, dst_p), ("src", src, src_p), ("typ", edge_type, typ_p)):
                flat = p.rearrange("t e -> (t e)")
                sp.dma_start(flat[0:E].rearrange("(a b) -> a b", a=FULLE),
                             a.rearrange("(a b) -> a b", a=FULLE)).then_inc(sem("edges_copied"), 16)
            sp.wait_ge(sem("tails_set"), 2)
            for p, t in ((dst_p, tail_d), (src_p, tail_z), (typ_p, tail_z)):
                flat = p.rearrange("t e -> (t e)")
                sp.dma_start(flat[E:NT * P].unsqueeze(0), t[:, 0:TAIL]).then_inc(sem("edges_copied"), 16)
            sp.dma_start(blk_d[ROUNDS:ROUNDS + 1], tail_z[:, 0:STEPS]).then_inc(sem("edges_copied"), 16)
            sp.wait_ge(sem("edges_copied"), 112)
            flat = dst_p.rearrange("t e -> (t e)")
            sp.dma_start(order_a, flat.rearrange("(p j) -> p j", p=P)).then_inc(sem("order_loaded"), 16)
            sp.dma_start(order_b[0:P - 1, :], flat[1:1 + (P - 1) * NT].rearrange("(p j) -> p j", j=NT)).then_inc(sem("order_loaded"), 16)
            sp.dma_start(order_b[P - 1:P, 0:NT - 1], flat[1 + (P - 1) * NT:NT * P].unsqueeze(0)).then_inc(sem("order_loaded"), 16)
            sp.wait_ge(sem("order_checked"), 1)
            unsorted = sp.value_load(unsorted_i[:, :])
            with sp.If(unsorted > 0):
                with sp.Fori(0, NT) as t:
                    sp.wait_ge(sem("tile_counted"), t + 1)
                    sp.dma_start(edge3[:, 0:1], dst_p[bass.ds(t, 1), :].rearrange("o e -> e o")).then_inc(sem("count_loaded"), 16)
                with sp.Fori(0, NT) as t:
                    sp.wait_ge(sem("tile_free"), t + 1)
                    sp.wait_ge(sem("tile_ranked"), t + 1)
                    for j, a in enumerate((dst_p, src_p, typ_p)):
                        sp.dma_start(edge3[:, j:j + 1], a[bass.ds(t, 1), :].rearrange("o e -> e o")).then_inc(sem("place_loaded"), 16)
                    sp.dma_start(row_i, dst_p[bass.ds(t, 1), :].to_broadcast([P, P])).then_inc(sem("place_loaded"), 16)
                sp.wait_ge(sem("tile_free"), NT + 1)
                for j, a in enumerate((dst_p, src_p, typ_p)):
                    sp.dma_start(a, sorted_d[:, j:j + 1].rearrange("(t e) o -> t (e o)", e=P)).then_inc(sem("sorted_back"), 16)
                sp.wait_ge(sem("sorted_back"), 48)
            sp.dma_start(last_i, dst_p[:, P - 1:P].rearrange("t o -> o t")).then_inc(sem("last_loaded"), 16)
            for s_, w in ((Wk_s, Wk), (Wq_s, Wq), (Wv_s, Wv), (Wa_s, Wa)):
                sp.dma_start(s_.rearrange("i (t o) -> i t o", t=TYPES), w.rearrange("t i o -> i t o")).then_inc(cst, 16)
            for j, b in enumerate((bk, bv, bq, ba, ln_g, ln_b)):
                sp.dma_start(bias3[:, j * P:(j + 1) * P], b).then_inc(cst, 16)
            sp.dma_start(W12[:, 0:P], W1).then_inc(cst, 16)
            sp.dma_start(W12[:, P:2 * P], W2).then_inc(cst, 16)
            for j, b in enumerate((b1, g1, be1, b2, g2, be2)):
                sp.dma_start(cols[:, j:j + 1], b.unsqueeze(1)).then_inc(cst, 16)
            sp.dma_start(cols[:, 6:7], eps.partition_broadcast(P)).then_inc(cst, 16)
            sp.dma_start(skip_s, skip.partition_broadcast(P)).then_inc(cst, 16)
            sp.wait_ge(sem("rels_zeroed"), 1)
            for h in range(HEADS):
                for s_, r in ((relk, rel_att), (relv, rel_msg)):
                    sp.dma_start(s_.rearrange("p (r f) -> p r f", r=RELS)[h * DK:(h + 1) * DK, :, h * DK:(h + 1) * DK],
                                 r[:, h].rearrange("r d f -> d r f")).then_inc(cst, 16)
                sp.dma_start(pri[h * DK:(h + 1) * DK, :], rel_pri[:, h].partition_broadcast(DK)).then_inc(cst, 16)
            sp.wait_ge(sem("nodes_zeroed"), 1)
            sp.dma_start(X[:, 0:NK * P].rearrange("p (b f) -> p b f", f=P),
                         x[0:NK * P, :].rearrange("(b p) f -> p b f", p=P)).then_inc(cst, 16)
            sp.dma_start(X[0:LASTN, NK * P:NB * P], x[NK * P:N, :]).then_inc(cst, 16)
            sp.dma_start(ntype_i[:, 0:NK], node_type[0:NK * P].rearrange("(b p) -> p b", p=P)).then_inc(cst, 16)
            sp.dma_start(ntype_i[0:LASTN, NK:NB], node_type[NK * P:N].unsqueeze(1)).then_inc(cst, 16)
            sp.dma_start(types_i[:, 0:N], node_type.partition_broadcast(TYPES)).then_inc(cst, 16)

            def store_table(b, u):
                sp.wait_ge(sem("tabk_copied"), b + 1)
                sp.sem_inc(sem("table_rounds"), 1)
                sp.wait_ge(sem("tabv_copied"), b + 3)
                sp.sem_inc(sem("table_rounds"), 1)
                sp.dma_start(kvtab.rearrange("(n r) f -> n (r f)", r=RELS)[bass.ds(b * P, P), :],
                             tab_s[u]).then_inc(sem(f"tab_stored{u}"), 16)

            def free_table(u, count):
                sp.wait_ge(sem(f"tab_stored{u}"), 16 * count)
                sp.sem_inc(sem("tab_free"), 1)

            sp.sem_inc(sem("tab_free"), 2)
            store_table(0, 0)
            with sp.Fori(0, NK // 2) as i:
                for u in range(2):
                    store_table(2 * i + u + 1, 1 - u)
                    free_table(u, i + 1)
            free_table(0, NK // 2 + 1)

            sp.wait_ge(sem("blk_made"), 1)
            sp.dma_start(blk_d[0:ROUNDS].rearrange("(g k) s -> g (k s)", g=SG), blkT[:, :]).then_inc(sem("blk_stored"), 16)
            sp.wait_ge(sem("blk_stored"), 16)
            sp.wait_ge(sem("resets_made"), 1)
            sp.dma_start(reset_d.rearrange("(g s) e -> s g e", s=P),
                         W(4).rearrange("s (g e) -> s g e", g=SG)).then_inc(sem("rec_stored"), 16)
            sp.sem_inc(sem("recs_free"), 2)
            for g in range(SG):
                sp.wait_ge(sem("reca_copied"), g + 1)
                sp.wait_ge(sem("recb_copied"), g + 1)
                sp.dma_start(rec_d[g * 8:(g + 1) * 8].rearrange("k e c -> e k c"),
                             rec_s[g % 2].rearrange("e (k c) -> e k c", c=REC)).then_inc(sem(f"rec_stored{g % 2}"), 16)
                sp.wait_ge(sem(f"rec_stored{g % 2}"), 16 * (g // 2 + 1))
                sp.sem_inc(sem("recs_free"), 1)
            sp.wait_ge(sem("pad_set"), 1)
            sp.dma_start(rec_d[ROUNDS], pad_s).then_inc(sem("rec_stored"), 16)
            sp.wait_ge(sem("rec_stored"), 32)

            def load_blks(k, u, loaded):
                sp.dma_start(blk_slot[u], blk_d[bass.ds(k, 1), :]).then_inc(sem(f"{loaded}{u}"), 16)

            def load_round(k, u):
                load_blks(k, u, "blk_loaded")
                sp.dma_start(rec_slot[u], rec_d[bass.ds(k, 1)].rearrange("o e c -> (o e) c")).then_inc(sem(f"rec_loaded{u}"), 16)
                sp.dma_start(reset_slot[u][:, 0:P], reset_d[bass.ds(k * STEPS, STEPS), :].unsqueeze(1)
                             .to_broadcast([STEPS, HEADS, P])).then_inc(sem(f"reset_loaded{u}"), 16)

            def store_list(k, u):
                sp.wait_ge(sem("list_copied"), k + 1)
                sp.dma_start(list_d[bass.ds(k * 2 * STEPS, 2 * STEPS), :],
                             listed[0:2 * STEPS, u * ROWW:(u + 1) * ROWW]).then_inc(sem("list_stored"), 16)
                sp.wait_ge(sem("list_stored"), 16 * (k + 1))

            sp.wait_ge(sem("resets_zeroed"), 1)
            for u in range(SLOTS):
                load_round(u, u)
            store_list(0, 0)
            with sp.Fori(0, ROUNDS // SLOTS - 1) as i:
                for u in range(SLOTS):
                    k = SLOTS * i + u
                    sp.wait_ge(sem("acc_done"), RING + STEPS * (k + 2))
                    store_list(k + 1, (u + 1) % SLOTS)
                    load_round(k + SLOTS, u)
            store_list(ROUNDS - SLOTS + 1, 1)
            sp.wait_ge(sem("acc_done"), RING + STEPS * (ROUNDS - SLOTS + 2))
            load_blks(ROUNDS, 0, "blk_loaded")
            sp.dma_start(rec_slot[0], rec_d[ROUNDS]).then_inc(sem("rec_loaded0"), 16)
            for u in range(2, SLOTS + 1):
                store_list(ROUNDS - SLOTS + u, u % SLOTS)
            sp.dma_start(plist.rearrange("p (g c) -> p g c", g=LG),
                         list_d[2 * STEPS:].rearrange("(g p) c -> p g c", p=P)).then_inc(sem("list_loaded"), 16)
            sp.wait_ge(sem("keys_merged"), 1)
            sp.dma_start(types2_i[:, 0:N], node_type.partition_broadcast(TYPES)).then_inc(sem("types_loaded"), 16)

            with sp.Fori(0, NB // EC) as i:
                sp.wait_ge(sem("x1_made"), i + 1)
                sp.dma_start(x1_d.rearrange("(b p) f -> p b f", p=P)[:, bass.ds(i * EC, EC), :],
                             X.rearrange("p (b f) -> p b f", f=P)[:, bass.ds(i * EC, EC), :]).then_inc(sem("x1_stored"), 16)
            sp.wait_ge(sem("x1_stored"), 16 * (NB // EC))
            sp.sem_inc(sem("x1_ready"), 1)

            def load_round2(k, u):
                load_blks(k, u, "blk2_loaded")
                sp.dma_start(rec_slot[u], rec_d[bass.ds(k, 1)].rearrange("o e c -> (o e) c")).then_inc(sem(f"rec2_loaded{u}"), 16)

            for u in range(SLOTS):
                load_round2(u, u)
            with sp.Fori(0, ROUNDS // SLOTS - 1) as i:
                for u in range(SLOTS):
                    k = SLOTS * i + u
                    sp.wait_ge(sem("agg_done"), STEPS * (k + 2))
                    load_round2(k + SLOTS, u)
            sp.wait_ge(sem("agg_done"), STEPS * (ROUNDS - SLOTS + 2))
            sp.dma_start(rec_slot[0], rec_d[ROUNDS]).then_inc(sem("rec2_loaded0"), 16)

            def store_out(lo, n, cnt):
                sp.dma_start(out[lo * P:(lo + n) * P, :].rearrange("(b p) f -> p b f", p=P),
                             X.rearrange("p (b f) -> p b f", f=P)[:, lo:lo + n, :]).then_inc(sem("out_stored"), 16)

            for c in range(NB // EC):
                sp.wait_ge(sem("out_made"), c + 1)
                store_out(c * EC, EC if c < NB // EC - 1 else EC - 1, c)
            sp.dma_start(out[NK * P:N, :], X[0:LASTN, NK * P:NB * P]).then_inc(sem("out_stored"), 16)
            sp.wait_ge(sem("out_stored"), 16 * (NB // EC + 1))

        @block.gpsimd
        def _(pool):
            made = sem("patterns_made")
            pool.iota(iota_i, [[1, P]], base=0, channel_multiplier=0).then_inc(made, 1)
            pool.iota(misc_i[:, 0:SG], [[P, SG]], base=0, channel_multiplier=1).then_inc(made, 1)
            pool.iota(misc_i[:, SG:SG + 1], [[0, 1]], base=0, channel_multiplier=1).then_inc(made, 1)
            pool.iota(tcount_i, [[1, NT]], base=1, channel_multiplier=0).then_inc(made, 1)

            pool.wait_ge(sem("order_checked"), 1)
            unsorted = pool.value_load(unsorted_i[:, :])
            with pool.If(unsorted > 0):
                pool.sem_inc(sem("tile_free"), 1)
                with pool.Fori(0, NT) as t:
                    pool.wait_ge(sem("tile_ranked"), t + 2)
                    pool.sem_inc(sem("pool_places"), 1)
                    pool.indirect_dma_start(sorted_d, bass.IndirectOffsetOnAxis(ap=place_i, axis=0), edge3,
                                            None).then_inc(sem("tile_placed"), 16)
                    pool.wait_ge(sem("tile_placed"), 16 * (t + 1))
                    pool.sem_inc(sem("tile_free"), 1)

            def gather(to, table, idx):
                return pool.indirect_dma_start(to, None, table, bass.IndirectOffsetOnAxis(ap=idx, axis=0))

            pool.wait_ge(sem("tiles_made"), 1)
            for g in range(SG):
                for w, table in ((2, dst_p), (3, src_p), (4, typ_p)):
                    gather(W(w)[:, g * P:(g + 1) * P].bitcast(I32), table,
                           tile_i[:, g:g + 1]).then_inc(sem("rows_gathered"), 16)

            pool.wait_ge(sem("tab_free"), NB + 2)

            def gather_kv(u):
                for t in range(STEPS):
                    gather(kv_slot[u][:, t * 2 * P:(t + 1) * 2 * P], kvtab,
                           rec_col(u, C_KVROW).bitcast(I32)[:, t:t + 1]).then_inc(sem(f"kv_loaded{u}"), 16)

            for u in range(SLOTS):
                pool.wait_ge(sem(f"rec_loaded{u}"), 16)
                gather_kv(u)
            with pool.Fori(1, ROUNDS // SLOTS) as i:
                for u in range(SLOTS):
                    pool.wait_ge(sem("msg_ready"), 4 * (SLOTS * (i - 1) + u + 1) + 1)
                    pool.wait_ge(sem(f"rec_loaded{u}"), 16 * (i + 1))
                    pool.sem_inc(sem("pool_rounds"), 1)
                    gather_kv(u)

            pool.wait_ge(sem("msg_ready"), 4 * ROUNDS + 1)
            pool.iota(mtile_i, [[1, MS]], base=0, channel_multiplier=0).then_inc(made, 1)
            pool.iota(mlast_i, [[1, LG - 1]], base=1, channel_multiplier=0).then_inc(made, 1)

            pool.wait_ge(sem("x1_ready"), 1)

            def gather_x(u):
                for t in range(STEPS):
                    gather(xg_slot[u][:, t * P:(t + 1) * P], x1_d,
                           rec_col(u, C_SRC).bitcast(I32)[:, t:t + 1]).then_inc(sem(f"xg_loaded{u}"), 16)

            for u in range(SLOTS):
                pool.wait_ge(sem(f"rec2_loaded{u}"), 16)
                gather_x(u)
            with pool.Fori(1, ROUNDS // SLOTS) as i:
                for u in range(SLOTS):
                    pool.wait_ge(sem(f"rec2_loaded{u}"), 16 * (i + 1))
                    pool.sem_inc(sem("pool_rounds"), 1)
                    gather_x(u)

        @block.scalar
        def _(act):
            link = Chain(act, sem("act_chain"))

            def copy(to, of, **kw):
                return act.activation(to, of, ACT.Copy, **kw)

            for c in range(-(-NT // 512)):
                n = min(NT - c * 512, 512)
                act.wait_ge(sem("starts_spread"), c + 1)
                copy(starts[:, c * 512:c * 512 + n], bank[c][:, 0:n]).then_inc(sem("starts_copied"), 1)
            act.wait_ge(sem("consts_loaded"), 16 * NCONST)
            act.activation(skip_s, skip_s, ACT.Sigmoid).then_inc(sem("skip_gated"), 1)

            def copy_xmT(b, u):
                act.wait_ge(sem("xm_turned"), b + 1)
                copy(xmT[u], bank[u][:, 0:384]).then_inc(sem("xmT_copied"), 1)

            def copy_kvT(b, u):
                act.wait_ge(sem("qkv_made"), b + 1)
                copy(kvT[u], bank[2 + u][:, 0:256]).then_inc(sem("kvT_copied"), 1)

            def copy_tabk(b, u):
                act.wait_ge(sem("tab_made"), b + 1)
                act.wait_ge(sem("tab_free"), b + 1)
                copy(tab_s[u].rearrange("p (r c) -> p r c", r=RELS)[:, :, 0:P],
                     bank[4 + u].rearrange("p (r c) -> p r c", r=RELS)).then_inc(sem("tabk_copied"), 1)

            copy_xmT(0, 0)
            copy_xmT(1, 1)
            copy_kvT(0, 0)
            with act.Fori(0, NK // 2 - 1) as i:
                for u in range(2):
                    b = 2 * i + u
                    copy_kvT(b + 1, 1 - u)
                    copy_xmT(b + 2, u)
                    copy_tabk(b, u)
            copy_kvT(NK - 1, 1)
            copy_xmT(NK, 0)
            copy_tabk(NK - 2, 0)
            copy_kvT(NK, 0)
            copy_tabk(NK - 1, 1)
            copy_tabk(NK, 0)

            for g in range(SG):
                act.wait_ge(sem("reca_turned"), g + 1)
                act.wait_ge(sem("recs_free"), g + 1)
                copy(rec_s[g % 2].rearrange("e (k c s) -> e c k s", c=7, s=STEPS)[:, C_KEY:C_HEAD + 1],
                     bank[g % 2 * 2].rearrange("e (c k s) -> e c k s", c=4, s=STEPS)).then_inc(sem("reca_copied"), 1)

            def copy_hotT(k, half):
                act.wait_ge(sem("hot_turned"), 2 * k + half + 1)
                copy(hotT[:, half * 1024:(half + 1) * 1024], bank[3].bitcast(BF16)).then_inc(sem("hotT_copied"), 1)

            def copy_list(k, u):
                act.wait_ge(sem("ends_summed"), k + 1)
                copy(listed[0:2 * STEPS, u * ROWW:(u + 1) * ROWW],
                     bank[7][0:2 * STEPS, u % 2 * 256:u % 2 * 256 + ROWW]).then_inc(sem("list_copied"), 1)

            act.activation(stat[:, 0:1], ident[:, 0:1], ACT.Exp)
            copy_hotT(0, 0)
            copy_hotT(0, 1)
            with act.Fori(0, ROUNDS // SLOTS) as i:
                for u in range(SLOTS):
                    k = SLOTS * i + u
                    act.wait_ge(sem("shift_turned"), k + 1)
                    act.activation(weight, bank[2][:, P:2 * P], ACT.Exp).then_inc(sem("exp_done"), 1)
                    copy_hotT(k + 1, 0)
                    copy_list(k, u)
                    copy_hotT(k + 1, 1)
            copy_list(ROUNDS, 0)

            for w, to in ((0, mT), (1, keyT)):
                for c in range(-(-LG // 4)):
                    n = min(LG - 4 * c, 4) * P
                    act.wait_ge(sem("list_turned"), w * (-(-LG // 4)) + c + 1)
                    copy(to[:, c * 512:c * 512 + n], bank[c][0:HEADS, 0:n]).then_inc(sem("list_taken"), 1)
            act.wait_ge(sem("mshift_made"), 1)
            act.activation(mT, mT, ACT.Exp).then_inc(sem("mexp_done"), 1)

            with act.Fori(0, NB // EC) as i:
                act.wait_ge(sem("aggr_made"), i + 1)
                act.activation(hbuf, res, ACT.Gelu).then_inc(sem("gelu_done"), 1)
                for j in range(EC):
                    act.wait_ge(sem("hm_turned"), EC * i + j + 1)
                    copy(hmT[:, j * 384:(j + 1) * 384], bank[j][:, 0:384]).then_inc(sem("hmT_copied"), 1)
                for n in range(2):
                    act.wait_ge(sem("var_made"), 2 * i + n + 1)
                    act.activation(stat[:, 0:EC], stat[:, EC:2 * EC], ACT.Sqrt).then_inc(sem("root_made"), 1)

            for c, (lo, hi) in enumerate(CH):
                act.wait_ge(sem("x1_turned"), c + 1)
                copy(aggT[:, lo:hi], bank[c % 8][:, 0:hi - lo], scale=cols[:, 7:8]).then_inc(sem("agg_begun"), 1)

            for m, y in ((0, y1), (1, y2)):
                for c, (lo, hi) in enumerate(CH):
                    act.wait_ge(sem("lin_made"), m * len(CH) + c + 1)
                    act.activation(y[:, lo:hi], bank[c % 8][:, 0:hi - lo], ACT.Identity,
                                   bias=cols[:, 3 * m:3 * m + 1]).then_inc(sem("lin_copied"), 1)
                act.wait_ge(sem("bvar_made"), m + 1)
                act.activation(stat[:, 0:1], stat[:, 1:2], ACT.Sqrt).then_inc(sem("broot_made"), 1)
                act.wait_ge(sem("bscale_made"), m + 1)
                for lo, hi in CH:
                    act.activation(y[:, lo:hi], y[:, lo:hi], ACT.Relu, bias=stat[:, 3:4],
                                   scale=stat[:, 2:3]).then_inc(sem("relu_done"), 1)
            for c in range(NB // EC):
                act.wait_ge(sem("ovar_made"), c + 1)
                act.activation(stat[:, 0:EC], stat[:, EC:2 * EC], ACT.Sqrt).then_inc(sem("oroot_made"), 1)

        @block.tensor
        def _(pe):
            mm, turn = nc.tensor.matmul, nc.tensor.transpose
            PE_ = mybir.EngineType.PE

            pe.wait_ge(sem("descents_counted"), 1)
            mm(bank[0][0:1, 0:1], before_f[:, 0:1], ones_f[:, 0:1], start=True, stop=True).then_inc(sem("descents_summed"), 1)
            pe.wait_ge(sem("order_checked"), 1)
            unsorted = pe.value_load(unsorted_i[:, :])
            with pe.If(unsorted > 0):
                with pe.Fori(0, NT) as t:
                    pe.wait_ge(sem("digits_hot"), t + 1)
                    mm(bank[0][:, 0:NB], one_lo, one_hi, start=True, stop=True).then_inc(sem("count_made"), 1)
                pe.wait_ge(sem("counts_made"), 1)
                mm(bank[0][:, 0:NB], earlier, counts, start=True, stop=True)
                mm(bank[0][:, 128:128 + NB], ones_f, counts, start=True, stop=True).then_inc(sem("prefix_made"), 1)
                with pe.Fori(0, NT) as t:
                    pe.wait_ge(sem("digits2_hot"), t + 1)
                    turn(bank[1][:, 0:P], one_lo, ident).then_inc(sem("lo_turned"), 1)
                    pe.wait_ge(sem("loT_copied"), t + 1)
                    mm(bank[0][:, 0:NB], one_loT, nextp, start=True, stop=True)
                    mm(bank[0][:, 128:128 + NB], one_lo, one_hi, start=True, stop=True).then_inc(sem("base_made"), 1)

            pe.wait_ge(sem("start_made"), 1)
            for c in range(-(-NT // 512)):
                n = min(NT - c * 512, 512)
                mm(bank[c][:, 0:n], ones1, start_row[:, c * 512:c * 512 + n],
                   start=True, stop=True).then_inc(sem("starts_spread"), 1)

            def turn_xm(b, u):
                pe.wait_ge(sem("xm_made"), b + 1)
                for t in range(TYPES):
                    last = turn(bank[u][:, t * P:(t + 1) * P], xm[u][:, t * P:(t + 1) * P], ident)
                last.then_inc(sem("xm_turned"), 1)

            def make_qkv(b, u):
                pe.wait_ge(sem("q_split"), b + 1)
                pe.wait_ge(sem("xmT_copied"), b + 1)
                hot3 = types_s[:, u * P:(u + 1) * P]
                for j, w in enumerate((Wk_s, Wv_s)):
                    o = bank[2 + u][:, j * P:(j + 1) * P]
                    for t in range(TYPES):
                        mm(o, w[:, t * P:(t + 1) * P], xmT[u][:, t * P:(t + 1) * P], start=(t == 0), stop=False)
                    mm(o, bias3[:, j * P:(j + 1) * P], hot3, start=False, stop=True)
                o = bank[2 + u][:, 2 * P:3 * P]
                for t in range(TYPES):
                    mm(o, xmT[u][:, t * P:(t + 1) * P], Wq_s[:, t * P:(t + 1) * P], start=(t == 0), stop=False)
                mm(o, hot3, bias3[:, 2 * P:3 * P], start=False, stop=True).then_inc(sem("qkv_made"), 1)

            def make_tab(b, u):
                pe.wait_ge(sem("tabv_copied"), b + 1)
                pe.wait_ge(sem("kvT_copied"), b + 1)
                mm(bank[4 + u], kvT[u][:, 0:P], relk, start=True, stop=True)
                mm(bank[6 + u], kvT[u][:, P:2 * P], relv, start=True, stop=True).then_inc(sem("tab_made"), 1)

            pe.wait_ge(sem("consts_loaded"), 16 * NCONST)
            pe.wait_ge(sem("masks_made"), 1)
            pe.wait_ge(sem("starts_copied"), -(-NT // 512))
            turn_xm(0, 0)
            turn_xm(1, 1)
            make_qkv(0, 0)
            with pe.Fori(0, NK // 2 - 1) as i:
                for u in range(2):
                    b = 2 * i + u
                    make_qkv(b + 1, 1 - u)
                    turn_xm(b + 2, u)
                    make_tab(b, u)
            make_qkv(NK - 1, 1)
            turn_xm(NK, 0)
            make_tab(NK - 2, 0)
            make_qkv(NK, 0)
            make_tab(NK - 1, 1)
            make_tab(NK, 0)

            pe.wait_ge(sem("arrays_made"), 1)
            pe.wait_ge(sem("tabk_copied"), NB)
            turn(bank[4][0:SG, 0:P], small[:, SG:2 * SG], ident).then_inc(sem("blk_turned"), 1)
            for g in range(SG):
                if g >= 2:
                    pe.wait_ge(sem("reca_copied"), g - 1)
                    pe.wait_ge(sem("recb_copied"), g - 1)
                for j, w in enumerate((7, 1, 2, 9)):
                    last = turn(bank[g % 2 * 2][:, j * P:(j + 1) * P], W(w)[:, g * P:(g + 1) * P], ident)
                last.then_inc(sem("reca_turned"), 1)
                for j, w in enumerate((3, 8, 6)):
                    last = turn(bank[g % 2 * 2 + 1][:, j * P:(j + 1) * P], W(w)[:, g * P:(g + 1) * P], ident)
                last.then_inc(sem("recb_turned"), 1)

            def turn_hot(k, par, half):
                pe.wait_ge(sem("hot_made"), 4 * k + 2 * half + 2)
                if half:
                    pe.wait_ge(sem("hotT_copied"), 2 * k + 1)
                for t in range(8):
                    last = turn(bank[3].bitcast(BF16)[:, t * P:(t + 1) * P],
                                hot_step_bf16(par, 8 * half + t), identb)
                last.then_inc(sem("hot_turned"), 1)

            def spread_q(k, q, regs):
                if q % 2 == 0:
                    pe.wait_ge(sem("hotT_copied"), 2 * k + q // 2 + 1)
                for j in range(4):
                    t = 4 * q + j
                    for part in range(3):
                        last = mm(bank[Q_BANK[q]][:, j * P:(j + 1) * P], hotT[:, t * P:(t + 1) * P],
                                  Qsplit[:, bass.ds(regs[t] * (3 * P) + part * P, P)],
                                  start=(part == 0), stop=(part == 2))
                last.then_inc(sem("q_spread"), 1)

            pe.wait_ge(sem("blk_loaded0"), 16)
            pe.wait_ge(sem("reca_copied"), SG)
            pe.wait_ge(sem("recb_copied"), SG)
            regs = load_regs(PE_, blk_slot[0][:, 0:12], NB - 1)
            for half in range(2):
                turn_hot(0, 0, half)
            for q in range(3):
                spread_q(0, q, regs)

            def sum_edges(k, u, ts):
                for t in ts:
                    if t % 2 == 0:
                        pe.wait_ge(sem("acc_done"), STEPS * k + t + 2)
                    mm(bank[5 + t % RING // 2][:, t % 2 * 256:t % 2 * 256 + SUMW], hot_step((u + 1) % 2, t),
                       rows3[:, t, 0:SUMW], start=True, stop=True).then_inc(sem("sum_made"), 1)
                    last = mm(bank[7][0:2 * STEPS, u % 2 * 256:u % 2 * 256 + ROWW],
                              ends[:, t * 2 * STEPS:(t + 1) * 2 * STEPS], rows3[:, t, :],
                              start=(t == 0), stop=(t == STEPS - 1))
                    if t == STEPS - 1:
                        last.then_inc(sem("ends_summed"), 1)

            with pe.Fori(0, ROUNDS // SLOTS) as i:
                for u in range(SLOTS):
                    k = SLOTS * i + u
                    pe.wait_ge(sem("msg_ready"), 4 * k + 1)
                    sum_edges(k, u, range(0, 2))
                    regs = [None] * 12 + list(load_regs(PE_, blk_slot[u][:, 12:16], NB - 1))
                    pe.wait_ge(sem("q_used"), 4 * k + 1)
                    spread_q(k, 3, regs)
                    sum_edges(k, u, range(2, 6))
                    pe.wait_ge(sem("att_made"), 4 * (k + 1))
                    turn(bank[2][:, 0:P], att, ident).then_inc(sem("att_turned"), 1)
                    sum_edges(k, u, range(6, 12))
                    pe.wait_ge(sem("shift_made"), k + 1)
                    turn(bank[2][:, P:2 * P], shifted, ident)
                    turn(bank[2][:, 2 * P:3 * P], seg, ident).then_inc(sem("shift_turned"), 1)
                    sum_edges(k, u, range(12, 14))
                    turn_hot(k + 1, (u + 1) % 2, 0)
                    sum_edges(k, u, range(14, 16))
                    pe.wait_ge(sem(f"blk_loaded{(u + 1) % SLOTS}"), 16 * (i + 1 + (u + 1) // SLOTS))
                    turn_hot(k + 1, (u + 1) % 2, 1)
                    regs = load_regs(PE_, blk_slot[(u + 1) % SLOTS][:, 0:12], NB - 1)
                    for q, used in ((0, 4), (1, 2), (2, 3)):
                        pe.wait_ge(sem("q_used"), 4 * k + used)
                        spread_q(k + 1, q, regs)
            pe.wait_ge(sem("msg_ready"), 4 * ROUNDS + 1)
            pe.wait_ge(sem("list_copied"), ROUNDS)
            sum_edges(ROUNDS, 0, range(STEPS))

            pe.wait_ge(sem("mval_made"), 1)
            pe.wait_ge(sem("list_copied"), ROUNDS + 1)
            nc4 = -(-LG // 4)
            for w, of in ((0, mval), (1, key8)):
                for c in range(nc4):
                    if w:
                        pe.wait_ge(sem("list_taken"), c + 1)
                    for g in range(4 * c, min(4 * c + 4, LG)):
                        last = turn(bank[c][0:HEADS, g % 4 * P:(g % 4 + 1) * P], of[:, g * HEADS:(g + 1) * HEADS], ident)
                    last.then_inc(sem("list_turned"), 1)
            pe.wait_ge(sem("keys_filled"), 1)
            pe.wait_ge(sem("list_taken"), 2 * nc4)
            for g in range(LG):
                last = turn(bank[1][:, g * HEADS:(g + 1) * HEADS], keyT[:, g * P:(g + 1) * P], ident[0:HEADS, 0:HEADS])
            last.then_inc(sem("keys_back"), 1)
            pe.wait_ge(sem("mexp_done"), 1)
            for g in range(LG):
                last = turn(bank[0][:, g * HEADS:(g + 1) * HEADS], mT[:, g * P:(g + 1) * P], ident[0:HEADS, 0:HEADS])
            last.then_inc(sem("factors_back"), 1)
            pe.wait_ge(sem("mblk_made"), 1)
            mm(bank[4][:, 0:MS], ones1, mblk_f, start=True, stop=True).then_inc(sem("mbase_spread"), 1)
            with pe.Fori(0, MR) as i:
                regs = load_regs(PE_, mtile_i[:, bass.ds(i * MERGES, MERGES)], LG - 1)
                for j in range(MERGES):
                    pe.wait_ge(sem("mhot_made"), MERGES * i + j + 1)
                    mm(bank[2 + j // 3][:, j % 3 * AW:(j % 3 + 1) * AW], hot[:, j * P:(j + 1) * P],
                       plist[:, bass.ds(regs[j] * ROWW, AW)], start=True, stop=True).then_inc(sem("msum_made"), 1)

            with pe.Fori(0, NB // EC) as i:
                pe.wait_ge(sem("hm_made"), i + 1)
                for j in range(EC):
                    for t in range(TYPES):
                        last = turn(bank[j][:, t * P:(t + 1) * P], hm[:, (t * EC + j) * P:(t * EC + j + 1) * P], ident)
                    last.then_inc(sem("hm_turned"), 1)
                for j in range(EC):
                    pe.wait_ge(sem("hmT_copied"), EC * (i + 1))
                    hot3 = types_s[:, j * P:(j + 1) * P]
                    o = bank[j // 4][:, j % 4 * P:(j % 4 + 1) * P]
                    for t in range(TYPES):
                        mm(o, hmT[:, (j * TYPES + t) * P:(j * TYPES + t + 1) * P], Wa_s[:, t * P:(t + 1) * P],
                           start=(t == 0), stop=False)
                    mm(o, hot3, bias3[:, 3 * P:4 * P], start=False, stop=True)
                    last = mm(bank[2 + j // 2][:, j % 2 * 256:j % 2 * 256 + 256], hot3, bias3[:, 4 * P:6 * P],
                              start=True, stop=True)
                last.then_inc(sem("trans_made"), 1)

            pe.wait_ge(sem("x1_made"), NB // EC)
            for c, (lo, hi) in enumerate(CH):
                if c >= 8:
                    pe.wait_ge(sem("agg_begun"), c - 7)
                for b in range(lo // P, hi // P):
                    last = turn(bank[c % 8][:, b * P - lo:b * P - lo + P], X[:, b * P:(b + 1) * P], ident)
                last.then_inc(sem("x1_turned"), 1)

            pe.wait_ge(sem("agg_begun"), len(CH))
            with pe.Fori(0, ROUNDS // SLOTS) as i:
                for u in range(SLOTS):
                    k = SLOTS * i + u
                    pe.wait_ge(sem(f"xg_loaded{u}"), 16 * STEPS * (i + 1))
                    for t in range(STEPS):
                        if t % 4 == 0:
                            pe.wait_ge(sem("hot2_made"), 4 * k + t // 4 + 1)
                            pe.wait_ge(sem("agg_done"), STEPS * k + t + 4)
                        mm(bank[t // 4][:, t % 4 * P:(t % 4 + 1) * P], xg_slot[u][:, t * P:(t + 1) * P],
                           hot_step(u % 2, t), start=True, stop=True).then_inc(sem("agg_made"), 1)

            pe.wait_ge(sem("agg_done"), STEPS * (ROUNDS + 1))
            for m, of in ((0, aggT), (1, y1)):
                if m:
                    pe.wait_ge(sem("relu_done"), len(CH))
                for c, (lo, hi) in enumerate(CH):
                    if m * len(CH) + c >= 8:
                        pe.wait_ge(sem("lin_copied"), m * len(CH) + c - 7)
                    mm(bank[c % 8][:, 0:hi - lo], W12[:, m * P:(m + 1) * P], of[:, lo:hi],
                       start=True, stop=True).then_inc(sem("lin_made"), 1)
            pe.wait_ge(sem("relu_done"), 2 * len(CH))
            for c in range(NB // EC):
                if c >= 4:
                    pe.wait_ge(sem("h2_used"), c - 3)
                for j in range(EC):
                    last = turn(bank[c % 4 * 2 + j // 4][:, j % 4 * P:(j % 4 + 1) * P],
                                y2[:, (c * EC + j) * P:(c * EC + j + 1) * P], ident)
                last.then_inc(sem("h2_turned"), 1)

        @block.vector
        def _(dve):
            v = nc.vector
            link = Chain(dve, sem("dve_chain"))
            then = link.then
            DVE_ = mybir.EngineType.DVE

            v.memset(tail_d, PADNODE).then_inc(sem("tails_set"), 1)
            v.memset(tail_z, 0).then_inc(sem("tails_set"), 1)
            v.memset(relk, 0.0)
            v.memset(relv, 0.0).then_inc(sem("rels_zeroed"), 1)
            v.memset(X[:, NK * P:NB * P], 0.0)
            v.memset(ntype_i, 0)
            v.memset(types_i, 0).then_inc(sem("nodes_zeroed"), 1)
            v.memset(resets, 0.0).then_inc(sem("resets_zeroed"), 1)
            v.memset(ones1, 1.0)
            dve.wait_ge(sem("patterns_made"), 4)
            v.tensor_copy(iota_f, iota_i)
            v.tensor_copy(step_f, misc_i[:, 0:SG])
            v.tensor_copy(tcol, misc_i[0:TYPES, SG:SG + 1])
            v.tensor_copy(tcount, tcount_i)
            then(v.tensor_copy(pcol, misc_i[:, SG:SG + 1]))
            v.tensor_scalar(identb, iota_f, pcol, None, ALU.is_equal)
            then(v.tensor_scalar(ident, iota_f, pcol, None, ALU.is_equal))

            v.memset(ones_f, 1.0)
            dve.wait_ge(sem("order_loaded"), 48)
            then(v.tensor_tensor(descents[:, 0:NT - 1], order_a[:, 0:NT - 1], order_b[:, 0:NT - 1], ALU.is_gt))
            then(v.memset(descents[:, NT - 1:NT], 0.0))
            then(v.tensor_tensor(descents[0:P - 1, NT - 1:NT], order_a[0:P - 1, NT - 1:NT], order_b[0:P - 1, NT - 1:NT],
                                 ALU.is_gt))
            v.tensor_reduce(before_f[:, 0:1], descents, AX.X, ALU.add).then_inc(sem("descents_counted"), 1)
            dve.wait_ge(sem("descents_summed"), 1)
            v.tensor_copy(unsorted_i, bank[0][0:1, 0:1]).then_inc(sem("order_checked"), 1)
            dve.wait_ge(sem("order_checked"), 1)
            unsorted = dve.value_load(unsorted_i[:, :])
            srt_link = Chain(dve, sem("sort_chain"))
            then_s = srt_link.then

            def digit_hots():
                then_s(v.tensor_scalar(digits_i[:, 0:1], edge3[:, 0:1], P - 1, None, ALU.bitwise_and))
                then_s(v.tensor_scalar(digits_i[:, 1:2], edge3[:, 0:1], 7, None, ALU.arith_shift_right))
                then_s(v.tensor_copy(digits_f, digits_i))
                then_s(v.tensor_scalar(one_lo, iota_f, digits_f[:, 0:1], None, ALU.is_equal))
                then_s(v.tensor_scalar(one_hi, iota_f[:, 0:NB], digits_f[:, 1:2], None, ALU.is_equal))

            with dve.If(unsorted > 0):
                then_s(v.memset(counts, 0.0))
                then_s(v.tensor_scalar(later, iota_f, pcol, None, ALU.is_lt))
                then_s(v.tensor_scalar(earlier, iota_f, pcol, None, ALU.is_gt))
                dve.sem_inc(sem("tile_counted"), 1)
                with dve.Fori(0, NT) as t:
                    srt_link.enter(t, 6)
                    dve.wait_ge(sem("count_loaded"), 16 * (t + 1))
                    digit_hots()
                    dve.sem_inc(sem("digits_hot"), 1)
                    dve.wait_ge(sem("count_made"), t + 1)
                    then_s(v.tensor_tensor(counts, counts, bank[0][:, 0:NB], ALU.add))
                    dve.sem_inc(sem("tile_counted"), 1)
                srt_link.leave(NT)
                dve.sem_inc(sem("counts_made"), 1)
                dve.wait_ge(sem("prefix_made"), 1)
                then_s(v.tensor_copy(counts, bank[0][:, 128:128 + NB]))
                then_s(v.memset(before_f, 0.0))
                then_s(v.tensor_tensor_scan(nextp, counts, before_f, 0.0, ALU.add, ALU.add))
                then_s(v.tensor_tensor(nextp, nextp, counts, ALU.subtract))
                then_s(v.tensor_tensor(nextp, nextp, bank[0][:, 0:NB], ALU.add))
                dve.sem_inc(sem("tile_ranked"), 1)
                with dve.Fori(0, NT) as t:
                    srt_link.enter(t, 16)
                    dve.wait_ge(sem("place_loaded"), 64 * (t + 1))
                    digit_hots()
                    dve.sem_inc(sem("digits2_hot"), 1)
                    then_s(v.tensor_copy(row_f, row_i))
                    then_s(v.tensor_copy(dst_f, edge3[:, 0:1]))
                    then_s(v.tensor_scalar(row_f, row_f, dst_f, None, ALU.is_equal))
                    then_s(v.tensor_tensor(row_f, row_f, later, ALU.mult))
                    then_s(v.tensor_reduce(rank, row_f, AX.X, ALU.add))
                    dve.wait_ge(sem("lo_turned"), t + 1)
                    then_s(v.tensor_copy(one_loT, bank[1][:, 0:P]))
                    dve.sem_inc(sem("loT_copied"), 1)
                    dve.wait_ge(sem("base_made"), t + 1)
                    then_s(v.tensor_tensor(before_f, bank[0][:, 0:NB], one_hi, ALU.mult))
                    then_s(v.tensor_reduce(base_f, before_f, AX.X, ALU.add))
                    then_s(v.tensor_tensor(base_f, base_f, rank, ALU.add))
                    then_s(v.tensor_copy(place_i, base_f))
                    then_s(v.tensor_tensor(nextp, nextp, bank[0][:, 128:128 + NB], ALU.add))
                    dve.sem_inc(sem("tile_ranked"), 1)
                srt_link.leave(NT)

            dve.wait_ge(sem("last_loaded"), 16)
            then(v.tensor_scalar(last_b, last_i, 7, None, ALU.arith_shift_right))
            then(v.tensor_copy(start_row, last_b))
            v.tensor_tensor(start_row, start_row, tcount, ALU.add).then_inc(sem("start_made"), 1)
            dve.wait_ge(sem("starts_copied"), -(-NT // 512))
            for g in range(SG):
                then(v.tensor_scalar(started[:, 0:NT - 1], starts[:, 0:NT - 1], step_f[:, g:g + 1], None, ALU.is_le))
                then(v.tensor_reduce(small[:, g:g + 1], started[:, 0:NT - 1], AX.X, ALU.add))
            v.tensor_copy(tile_i, small[:, 0:SG]).then_inc(sem("tiles_made"), 1)
            then(v.tensor_tensor(small[:, SG:2 * SG], step_f, small[:, 0:SG], ALU.subtract))
            then(v.tensor_scalar(small[:, 2 * SG:3 * SG], small[:, SG:2 * SG], float(P), None, ALU.mult))

            dve.wait_ge(sem("consts_loaded"), 16 * NCONST)
            then(v.tensor_copy(ntype_f, ntype_i))
            for t in range(TYPES):
                then(v.tensor_scalar(tmask[:, t * NB:(t + 1) * NB], ntype_f, float(t), None, ALU.is_equal))
            then(v.tensor_scalar(onehot3, types_i, tcol, None, ALU.is_equal))
            for r in range(RELS):
                v.tensor_scalar(relk[:, r * P:(r + 1) * P], relk[:, r * P:(r + 1) * P], pri[:, r:r + 1],
                                DK ** -0.5, ALU.mult, ALU.mult)
            then(v.tensor_scalar(cols[:, 7:8], cols[:, 6:7], 1.0, None, ALU.add))
            dve.sem_inc(sem("masks_made"), 1)
            dve.wait_ge(sem("skip_gated"), 1)
            then(v.tensor_scalar(gate, tmask[:, 0:NB], skip_s[:, 0:1], None, ALU.mult))
            for t in range(1, TYPES):
                then(v.scalar_tensor_tensor(gate, tmask[:, t * NB:(t + 1) * NB], skip_s[:, t:t + 1], gate,
                                            ALU.mult, ALU.add))
            then(v.tensor_scalar(ungate, gate, -1.0, 1.0, ALU.mult, ALU.add))

            def mask_type(b, u, t):
                ins = v.tensor_scalar(xm[u][:, t * P:(t + 1) * P], X[:, bass.ds(b * P, P)],
                                      tmask[:, bass.ds(t * NB + b, 1)], None, ALU.mult)
                if t == TYPES - 1:
                    ins.then_inc(sem("xm_made"), 1)

            def node_types(b, u):
                v.tensor_scalar(types_s[:, u * P:(u + 1) * P], onehot3[:, bass.ds(b * P, P)], 0.0, None, ALU.add)

            def split_q(b, u, ahead):
                dve.wait_ge(sem("kvT_copied"), b + 1)
                q = bank[2 + u][:, 2 * P:3 * P]
                parts = [Qsplit[:, bass.ds(b * (3 * P) + j * P, P)] for j in range(3)]
                link.mark(v.tensor_scalar(parts[0], q, 0.0, None, ALU.add))
                if ahead is not None:
                    node_types(ahead, u)
                link.reach()
                link.mark(v.tensor_tensor(rest, q, parts[0], ALU.subtract))
                if ahead is not None:
                    mask_type(ahead, u, 0)
                link.reach()
                link.mark(v.tensor_scalar(parts[1], rest, 0.0, None, ALU.add))
                if ahead is not None:
                    mask_type(ahead, u, 1)
                link.reach()
                link.mark(v.tensor_tensor(parts[2], rest, parts[1], ALU.subtract))
                if ahead is not None:
                    mask_type(ahead, u, 2)
                link.reach()
                dve.sem_inc(sem("q_split"), 1)

            def copy_tabv(b, u):
                dve.wait_ge(sem("tab_made"), b + 1)
                dve.wait_ge(sem("tab_free"), b + 1)
                v.tensor_copy(tab_s[u].rearrange("p (r c) -> p r c", r=RELS)[:, :, P:2 * P],
                              bank[6 + u].rearrange("p (r c) -> p r c", r=RELS)).then_inc(sem("tabv_copied"), 1)

            dve.sem_inc(sem("q_split"), 2)
            dve.sem_inc(sem("tabv_copied"), 2)
            for b in range(2):
                node_types(b, b)
                for t in range(TYPES):
                    mask_type(b, b, t)
            split_q(0, 0, 2)
            with dve.Fori(0, NK // 2 - 1) as i:
                link.enter(i, 8)
                for u in range(2):
                    b = 2 * i + u
                    split_q(b + 1, 1 - u, b + 3)
                    copy_tabv(b, u)
            link.leave(NK // 2 - 1)
            split_q(NK - 1, 1, None)
            copy_tabv(NK - 2, 0)
            split_q(NK, 0, None)
            copy_tabv(NK - 1, 1)
            copy_tabv(NK, 0)

            dve.wait_ge(sem("rows_gathered"), 16 * 3 * SG)
            W3 = [W(j).rearrange("s (g e) -> s g e", e=P) for j in range(10)]
            v.tensor_copy(W(5), W(2).bitcast(I32))
            v.tensor_copy(W(6), W(3).bitcast(I32))
            then(v.tensor_copy(W(7), W(4).bitcast(I32)))
            then(v.scalar_tensor_tensor(W(8), W(6), float(RELS), W(7), ALU.mult, ALU.add))
            then(v.tensor_tensor(W3[7], W3[5], spread(small[:, 2 * SG:3 * SG], P), ALU.subtract))
            then(v.tensor_scalar(W(0), W(7), 0.0, None, ALU.is_ge))
            then(v.scalar_tensor_tensor(W(0), W(7), float(P - 1), W(0), ALU.is_le, ALU.mult))
            v.memset(W3[9][:, :, 0:1], 1.0)
            then(v.tensor_tensor(W3[9][:, :, 1:P], W3[5][:, :, 1:P], W3[5][:, :, 0:P - 1], ALU.not_equal))
            v.tensor_scalar(W(4), W(9), -BIG, None, ALU.mult).then_inc(sem("resets_made"), 1)
            v.tensor_tensor(W(3), W(5), W(9), ALU.mult)
            v.tensor_tensor(W3[1], W3[5], W3[5][:, :, 0:1].to_broadcast([P, SG, P]), ALU.is_equal)
            then(v.tensor_tensor(W3[2], W3[5], W3[5][:, :, P - 1:P].to_broadcast([P, SG, P]), ALU.is_equal))
            then(v.scalar_tensor_tensor(W(2), W(1), 0.0, W(2), ALU.is_equal, ALU.mult))
            v.tensor_tensor(W(2), W(2), W(0), ALU.mult)
            then(v.tensor_tensor(W(1), W(1), W(0), ALU.mult))
            dve.sem_inc(sem("arrays_made"), 1)
            then(v.memset(pad_s, -1.0))
            dve.sem_inc(sem("pad_set"), 1)
            dve.wait_ge(sem("blk_turned"), 1)
            v.tensor_scalar(blkT, bank[4][0:SG, 0:P], float(NB - 1), None, ALU.min).then_inc(sem("blk_made"), 1)
            for g in range(SG):
                dve.wait_ge(sem("recb_turned"), g + 1)
                dve.wait_ge(sem("recs_free"), g + 1)
                to = rec_s[g % 2].rearrange("e (k c s) -> e c k s", c=7, s=STEPS)
                of = bank[g % 2 * 2 + 1][:, 0:3 * P].rearrange("e (c k s) -> e c k s", c=3, s=STEPS)
                v.tensor_copy(to[:, C_HEADKEY], of[:, 0])
                v.tensor_copy(to[:, C_KVROW].bitcast(I32), of[:, 1])
                v.tensor_copy(to[:, C_SRC].bitcast(I32), of[:, 2]).then_inc(sem("recb_copied"), 1)

            def one_hot_quad(par, u, q, made):
                key = rec_col(u, C_KEY)[:, 4 * q:4 * q + 4]
                v.tensor_tensor(hot[:, (par * STEPS + 4 * q) * P:(par * STEPS + 4 * q + 4) * P]
                                .rearrange("e (t n) -> e t n", n=P),
                                iota_f.unsqueeze(1).to_broadcast([P, 4, P]), spread(key, P),
                                ALU.is_equal).then_inc(made, 1)

            def one_hot(par, u, made):
                for q in range(4):
                    one_hot_quad(par, u, q, made)

            v.memset(acc, 0.0).then_inc(sem("acc_done"), RING)
            dve.wait_ge(sem("rec_loaded0"), 16)
            dve.wait_ge(sem("rec_stored0"), 16 * ((SG + 1) // 2))
            dve.wait_ge(sem("rec_stored1"), 16 * (SG // 2))
            dve.wait_ge(sem("acc_done"), RING)
            one_hot(0, 0, sem("hot_made"))
            v.memset(ends, 0.0)
            v.memset(hot[:, STEPS * P:2 * STEPS * P], 0.0)
            v.memset(rows, 0.0).then_inc(sem("msg_ready"), 1)

            def add_sums(k, ts, regs):
                for t in ts:
                    dve.wait_ge(sem("acc_done"), RING + STEPS * k + t)
                    if t % 2 == 0:
                        dve.wait_ge(sem("sum_made"), STEPS * k + t + 2)
                    a = acc[:, bass.ds(regs[t] * SUMW, SUMW)]
                    v.tensor_tensor(a, bank[5 + t % RING // 2][:, t % 2 * 256:t % 2 * 256 + SUMW], a,
                                    ALU.add).then_inc(sem("acc_done"), 1)

            dve.wait_ge(sem("blk_loaded3"), 16)
            with dve.Fori(0, ROUNDS // SLOTS) as i:
                for u in range(SLOTS):
                    k = SLOTS * i + u
                    regs = load_regs(DVE_, blk_slot[u - 1], NB - 1)
                    dve.wait_ge(sem(f"kv_loaded{u}"), 16 * STEPS * (i + 1))
                    kv3 = kv_slot[u].rearrange("e (t c) -> e t c", c=2 * P)
                    pr = [prod[:, q * 512:q * 512 + 512] for q in range(2)]

                    def product(q):
                        dve.wait_ge(sem("q_spread"), 4 * k + q + 1)
                        v.tensor_tensor(pr[q % 2].rearrange("e (t c) -> e t c", c=P), kv3[:, 4 * q:4 * q + 4, 0:P],
                                        bank[Q_BANK[q]].rearrange("e (t c) -> e t c", c=P),
                                        ALU.mult).then_inc(sem("q_used"), 1)

                    def head_sums(q):
                        dve.wait_ge(sem("q_used"), 4 * k + q + 1)
                        v.tensor_reduce(att[:, q * 32:q * 32 + 32], pr[q % 2].rearrange("e (a d) -> e a d", d=DK),
                                        AX.X, ALU.add).then_inc(sem("att_made"), 1)

                    product(0)
                    product(1)
                    head_sums(0)
                    head_sums(1)
                    dve.wait_ge(sem("att_made"), 4 * k + 1)
                    product(2)
                    add_sums(k, (0,), regs)
                    head_sums(2)
                    add_sums(k, (1,), regs)
                    dve.wait_ge(sem("att_made"), 4 * k + 2)
                    product(3)
                    add_sums(k, (2,), regs)
                    head_sums(3)
                    add_sums(k, (3, 4), regs)
                    dve.wait_ge(sem("att_turned"), k + 1)
                    dve.wait_ge(sem(f"reset_loaded{u}"), 16 * (i + 1))
                    rs = reset_slot[u]
                    v.tensor_tensor_scan(fwd, rs[:, 0:P], bank[2][:, 0:P], -BIG, ALU.add, ALU.max).then_inc(sem("scanned"), 1)
                    add_sums(k, (5, 6), regs)
                    dve.wait_ge(sem("scanned"), 2 * k + 1)
                    v.tensor_tensor_scan(seg[:, ::-1], rs[:, P:0:-1], fwd[:, ::-1], -BIG, ALU.add,
                                         ALU.max).then_inc(sem("scanned"), 1)
                    add_sums(k, (7, 8), regs)
                    dve.wait_ge(sem("scanned"), 2 * k + 2)
                    v.tensor_tensor(shifted, bank[2][:, 0:P], seg, ALU.subtract).then_inc(sem("shift_made"), 1)
                    if u + 1 < SLOTS:
                        dve.wait_ge(sem(f"rec_loaded{u + 1}"), 16 * (i + 1))
                    else:
                        dve.wait_ge(sem("rec_loaded0"), 16 * (i + 2))
                    add_sums(k, (9,), regs)
                    for q in range(4):
                        dve.wait_ge(sem("sum_made"), STEPS * k + 4 * q + 4)
                        one_hot_quad((u + 1) % 2, (u + 1) % SLOTS, q, sem("hot_made"))
                        add_sums(k, ((10,), (11,), (12,), ())[q], regs)
                    dve.wait_ge(sem("ends_summed"), k + 1)
                    v.tensor_copy(ends[:, 0:511:34], rec_col(u, C_FIRST))
                    v.tensor_copy(ends[:, 1:512:34], rec_col(u, C_LAST))
                    v.tensor_copy(rows3[:, :, M_KEY], rec_col(u, C_HEADKEY))
                    add_sums(k, (13,), regs)
                    dve.wait_ge(sem("exp_done"), k + 1)
                    w3 = weight.rearrange("e (t h) -> e t h", h=HEADS)
                    v.tensor_tensor(rows3[:, :, M_MAX:M_MAX + HEADS],
                                    bank[2][:, 2 * P:3 * P].rearrange("e (t h) -> e t h", h=HEADS),
                                    spread(rec_col(u, C_HEAD), HEADS), ALU.mult)
                    v.tensor_copy(rows3[:, :, M_EXP:M_EXP + HEADS], w3)
                    dve.wait_ge(sem(f"blk_loaded{u}"), 16 * (i + 1))
                    for q in range(4):
                        tt = slice(4 * q, 4 * q + 4)
                        v.tensor_tensor(rows3[:, tt, 0:P].rearrange("e t (h d) -> e t h d", d=DK),
                                        kv3[:, tt, P:2 * P].rearrange("e t (h d) -> e t h d", d=DK),
                                        w3[:, tt].unsqueeze(3).to_broadcast([P, 4, HEADS, DK]),
                                        ALU.mult).then_inc(sem("msg_ready"), 1)
                        add_sums(k, ((), (14,), (15,), ())[q], regs)
            add_sums(ROUNDS, range(STEPS), load_regs(DVE_, blk_slot[SLOTS - 1], NB - 1))

            dve.wait_ge(sem("list_loaded"), 16)
            g8 = lambda a: a.rearrange("p (g h) -> p g h", h=HEADS)
            den = pl[:, :, M_EXP:M_EXP + HEADS]
            v.tensor_copy(g8(key8), pl[:, :, M_KEY:M_KEY + 1].to_broadcast([P, LG, HEADS]))
            then(v.tensor_scalar(g8(mval), den, 0.0, -BIG, ALU.is_equal, ALU.mult))
            then(v.tensor_tensor(g8(mval), g8(mval), pl[:, :, M_MAX:M_MAX + HEADS], ALU.add))
            dve.sem_inc(sem("mval_made"), 1)
            v.tensor_scalar(pl[:, :, M_MAX:M_MAX + 1], pl[:, :, M_EXP:M_EXP + 1], 0.0, None, ALU.is_gt)
            dve.wait_ge(sem("list_taken"), 2 * -(-LG // 4))
            then(v.tensor_tensor_scan(keyT, keyT, keyT, 0.0, ALU.max, ALU.max))
            dve.sem_inc(sem("keys_filled"), 1)
            v.memset(resets2[:, 0:1], 1.0)
            v.memset(resets2[:, ENTRIES:ENTRIES + 1], 0.0)
            then(v.tensor_tensor(resets2[:, 1:ENTRIES], keyT[:, 1:ENTRIES], keyT[:, 0:ENTRIES - 1], ALU.not_equal))
            then(v.tensor_scalar(resets2, resets2, -BIG, None, ALU.mult))
            then(v.tensor_tensor_scan(seg2, resets2[:, 0:ENTRIES], mT, -BIG, ALU.add, ALU.max))
            then(v.tensor_tensor_scan(seg2[:, ::-1], resets2[:, ENTRIES:0:-1], seg2[:, ::-1], -BIG, ALU.add, ALU.max))
            v.tensor_tensor(mT, mT, seg2, ALU.subtract).then_inc(sem("mshift_made"), 1)
            dve.wait_ge(sem("patterns_made"), 6)
            v.tensor_copy(mstep_f, mtile_i)
            then(v.tensor_copy(mstart_f, mlast_i))
            mkeys = keyT[0:1, P - 1:(LG - 1) * P:P]
            then(v.tensor_copy(mlast_i, mkeys))
            then(v.tensor_scalar(mlast_i, mlast_i, 7, None, ALU.arith_shift_right))
            mc = mcount.rearrange("o (s g) -> o s g", g=LG - 1)
            then(v.tensor_copy(mblk_f[:, 0:LG - 1], mlast_i))
            then(v.tensor_tensor(mstart_f, mstart_f, mblk_f[:, 0:LG - 1], ALU.add))
            then(v.tensor_tensor(mc, mstart_f.unsqueeze(1).to_broadcast([1, MS, LG - 1]), spread(mstep_f, LG - 1), ALU.is_le))
            then(v.tensor_reduce(mtile_f, mc, AX.X, ALU.add))
            v.tensor_copy(mtile_i, mtile_f)
            then(v.tensor_tensor(mblk_f, mstep_f, mtile_f, ALU.subtract))
            v.tensor_scalar(mblk_i, mblk_f, float(NB - 1), None, ALU.min)
            then(v.tensor_scalar(mblk_f, mblk_f, float(P), None, ALU.mult))
            dve.sem_inc(sem("mblk_made"), 1)
            dve.wait_ge(sem("keys_back"), 1)
            then(v.tensor_copy(keyf, bank[1][:, 0:G8:HEADS]))
            dve.wait_ge(sem("mbase_spread"), 1)
            then(v.tensor_copy(mbase, bank[4][:, 0:MS]))
            dve.wait_ge(sem("factors_back"), 1)
            dve.sem_inc(sem("keys_merged"), 1)
            then(v.tensor_copy(factor, bank[0][:, 0:G8]))
            v.tensor_tensor(pl[:, :, 0:P].rearrange("p g (h d) -> p g h d", d=DK),
                            pl[:, :, 0:P].rearrange("p g (h d) -> p g h d", d=DK),
                            g8(factor).unsqueeze(3).to_broadcast([P, LG, HEADS, DK]), ALU.mult)
            then(v.tensor_tensor(den, den, g8(factor), ALU.mult))
            then(v.memset(acc2, 0.0))
            dve.sem_inc(sem("macc_done"), 1)
            with dve.Fori(0, MR) as i:
                rt = load_regs(DVE_, mtile_i[:, bass.ds(i * MERGES, MERGES)], LG - 1)
                rb = load_regs(DVE_, mblk_i[:, bass.ds(i * MERGES, MERGES)], NB - 1)
                for j in range(MERGES):
                    v.tensor_scalar(hot[:, j * P:(j + 1) * P], iota_f, mbase[:, bass.ds(i * MERGES + j, 1)],
                                    keyf[:, bass.ds(rt[j], 1)], ALU.add, ALU.is_equal).then_inc(sem("mhot_made"), 1)
                for j in range(MERGES):
                    dve.wait_ge(sem("macc_done"), MERGES * i + j + 1)
                    dve.wait_ge(sem("msum_made"), MERGES * (i + 1))
                    a = acc2[:, bass.ds(rb[j] * AW, AW)]
                    v.tensor_tensor(a, bank[2 + j // 3][:, j % 3 * AW:(j % 3 + 1) * AW], a,
                                    ALU.add).then_inc(sem("macc_done"), 1)

            dve.wait_ge(sem("macc_done"), MS + 1)
            dve.wait_ge(sem("types_loaded"), 16)
            if NPAD > N:
                then(v.memset(types2_i[:, N:NPAD], 0))
            then(v.tensor_scalar(onehot3b, types2_i, tcol, None, ALU.is_equal))

            def layer_norm(to, a, var_made, root_made, count):
                mean, var = stat[:, 2 * EC:3 * EC], stat[:, EC:2 * EC]
                then(v.tensor_reduce(mean, a, AX.X, ALU.add))
                then(v.tensor_scalar(mean, mean, 1.0 / P, None, ALU.mult))
                then(v.tensor_tensor(a, a, spread(mean, P), ALU.subtract))
                then(v.tensor_tensor(by_block(square), a, a, ALU.mult))
                then(v.tensor_reduce(var, by_block(square), AX.X, ALU.add))
                v.tensor_scalar(var, var, 1.0 / P, LN_EPS, ALU.mult, ALU.add).then_inc(var_made, 1)
                dve.wait_ge(root_made, count)
                then(v.reciprocal(stat[:, 0:EC], stat[:, 0:EC]))
                then(v.tensor_tensor(to, a, spread(stat[:, 0:EC], P), ALU.mult))

            with dve.Fori(0, NB // EC) as i:
                link.enter(i, 33)
                a2 = blocks(acc2, i, AW)
                f3, h3, r3, k3 = by_block(fin, SUMW), by_block(hbuf), by_block(res), by_block(kept)
                keep = stat[:, 3 * EC:4 * EC]
                then(v.tensor_scalar(keep, a2[:, :, SUMW], 0.0, None, ALU.is_equal))
                then(v.tensor_tensor(f3, blocks(acc, i, SUMW), spread(keep, SUMW), ALU.mult))
                then(v.tensor_tensor(f3, f3, a2[:, :, 0:SUMW], ALU.add))
                rd = stat[:, 8 * EC:8 * EC + EC * HEADS]
                rd3 = rd.rearrange("p (b h) -> p b h", h=HEADS)
                then(v.tensor_scalar(rd3, f3[:, :, P:SUMW], 1e-16, None, ALU.add))
                then(v.reciprocal(rd, rd))
                then(v.tensor_tensor(r3.rearrange("p b (h d) -> p b h d", d=DK),
                                     f3[:, :, 0:P].rearrange("p b (h d) -> p b h d", d=DK),
                                     rd3.unsqueeze(3).to_broadcast([P, EC, HEADS, DK]), ALU.mult))
                dve.sem_inc(sem("aggr_made"), 1)
                then(v.tensor_scalar(types_s, onehot3b[:, bass.ds(i * EW, EW)], 0.0, None, ALU.add))
                dve.wait_ge(sem("gelu_done"), i + 1)
                for t in range(TYPES):
                    then(v.tensor_tensor(by_block(hm[:, t * EW:(t + 1) * EW]), h3,
                                         spread(tmask[:, bass.ds(i * EC + t * NB, EC)], P), ALU.mult))
                dve.sem_inc(sem("hm_made"), 1)
                then(v.tensor_tensor(k3, blocks(X, i), spread(ungate[:, bass.ds(i * EC, EC)], P), ALU.mult))
                dve.wait_ge(sem("trans_made"), i + 1)
                for n in range(2):
                    m = min(4, EC - 4 * n)
                    then(v.tensor_tensor(r3[:, 4 * n:4 * n + m], bank[n][:, 0:m * P].rearrange("p (b c) -> p b c", c=P),
                                         spread(gate[:, bass.ds(i * EC + 4 * n, m)], P), ALU.mult))
                then(v.tensor_tensor(r3, r3, k3, ALU.add))
                layer_norm(k3, r3, sem("var_made"), sem("root_made"), 2 * i + 1)
                for n in range(4):
                    m = min(2, EC - 2 * n)
                    gains = bank[2 + n][:, 0:m * 256].rearrange("p (b c) -> p b c", c=256)
                    v.tensor_tensor(k3[:, 2 * n:2 * n + m], k3[:, 2 * n:2 * n + m], gains[:, :, 0:P], ALU.mult)
                    then(v.tensor_tensor(r3[:, 2 * n:2 * n + m], blocks(X, i)[:, 2 * n:2 * n + m], gains[:, :, P:2 * P], ALU.add))
                then(v.tensor_tensor(r3, r3, k3, ALU.add))
                layer_norm(blocks(X, i), r3, sem("var_made"), sem("root_made"), 2 * i + 2)
                dve.sem_inc(sem("x1_made"), 1)
            link.leave(NB // EC)

            dve.wait_ge(sem("agg_begun"), len(CH))
            dve.sem_inc(sem("agg_done"), STEPS)
            dve.wait_ge(sem("rec2_loaded0"), 16)
            one_hot(0, 0, sem("hot2_made"))
            with dve.Fori(0, ROUNDS // SLOTS) as i:
                for u in range(SLOTS):
                    k = SLOTS * i + u
                    if u + 1 < SLOTS:
                        dve.wait_ge(sem(f"rec2_loaded{u + 1}"), 16 * (i + 1))
                    else:
                        dve.wait_ge(sem("rec2_loaded0"), 16 * (i + 2))
                    dve.wait_ge(sem(f"blk2_loaded{u}"), 16 * (i + 1))
                    one_hot((u + 1) % 2, (u + 1) % SLOTS, sem("hot2_made"))
                    regs = load_regs(DVE_, blk_slot[u], NB - 1)
                    for t in range(STEPS):
                        dve.wait_ge(sem("agg_done"), STEPS * (k + 1) + t)
                        if t % 4 == 0:
                            dve.wait_ge(sem("agg_made"), STEPS * k + t + 4)
                        a = aggT[:, bass.ds(regs[t] * P, P)]
                        v.tensor_tensor(a, bank[t // 4][:, t % 4 * P:(t % 4 + 1) * P], a,
                                        ALU.add).then_inc(sem("agg_done"), 1)

            for m, y in ((0, y1), (1, y2)):
                for c, (lo, hi) in enumerate(CH):
                    dve.wait_ge(sem("lin_copied"), m * len(CH) + c + 1)
                    last = v.bn_stats(stat[:, 8 + 6 * c:14 + 6 * c], y[:, lo:min(hi, N)])
                then(last)
                then(v.bn_aggr(stat[:, 4:6], stat[:, 8:8 + 6 * len(CH)]))
                v.tensor_scalar(stat[:, 1:2], stat[:, 5:6], BN_EPS, None, ALU.add).then_inc(sem("bvar_made"), 1)
                dve.wait_ge(sem("broot_made"), m + 1)
                then(v.reciprocal(stat[:, 0:1], stat[:, 0:1]))
                then(v.tensor_tensor(stat[:, 2:3], stat[:, 0:1], cols[:, 3 * m + 1:3 * m + 2], ALU.mult))
                then(v.tensor_tensor(stat[:, 6:7], stat[:, 4:5], stat[:, 2:3], ALU.mult))
                v.tensor_tensor(stat[:, 3:4], cols[:, 3 * m + 2:3 * m + 3], stat[:, 6:7],
                                ALU.subtract).then_inc(sem("bscale_made"), 1)
                dve.wait_ge(sem("relu_done"), (m + 1) * len(CH))
            for c in range(NB // EC):
                xc = blocks(X, c)
                r3 = by_block(res)
                dve.wait_ge(sem("h2_turned"), c + 1)
                for n in range(2):
                    m = min(4, EC - 4 * n)
                    then(v.tensor_tensor(r3[:, 4 * n:4 * n + m],
                                         bank[c % 4 * 2 + n][:, 0:m * P].rearrange("p (b c) -> p b c", c=P),
                                         xc[:, 4 * n:4 * n + m], ALU.add))
                dve.sem_inc(sem("h2_used"), 1)
                then(v.tensor_tensor(r3, r3, xc, ALU.add))
                layer_norm(xc, r3, sem("ovar_made"), sem("oroot_made"), c + 1)
                dve.sem_inc(sem("out_made"), 1)


_INS = ["x", "src", "dst", "edge_type_4", "node_type_3"] + ["L0_gnn_" + n for n in (
    "Wk", "bk", "Wq", "bq", "Wv", "bv", "Wa", "ba", "rel_pri", "rel_att", "rel_msg", "skip", "ln_g", "ln_b")] + [
    "L1_gnn_" + n for n in ("eps", "W1", "b1", "g1", "be1", "W2", "b2", "g2", "be2")]


def kernel(**inputs):
    import numpy as np
    import concourse.bacc as bacc
    from concourse.bass_utils import run_bass_kernel_spmd as run

    nc = bacc.Bacc("TRN2", target_bir_lowering=False, num_devices=1)
    arrays, args = {}, []
    for name in _INS:
        a = np.ascontiguousarray(inputs[name])
        if a.ndim == 0:
            a = a.reshape(1)
        arrays[f"in_{name}"] = a
        args.append(nc.dram_tensor(f"in_{name}", a.shape, mybir.dt.from_np(a.dtype), kind="ExternalInput").ap())
    out = nc.dram_tensor("out_x", tuple(inputs["x"].shape), F32, kind="ExternalOutput").ap()
    gnn_kernel(nc, *args, out)
    r = run(nc, [arrays], core_ids=[0])
    return r.results[0]["out_x"]
```

```python
from contextlib import ExitStack

import concourse.bass as bass
from concourse import mybir

F32 = mybir.dt.float32
BF16 = mybir.dt.bfloat16
I32 = mybir.dt.int32
ALU = mybir.AluOpType
ACT = mybir.ActivationFunctionType
AX = mybir.AxisListType

P = 128
HEADS = 8
DK = 16
RELS = 4
TYPES = 3
STEPS = 16
SLOTS = 4
BIG = 1.0e30
LN_EPS = 1e-5
BN_EPS = 1e-5
C_KVROW, C_KEY, C_FIRST, C_LAST, C_HEAD, C_HEADKEY, C_SRC = range(7)
REC = 7 * STEPS
M_EXP, M_MAX, M_KEY = P, P + HEADS, P + 2 * HEADS
SUMW = P + HEADS
ROWW = P + 2 * HEADS + 1


class Chain:

    def __init__(self, eng, sem):
        self.eng, self.sem, self.base, self.n = eng, sem, 0, 0

    def then(self, ins):
        ins.then_inc(self.sem, 1)
        self.n += 1
        self.eng.wait_ge(self.sem, self.base + self.n)

    def mark(self, ins):
        ins.then_inc(self.sem, 1)
        self.n += 1

    def reach(self):
        self.eng.wait_ge(self.sem, self.base + self.n)

    def enter(self, i, per):
        self.start, self.per = self.base + self.n, per
        self.base, self.n = self.start + i * per, 0

    def leave(self, rounds):
        assert self.n == self.per, (self.n, self.per)
        self.base, self.n = self.start + rounds * self.per, 0


def gnn_kernel(nc, x, src, dst, edge_type, node_type, Wk, bk, Wq, bq, Wv, bv, Wa, ba, rel_pri, rel_att,
               rel_msg, skip, ln_g, ln_b, eps, W1, b1, g1, be1, W2, b2, g2, be2, out):
    N = x.shape[0]
    E = src.shape[0]
    NB = -(-N // P)
    LASTN = N - (NB - 1) * P
    NT = -(-E // P)
    TAIL = NT * P - E
    SG = -(-(NT + NB - 1) // P)
    S = SG * P
    ROUNDS = S // STEPS
    ENTRIES = 2 * S
    LG = ENTRIES // P
    MERGES = 5
    MR = -(-(LG + NB - 1) // MERGES)
    PADNODE = NB * P - 1
    EC = 7
    assert NB % EC == 0 and NB % 2 == 1 and PADNODE >= N and TAIL > 0 and ROUNDS % SLOTS == 0
    NPAD = NB * P
    NCONST = 49
    FULLE = [d for d in range(64, 4000) if E % d == 0][0]

    dram = nc.dram_tensor
    dst_p = dram("dst_p", (NT, P), I32).ap()
    src_p = dram("src_p", (NT, P), I32).ap()
    typ_p = dram("typ_p", (NT, P), I32).ap()
    sorted_d = dram("sorted_d", (NT * P, 3), I32).ap()
    kvtab = dram("kvtab", (NPAD * RELS, 2 * P), F32).ap()
    rec_d = dram("rec_d", (ROUNDS + 1, P, REC), F32).ap()
    reset_d = dram("reset_d", (S, P), F32).ap()
    blk_d = dram("blk_d", (ROUNDS + 1, STEPS), I32).ap()
    list_d = dram("list_d", (2 * STEPS + ENTRIES, ROWW), F32).ap()
    x1_d = dram("x1_d", (NPAD, P), F32).ap()

    with ExitStack() as ctx:
        def sb(name, shape, dt=F32):
            return ctx.enter_context(nc.sbuf_tensor(name, shape, dt))[:, :]

        sems = {}

        def sem(name):
            if name not in sems:
                sems[name] = ctx.enter_context(nc.semaphore(name))
            return sems[name]

        bank = [ctx.enter_context(nc.psum_tensor(f"bank{i}", [P, 512], F32))[:, :] for i in range(8)]

        A2 = LG * ROWW
        A3 = A2 + NB * (SUMW + 1)
        AR = max(10 * S, SLOTS * STEPS * 2 * P, A3 + ENTRIES, A3 + EC * (SUMW + P))
        QW = max(NB * 3 * P, 2 * NPAD + 6 * EC * P, 4 * ENTRIES)
        arena = sb("arena", [P, AR])
        X = sb("X", [P, NB * P])
        acc_s = sb("acc", [P, max(NB * SUMW, NPAD + TYPES * P)])
        Qsplit = sb("Qsplit", [P, QW], BF16)
        blks = sb("blks", [1, SLOTS * STEPS], I32)
        hot = sb("hot", [P, 2 * STEPS * P])
        rows = sb("rows", [P, STEPS * ROWW])
        rec = sb("rec", [P, SLOTS * REC])
        resets = sb("resets", [P, SLOTS * (P + 1)])
        prod = sb("prod", [P, 2 * 4 * P])
        att = sb("att", [P, P])
        fwd = sb("fwd", [P, P])
        seg = sb("seg", [P, P])
        shifted = sb("shifted", [P, P])
        weight = sb("weight", [P, P])
        hotT = sb("hotT", [P, 16 * P], BF16)
        ends = sb("ends", [P, STEPS * 2 * STEPS])
        listed = sb("listed", [P, SLOTS * ROWW])
        iota_f = sb("iota_f", [P, P])
        unsorted_i = sb("unsorted_i", [1, 1], I32)
        iota_i = sb("iota_i", [P, P], I32)
        ident = sb("ident", [P, P])
        identb = sb("identb", [P, P], BF16)
        ones1 = sb("ones1", [1, P])
        Wa_s = sb("Wa_s", [P, TYPES * P])
        pri = sb("pri", [P, RELS])
        W12 = sb("W12", [P, 2 * P])
        bias3 = sb("bias3", [TYPES, 6 * P])
        cols = sb("cols", [P, 8])
        skip_s = sb("skip_s", [P, TYPES])
        ntype_i = sb("ntype_i", [P, NB], I32)
        ntype_f = sb("ntype_f", [P, NB])
        tmask = sb("tmask", [P, TYPES * NB])
        gate = sb("gate", [P, NB])
        tcol = sb("tcol", [TYPES, 1])
        small = sb("small", [P, 3 * SG])
        misc_i = sb("misc_i", [P, SG + 1], I32)
        tile_i = sb("tile_i", [P, SG], I32)
        step_f = sb("step_f", [P, SG])
        stat = sb("stat", [P, 8 * EC + EC * HEADS])
        pcol = sb("pcol", [P, 1])
        ungate = sb("ungate", [P, NB])

        def W(i):
            return arena[:, i * S:(i + 1) * S]

        last_i = W(0)[0:1, 0:NT].bitcast(I32)
        last_b = W(1)[0:1, 0:NT].bitcast(I32)
        last_row = W(2)[0:1, 0:NT]
        passed = W(3)[:, 0:SG * (NB - 1)]
        diag = W(4)[0:NB, 0:NB]
        assert NB <= P and SG * (NB - 1) <= S
        order_a, order_b = (W(j)[:, 0:NT].bitcast(I32) for j in (0, 1))
        descents = W(2)[:, 0:NT]
        srt = W(8)
        edge3 = srt[:, 0:3].bitcast(I32)
        digits_i, digits_f, dst_f = srt[:, 3:5].bitcast(I32), srt[:, 5:7], srt[:, 7:8]
        rank, base_f, place_i = srt[:, 8:9], srt[:, 9:10], srt[:, 10:11].bitcast(I32)
        nextp, counts, before_f = W(4)[:, 0:NB], W(5)[:, 0:NB], W(6)[:, 0:NB]
        one_lo, one_hi, one_loT = W(7)[:, 0:P], acc_s[:, 0:NB], acc_s[:, P:2 * P]
        row_i, row_f = acc_s[:, 2 * P:3 * P].bitcast(I32), acc_s[:, 3 * P:4 * P]
        earlier, later, ones_f = hot[:, 0:P], hot[:, P:2 * P], hot[:, 2 * P:3 * P]
        tail_d = W(9)[0:1, 0:P].bitcast(I32)
        tail_z = W(8)[0:1, 0:P].bitcast(I32)
        blkT = prod[0:SG, P:2 * P].bitcast(I32)
        below = W(6)[0:NB, 0:NT]

        types_i = acc_s[0:TYPES, 0:NPAD].bitcast(I32)
        onehot3 = acc_s[0:TYPES, 0:NPAD]
        acc = acc_s[:, 0:NB * SUMW]
        NK = NB - 1

        xm = [hot[:, u * 384:(u + 1) * 384] for u in range(2)]
        xmT = [hot[:, 768 + u * 384:768 + (u + 1) * 384] for u in range(2)]
        kvT = [hot[:, 1536 + u * 256:1536 + (u + 1) * 256] for u in range(2)]
        tab_s = [rows[:, u * 1024:(u + 1) * 1024] for u in range(2)]
        rest = prod[:, 0:P]
        relk, relv = hot[:, 2048:2048 + 512], hot[:, 2560:2560 + 512]
        Wk_s, Wv_s = hot[:, 3072:3072 + 384], hot[:, 3456:3456 + 384]
        Wq_s = acc_s[:, NPAD:NPAD + TYPES * P]
        types_s = hotT.bitcast(F32)[0:TYPES, 0:EC * P]

        RECS = 4
        rec_s = [hot[:, u * 8 * REC:(u + 1) * 8 * REC] for u in range(RECS)]
        pad_s = prod[:, 0:REC]

        RING = 4
        Q_BANK = (0, 1, 4, 0)
        rec_slot = [rec[:, u * REC:(u + 1) * REC] for u in range(SLOTS)]
        reset_slot = [resets[:, u * (P + 1):(u + 1) * (P + 1)] for u in range(SLOTS)]
        blk_slot = [blks[:, u * STEPS:(u + 1) * STEPS] for u in range(SLOTS)]
        kv_slot = [arena[:, u * STEPS * 2 * P:(u + 1) * STEPS * 2 * P] for u in range(SLOTS)]
        xg_slot = [arena[:, u * STEPS * P:(u + 1) * STEPS * P] for u in range(SLOTS)]
        rows3 = rows.rearrange("e (t c) -> e t c", c=ROWW)
        hotb = hot.bitcast(BF16)

        def rec_col(u, c):
            return rec_slot[u][:, c * STEPS:(c + 1) * STEPS]

        def hot_step(par, t):
            o = (par * STEPS + t) * P
            return hot[:, o:o + P]

        def hot_step_bf16(par, t):
            o = (par * STEPS + t) * P * 2
            return hotb[:, o + 1:o + 2 * P:2]

        AW = SUMW + 1
        plist = arena[:, 0:A2]
        pl = plist.rearrange("p (g c) -> p g c", c=ROWW)
        acc2 = arena[:, A2:A3]
        Qf = Qsplit.bitcast(F32)
        mT = Qf[0:HEADS, 0:ENTRIES]
        keyT = Qf[0:HEADS, ENTRIES:2 * ENTRIES]
        resets2 = hot[0:HEADS, 0:ENTRIES + 1]
        seg2 = arena[0:HEADS, A3:A3 + ENTRIES]
        G8 = LG * HEADS
        mval, key8, factor, keyf = (rows[:, 0:G8], rows[:, G8:2 * G8], rows[:, 2 * G8:3 * G8],
                                    rows[:, 3 * G8:3 * G8 + LG])
        MS = MR * MERGES
        merge_i = prod[0:1, 512:512 + 2 * MS + LG].bitcast(I32)
        merge_f = prod[:, 0:4 * MS + LG]
        assert 4 * MS + LG <= 512
        mtile_i, mblk_i = merge_i[:, 0:MS], merge_i[:, MS:2 * MS]
        mlast_i = merge_i[:, 2 * MS:2 * MS + LG - 1]
        mstep_f, mtile_f, mblk_f = (merge_f[0:1, j * MS:(j + 1) * MS] for j in range(3))
        mbase = merge_f[:, 3 * MS:4 * MS]
        mstart_f = merge_f[0:1, 4 * MS:4 * MS + LG - 1]
        mcount = arena[0:1, A3:A3 + MS * (LG - 1)]
        assert A3 + max(ENTRIES, MS * (LG - 1)) <= AR and ENTRIES + 1 <= 2 * STEPS * P and 2 * ENTRIES <= Qf.shape[1]

        EW = EC * P
        types2_i = Qf[0:TYPES, 0:NPAD].bitcast(I32)
        onehot3b = Qf[0:TYPES, 0:NPAD]
        hmT = Qf[:, NPAD:NPAD + 3 * EW]
        hm = hot[:, 0:3 * EW]
        shift = hot[:, 3 * EW:4 * EW]
        hbuf, res = rows[:, 0:EW], rows[:, EW:2 * EW]
        fin = arena[:, A3:A3 + EC * SUMW]
        kept, aggr = (arena[:, A3 + EC * SUMW + j * EW:A3 + EC * SUMW + (j + 1) * EW] for j in range(2))
        types_n = arena[0:TYPES, A3 + EC * SUMW + 2 * EW:A3 + EC * SUMW + 3 * EW]
        keep = ntype_f
        NR = NB // EC
        assert A3 + EC * SUMW + 3 * EW <= AR
        aggT = acc_s[:, 0:NPAD]
        y1 = Qf[:, 0:NPAD]
        y2 = arena[:, SLOTS * STEPS * P:SLOTS * STEPS * P + NPAD]
        CH = [(c, min(c + 512, NPAD)) for c in range(0, NPAD, 512)]
        assert NPAD + 3 * EW <= Qf.shape[1] and SLOTS * STEPS * P + NPAD <= AR

        def blocks(a, i, w=P):
            return a.rearrange("p (b c) -> p b c", c=w)[:, bass.ds(i * EC, EC), :]

        def by_block(a, w=P):
            return a.rearrange("p (b c) -> p b c", c=w)

        def spread(a, n):
            return a.unsqueeze(2).to_broadcast([a.shape[0], a.shape[1], n])

        def load_regs(engine, row, top):
            return nc.values_load_multi_w_load_instructions(
                row, engines=(engine,), min_val=0, max_val=top,
                skip_runtime_bounds_check_because="the schedule is clamped")[1]

        ctx.enter_context(nc.allow_non_contiguous_dma(reason="a few columns of the inputs, once"))
        block = ctx.enter_context(nc.Block())

        @block.sync
        def _(sp):
            for name, a, p in (("dst", dst, dst_p), ("src", src, src_p), ("typ", edge_type, typ_p)):
                flat = p.rearrange("t e -> (t e)")
                sp.dma_start(flat[0:E].rearrange("(a b) -> a b", a=FULLE),
                             a.rearrange("(a b) -> a b", a=FULLE)).then_inc(sem("edges_copied"), 16)
            sp.wait_ge(sem("tails_set"), 2)
            for p, t in ((dst_p, tail_d), (src_p, tail_z), (typ_p, tail_z)):
                flat = p.rearrange("t e -> (t e)")
                sp.dma_start(flat[E:NT * P].unsqueeze(0), t[:, 0:TAIL]).then_inc(sem("edges_copied"), 16)
            sp.dma_start(blk_d[ROUNDS:ROUNDS + 1], tail_z[:, 0:STEPS]).then_inc(sem("edges_copied"), 16)
            sp.wait_ge(sem("edges_copied"), 112)
            flat = dst_p.rearrange("t e -> (t e)")
            sp.dma_start(order_a, flat.rearrange("(p j) -> p j", p=P)).then_inc(sem("order_loaded"), 16)
            sp.dma_start(order_b[0:P - 1, :], flat[1:1 + (P - 1) * NT].rearrange("(p j) -> p j", j=NT)).then_inc(sem("order_loaded"), 16)
            sp.dma_start(order_b[P - 1:P, 0:NT - 1], flat[1 + (P - 1) * NT:NT * P].unsqueeze(0)).then_inc(sem("order_loaded"), 16)
            sp.wait_ge(sem("order_checked"), 1)
            unsorted = sp.value_load(unsorted_i[:, :])
            with sp.If(unsorted > 0):
                with sp.Fori(0, NT) as t:
                    sp.wait_ge(sem("tile_counted"), t + 1)
                    sp.dma_start(edge3[:, 0:1], dst_p[bass.ds(t, 1), :].rearrange("o e -> e o")).then_inc(sem("count_loaded"), 16)
                with sp.Fori(0, NT) as t:
                    sp.wait_ge(sem("tile_free"), t + 1)
                    sp.wait_ge(sem("tile_ranked"), t + 1)
                    for j, a in enumerate((dst_p, src_p, typ_p)):
                        sp.dma_start(edge3[:, j:j + 1], a[bass.ds(t, 1), :].rearrange("o e -> e o")).then_inc(sem("place_loaded"), 16)
                    sp.dma_start(row_i, dst_p[bass.ds(t, 1), :].to_broadcast([P, P])).then_inc(sem("place_loaded"), 16)
                sp.wait_ge(sem("tile_free"), NT + 1)
                for j, a in enumerate((dst_p, src_p, typ_p)):
                    sp.dma_start(a, sorted_d[:, j:j + 1].rearrange("(t e) o -> t (e o)", e=P)).then_inc(sem("sorted_back"), 16)
                sp.wait_ge(sem("sorted_back"), 48)
            sp.dma_start(last_i, dst_p[:, P - 1:P].rearrange("t o -> o t")).then_inc(sem("last_loaded"), 16)
            sp.dma_start(types_i[:, 0:N], node_type.partition_broadcast(TYPES)).then_inc(sem("consts_loaded"), 16)

            def store_table(b, u):
                sp.wait_ge(sem("tabk_copied"), b + 1)
                sp.sem_inc(sem("taken"), 1)
                sp.wait_ge(sem("tabv_copied"), b + 3)
                sp.sem_inc(sem("taken"), 1)
                sp.dma_start(kvtab.rearrange("(n r) f -> n (r f)", r=RELS)[bass.ds(b * P, P), :],
                             tab_s[u]).then_inc(sem(f"tab_stored{u}"), 16)

            def free_table(u, count):
                sp.wait_ge(sem(f"tab_stored{u}"), 16 * count)
                sp.sem_inc(sem("tab_free"), 1)

            sp.sem_inc(sem("tab_free"), 2)
            store_table(0, 0)
            with sp.Fori(0, NK // 2) as i:
                for u in range(2):
                    store_table(2 * i + u + 1, 1 - u)
                    free_table(u, i + 1)
            free_table(0, NK // 2 + 1)

            sp.wait_ge(sem("blk_made"), 1)
            sp.dma_start(blk_d[0:ROUNDS].rearrange("(g k) s -> g (k s)", g=SG), blkT[:, :]).then_inc(sem("blk_stored"), 16)
            sp.wait_ge(sem("blk_stored"), 16)
            sp.wait_ge(sem("arrays_made"), 1)
            sp.dma_start(reset_d.rearrange("(g s) e -> s g e", s=P),
                         W(4).rearrange("s (g e) -> s g e", g=SG)).then_inc(sem("rec_stored"), 16)
            sp.sem_inc(sem("recs_free"), RECS)

            def free_records(g):
                sp.wait_ge(sem(f"rec_stored{g % RECS}"), 16 * (g // RECS + 1))
                sp.sem_inc(sem("recs_free"), 1)

            for g in range(SG):
                sp.wait_ge(sem("reca_copied"), g + 1)
                sp.wait_ge(sem("recb_copied"), g + 1)
                sp.dma_start(rec_d[g * 8:(g + 1) * 8].rearrange("k e c -> e k c"),
                             rec_s[g % RECS].rearrange("e (k c) -> e k c", c=REC)).then_inc(sem(f"rec_stored{g % RECS}"), 16)
                if g >= 2:
                    free_records(g - 2)
            for g in range(max(SG - 2, 0), SG):
                free_records(g)
            sp.wait_ge(sem("pad_set"), 1)
            sp.dma_start(rec_d[ROUNDS], pad_s).then_inc(sem("rec_stored"), 16)
            sp.wait_ge(sem("rec_stored"), 32)

            def load_blks(k, u, loaded):
                sp.dma_start(blk_slot[u], blk_d[bass.ds(k, 1), :]).then_inc(sem(f"{loaded}{u}"), 16)

            def load_round(k, u):
                load_blks(k, u, "blk_loaded")
                sp.dma_start(rec_slot[u], rec_d[bass.ds(k, 1)].rearrange("o e c -> (o e) c")).then_inc(sem(f"rec_loaded{u}"), 16)
                sp.dma_start(reset_slot[u][:, 0:P], reset_d[bass.ds(k * STEPS, STEPS), :].unsqueeze(1)
                             .to_broadcast([STEPS, HEADS, P])).then_inc(sem(f"reset_loaded{u}"), 16)

            def store_list(k, u):
                sp.wait_ge(sem("list_copied"), k + 1)
                sp.dma_start(list_d[bass.ds(k * 2 * STEPS, 2 * STEPS), :],
                             listed[0:2 * STEPS, u * ROWW:(u + 1) * ROWW]).then_inc(sem("list_stored"), 16)
                sp.wait_ge(sem("list_stored"), 16 * (k + 1))

            sp.wait_ge(sem("zeroed"), 3)
            for u in range(SLOTS):
                load_round(u, u)
            store_list(0, 0)
            with sp.Fori(0, ROUNDS // SLOTS - 1) as i:
                for u in range(SLOTS):
                    k = SLOTS * i + u
                    sp.wait_ge(sem("acc_done"), RING + STEPS * (k + 2))
                    store_list(k + 1, (u + 1) % SLOTS)
                    load_round(k + SLOTS, u)
            store_list(ROUNDS - SLOTS + 1, 1)
            sp.wait_ge(sem("acc_done"), RING + STEPS * (ROUNDS - SLOTS + 2))
            load_blks(ROUNDS, 0, "blk_loaded")
            sp.dma_start(rec_slot[0], rec_d[ROUNDS]).then_inc(sem("rec_loaded0"), 16)
            for u in range(2, SLOTS + 1):
                store_list(ROUNDS - SLOTS + u, u % SLOTS)
            sp.dma_start(plist.rearrange("p (g c) -> p g c", g=LG),
                         list_d[2 * STEPS:].rearrange("(g p) c -> p g c", p=P)).then_inc(sem("list_loaded"), 16)
            sp.wait_ge(sem("keys_merged"), 1)
            sp.dma_start(types2_i[:, 0:N], node_type.partition_broadcast(TYPES)).then_inc(sem("types_loaded"), 16)

            with sp.Fori(0, NB // EC) as i:
                sp.wait_ge(sem("x1_made"), i + 1)
                sp.dma_start(x1_d.rearrange("(b p) f -> p b f", p=P)[:, bass.ds(i * EC, EC), :],
                             X.rearrange("p (b f) -> p b f", f=P)[:, bass.ds(i * EC, EC), :]).then_inc(sem("x1_stored"), 16)
            sp.wait_ge(sem("x1_stored"), 16 * (NB // EC))
            sp.sem_inc(sem("x1_ready"), 1)

            def load_round2(k, u):
                load_blks(k, u, "blk2_loaded")
                sp.dma_start(rec_slot[u], rec_d[bass.ds(k, 1)].rearrange("o e c -> (o e) c")).then_inc(sem(f"rec2_loaded{u}"), 16)

            for u in range(SLOTS):
                load_round2(u, u)
            with sp.Fori(0, ROUNDS // SLOTS - 1) as i:
                for u in range(SLOTS):
                    k = SLOTS * i + u
                    sp.wait_ge(sem("agg_done"), STEPS * (k + 2))
                    load_round2(k + SLOTS, u)
            sp.wait_ge(sem("agg_done"), STEPS * (ROUNDS - SLOTS + 2))
            sp.dma_start(rec_slot[0], rec_d[ROUNDS]).then_inc(sem("rec2_loaded0"), 16)

            def store_out(lo, n, cnt):
                sp.dma_start(out[lo * P:(lo + n) * P, :].rearrange("(b p) f -> p b f", p=P),
                             X.rearrange("p (b f) -> p b f", f=P)[:, lo:lo + n, :]).then_inc(sem("out_stored"), 16)

            for c in range(NB // EC):
                sp.wait_ge(sem("out_made"), c + 1)
                store_out(c * EC, EC if c < NB // EC - 1 else EC - 1, c)
            sp.dma_start(out[NK * P:N, :], X[0:LASTN, NK * P:NB * P]).then_inc(sem("out_stored"), 16)
            sp.wait_ge(sem("out_stored"), 16 * (NB // EC + 1))

        @block.gpsimd
        def _(pool):
            made = sem("patterns_made")
            pool.iota(iota_i, [[1, P]], base=0, channel_multiplier=0).then_inc(made, 1)
            pool.iota(misc_i[:, 0:SG], [[P, SG]], base=0, channel_multiplier=1).then_inc(made, 1)
            pool.iota(misc_i[:, SG:SG + 1], [[0, 1]], base=0, channel_multiplier=1).then_inc(made, 1)

            pool.wait_ge(sem("order_checked"), 1)
            unsorted = pool.value_load(unsorted_i[:, :])
            with pool.If(unsorted > 0):
                pool.sem_inc(sem("tile_free"), 1)
                with pool.Fori(0, NT) as t:
                    pool.wait_ge(sem("tile_ranked"), t + 2)
                    pool.sem_inc(sem("taken"), 1)
                    pool.indirect_dma_start(sorted_d, bass.IndirectOffsetOnAxis(ap=place_i, axis=0), edge3,
                                            None).then_inc(sem("tile_placed"), 16)
                    pool.wait_ge(sem("tile_placed"), 16 * (t + 1))
                    pool.sem_inc(sem("tile_free"), 1)

            def gather(to, table, idx):
                return pool.indirect_dma_start(to, None, table, bass.IndirectOffsetOnAxis(ap=idx, axis=0))

            pool.wait_ge(sem("tiles_made"), 1)
            for g in range(SG):
                for w, table in ((2, dst_p), (3, src_p), (4, typ_p)):
                    gather(W(w)[:, g * P:(g + 1) * P].bitcast(I32), table,
                           tile_i[:, g:g + 1]).then_inc(sem("rows_gathered"), 16)

            pool.wait_ge(sem("tab_free"), NB + 2)

            def gather_kv(u):
                for t in range(STEPS):
                    gather(kv_slot[u][:, t * 2 * P:(t + 1) * 2 * P], kvtab,
                           rec_col(u, C_KVROW).bitcast(I32)[:, t:t + 1]).then_inc(sem(f"kv_loaded{u}"), 16)

            for u in range(SLOTS):
                pool.wait_ge(sem(f"rec_loaded{u}"), 16)
                gather_kv(u)
            with pool.Fori(1, ROUNDS // SLOTS) as i:
                for u in range(SLOTS):
                    pool.wait_ge(sem("msg_ready"), 4 * (SLOTS * (i - 1) + u + 1) + 1)
                    pool.wait_ge(sem(f"rec_loaded{u}"), 16 * (i + 1))
                    pool.sem_inc(sem("taken"), 1)
                    gather_kv(u)

            pool.wait_ge(sem("msg_ready"), 4 * ROUNDS + 1)
            pool.iota(mtile_i, [[1, MS]], base=0, channel_multiplier=0).then_inc(made, 1)
            pool.iota(mlast_i, [[1, LG - 1]], base=1, channel_multiplier=0).then_inc(made, 1)

            g_, link = nc.gpsimd, Chain(pool, sem("pool_chain"))
            then = link.then
            f3, k3, h3 = by_block(fin, SUMW), by_block(kept), by_block(hbuf)
            with pool.Fori(0, NR) as i:
                link.enter(i, 5)
                pool.wait_ge(sem("fin_used"), i + 1)
                then(g_.tensor_tensor(f3, blocks(acc, i, SUMW), spread(keep[:, bass.ds(i * EC, EC)], SUMW), ALU.mult))
                g_.tensor_tensor(f3, f3, blocks(acc2, i, AW)[:, :, 0:SUMW], ALU.add).then_inc(sem("fin_made"), 1)
                pool.wait_ge(sem("kept_used"), i + 1)
                then(g_.tensor_tensor(k3, blocks(X, i), spread(ungate[:, bass.ds(i * EC, EC)], P), ALU.mult))
                pool.sem_inc(sem("kept_made"), 1)
                pool.wait_ge(sem("gelu_done"), i + 1)
                for t in range(TYPES):
                    then(g_.tensor_tensor(by_block(hm[:, t * EW:(t + 1) * EW]), h3,
                                          spread(tmask[:, bass.ds(i * EC + t * NB, EC)], P), ALU.mult))
                pool.sem_inc(sem("hm_made"), 1)
            link.leave(NR)

            pool.wait_ge(sem("x1_ready"), 1)

            def gather_x(u):
                for t in range(STEPS):
                    gather(xg_slot[u][:, t * P:(t + 1) * P], x1_d,
                           rec_col(u, C_SRC).bitcast(I32)[:, t:t + 1]).then_inc(sem(f"xg_loaded{u}"), 16)

            for u in range(SLOTS):
                pool.wait_ge(sem(f"rec2_loaded{u}"), 16)
                gather_x(u)
            with pool.Fori(1, ROUNDS // SLOTS) as i:
                for u in range(SLOTS):
                    pool.wait_ge(sem(f"rec2_loaded{u}"), 16 * (i + 1))
                    pool.sem_inc(sem("taken"), 1)
                    gather_x(u)

        @block.scalar
        def _(act):

            def copy(to, of, **kw):
                return act.activation(to, of, ACT.Copy, **kw)

            cst = sem("consts_loaded")
            for s_, w in ((Wk_s, Wk), (Wq_s, Wq), (Wv_s, Wv), (Wa_s, Wa)):
                act.dma_start(s_.rearrange("i (t o) -> i t o", t=TYPES), w.rearrange("t i o -> i t o")).then_inc(cst, 16)
            for j, b in enumerate((bk, bv, bq, ba, ln_g, ln_b)):
                act.dma_start(bias3[:, j * P:(j + 1) * P], b).then_inc(cst, 16)
            act.dma_start(W12[:, 0:P], W1).then_inc(cst, 16)
            act.dma_start(W12[:, P:2 * P], W2).then_inc(cst, 16)
            for j, b in enumerate((b1, g1, be1, b2, g2, be2)):
                act.dma_start(cols[:, j:j + 1], b.unsqueeze(1)).then_inc(cst, 16)
            act.dma_start(cols[:, 6:7], eps.partition_broadcast(P)).then_inc(cst, 16)
            act.dma_start(skip_s, skip.partition_broadcast(P)).then_inc(cst, 16)
            act.wait_ge(sem("zeroed"), 1)
            for h in range(HEADS):
                for s_, r in ((relk, rel_att), (relv, rel_msg)):
                    act.dma_start(s_.rearrange("p (r f) -> p r f", r=RELS)[h * DK:(h + 1) * DK, :, h * DK:(h + 1) * DK],
                                 r[:, h].rearrange("r d f -> d r f")).then_inc(cst, 16)
                act.dma_start(pri[h * DK:(h + 1) * DK, :], rel_pri[:, h].partition_broadcast(DK)).then_inc(cst, 16)
            act.wait_ge(sem("zeroed"), 2)
            act.dma_start(X[:, 0:NK * P].rearrange("p (b f) -> p b f", f=P),
                         x[0:NK * P, :].rearrange("(b p) f -> p b f", p=P)).then_inc(cst, 16)
            act.dma_start(X[0:LASTN, NK * P:NB * P], x[NK * P:N, :]).then_inc(cst, 16)
            act.dma_start(ntype_i[:, 0:NK], node_type[0:NK * P].rearrange("(b p) -> p b", p=P)).then_inc(cst, 16)
            act.dma_start(ntype_i[0:LASTN, NK:NB], node_type[NK * P:N].unsqueeze(1)).then_inc(cst, 16)
            act.wait_ge(sem("consts_loaded"), 16 * NCONST)
            act.activation(skip_s, skip_s, ACT.Sigmoid).then_inc(sem("skip_gated"), 1)

            def copy_xmT(b, u):
                act.wait_ge(sem("xm_turned"), b + 1)
                copy(xmT[u], bank[u][:, 0:384]).then_inc(sem("xmT_copied"), 1)

            def copy_kvT(b, u):
                act.wait_ge(sem("qkv_made"), b + 1)
                copy(kvT[u], bank[2 + u][:, 0:256]).then_inc(sem("kvT_copied"), 1)

            def copy_tabk(b, u):
                act.wait_ge(sem("tab_made"), b + 1)
                act.wait_ge(sem("tab_free"), b + 1)
                copy(tab_s[u].rearrange("p (r c) -> p r c", r=RELS)[:, :, 0:P],
                     bank[4 + u].rearrange("p (r c) -> p r c", r=RELS)).then_inc(sem("tabk_copied"), 1)

            copy_xmT(0, 0)
            copy_xmT(1, 1)
            copy_kvT(0, 0)
            with act.Fori(0, NK // 2 - 1) as i:
                for u in range(2):
                    b = 2 * i + u
                    copy_kvT(b + 1, 1 - u)
                    copy_xmT(b + 2, u)
                    copy_tabk(b, u)
            copy_kvT(NK - 1, 1)
            copy_xmT(NK, 0)
            copy_tabk(NK - 2, 0)
            copy_kvT(NK, 0)
            copy_tabk(NK - 1, 1)
            copy_tabk(NK, 0)

            for g in range(SG):
                act.wait_ge(sem("reca_turned"), g + 1)
                act.wait_ge(sem("recs_free"), g + 1)
                copy(rec_s[g % RECS].rearrange("e (k c s) -> e c k s", c=7, s=STEPS)[:, C_KEY:C_HEAD + 1],
                     bank[g % 2 * 2].rearrange("e (c k s) -> e c k s", c=4, s=STEPS)).then_inc(sem("reca_copied"), 1)

            def copy_hotT(k, half):
                act.wait_ge(sem("hot_turned"), 2 * k + half + 1)
                copy(hotT[:, half * 1024:(half + 1) * 1024], bank[3].bitcast(BF16)).then_inc(sem("hotT_copied"), 1)

            def copy_list(k, u):
                act.wait_ge(sem("ends_summed"), k + 1)
                copy(listed[0:2 * STEPS, u * ROWW:(u + 1) * ROWW],
                     bank[7][0:2 * STEPS, u % 2 * 256:u % 2 * 256 + ROWW]).then_inc(sem("list_copied"), 1)

            act.activation(stat[:, 0:1], ident[:, 0:1], ACT.Exp)
            copy_hotT(0, 0)
            copy_hotT(0, 1)
            with act.Fori(0, ROUNDS // SLOTS) as i:
                for u in range(SLOTS):
                    k = SLOTS * i + u
                    act.wait_ge(sem("shift_turned"), k + 1)
                    act.activation(weight, bank[2][:, P:2 * P], ACT.Exp).then_inc(sem("exp_done"), 1)
                    copy_hotT(k + 1, 0)
                    copy_list(k, u)
                    copy_hotT(k + 1, 1)
            copy_list(ROUNDS, 0)

            for w, to in ((0, mT), (1, keyT)):
                for c in range(-(-LG // 4)):
                    n = min(LG - 4 * c, 4) * P
                    act.wait_ge(sem("list_turned"), w * (-(-LG // 4)) + c + 1)
                    copy(to[:, c * 512:c * 512 + n], bank[c][0:HEADS, 0:n]).then_inc(sem("list_taken"), 1)
            act.wait_ge(sem("mshift_made"), 1)
            act.activation(mT, mT, ACT.Exp).then_inc(sem("mexp_done"), 1)

            roots = stat[:, 6 * EC + 1:8 * EC:2]

            def gelu(i):
                act.wait_ge(sem("aggr_made"), i + 1)
                act.activation(hbuf, aggr, ACT.Gelu).then_inc(sem("gelu_done"), 1)

            def copy_hmT(i):
                for j in range(EC):
                    act.wait_ge(sem("hm_turned"), EC * i + j + 1)
                    copy(hmT[:, j * 384:(j + 1) * 384], bank[6 + j % 2][:, 0:384]).then_inc(sem("hmT_copied"), 1)

            def root(n):
                act.wait_ge(sem("var_made"), n)
                act.activation(roots, roots, ACT.Sqrt).then_inc(sem("root_made"), 1)

            gelu(0)
            copy_hmT(0)
            if NR > 1:
                with act.Fori(0, NR - 1) as i:
                    gelu(i + 1)
                    root(2 * i + 1)
                    copy_hmT(i + 1)
                    root(2 * i + 2)
            root(2 * NR - 1)
            root(2 * NR)

            for c, (lo, hi) in enumerate(CH):
                act.wait_ge(sem("x1_turned"), c + 1)
                copy(aggT[:, lo:hi], bank[c % 8][:, 0:hi - lo], scale=cols[:, 7:8]).then_inc(sem("agg_begun"), 1)

            for m, y in ((0, y1), (1, y2)):
                for c, (lo, hi) in enumerate(CH):
                    act.wait_ge(sem("lin_made"), m * len(CH) + c + 1)
                    act.activation(y[:, lo:hi], bank[c % 8][:, 0:hi - lo], ACT.Identity,
                                   bias=cols[:, 3 * m:3 * m + 1]).then_inc(sem("lin_copied"), 1)
                act.wait_ge(sem("var_made"), 2 * NR + m + 1)
                act.activation(stat[:, 0:1], stat[:, 1:2], ACT.Sqrt).then_inc(sem("root_made"), 1)
                act.wait_ge(sem("bscale_made"), m + 1)
                for lo, hi in CH:
                    act.activation(y[:, lo:hi], y[:, lo:hi], ACT.Relu, bias=stat[:, 3:4],
                                   scale=stat[:, 2:3]).then_inc(sem("relu_done"), 1)
            for c in range(NR):
                act.wait_ge(sem("var_made"), 2 * NR + 2 + c + 1)
                act.activation(roots, roots, ACT.Sqrt).then_inc(sem("root_made"), 1)

        @block.tensor
        def _(pe):
            mm, turn = nc.tensor.matmul, nc.tensor.transpose
            PE_ = mybir.EngineType.PE

            pe.wait_ge(sem("descents_counted"), 1)
            mm(bank[0][0:1, 0:1], before_f[:, 0:1], ones_f[:, 0:1], start=True, stop=True).then_inc(sem("descents_summed"), 1)
            pe.wait_ge(sem("order_checked"), 1)
            unsorted = pe.value_load(unsorted_i[:, :])
            with pe.If(unsorted > 0):
                with pe.Fori(0, NT) as t:
                    pe.wait_ge(sem("digits_hot"), t + 1)
                    mm(bank[0][:, 0:NB], one_lo, one_hi, start=True, stop=True).then_inc(sem("count_made"), 1)
                pe.wait_ge(sem("counts_made"), 1)
                mm(bank[0][:, 0:NB], earlier, counts, start=True, stop=True)
                mm(bank[0][:, 128:128 + NB], ones_f, counts, start=True, stop=True).then_inc(sem("prefix_made"), 1)
                with pe.Fori(0, NT) as t:
                    pe.wait_ge(sem("digits2_hot"), t + 1)
                    turn(bank[1][:, 0:P], one_lo, ident).then_inc(sem("lo_turned"), 1)
                    pe.wait_ge(sem("loT_copied"), t + 1)
                    mm(bank[0][:, 0:NB], one_loT, nextp, start=True, stop=True)
                    mm(bank[0][:, 128:128 + NB], one_lo, one_hi, start=True, stop=True).then_inc(sem("base_made"), 1)

            pe.wait_ge(sem("last_made"), 1)
            for c in range(-(-NT // 512)):
                n = min(NT - c * 512, 512)
                mm(bank[c][0:NB, 0:n], ones1[:, 0:NB], last_row[:, c * 512:c * 512 + n],
                   start=True, stop=True).then_inc(sem("last_spread"), 1)
            pe.wait_ge(sem("starts_made"), 1)
            mm(bank[4][:, 0:NB], ones_f[0:NB, :], diag, start=True, stop=True).then_inc(sem("starts_spread"), 1)

            def turn_xm(b, u):
                pe.wait_ge(sem("xm_made"), b + 1)
                for t in range(TYPES):
                    last = turn(bank[u][:, t * P:(t + 1) * P], xm[u][:, t * P:(t + 1) * P], ident)
                last.then_inc(sem("xm_turned"), 1)

            def make_qkv(b, u):
                pe.wait_ge(sem("q_split"), b + 1)
                pe.wait_ge(sem("xmT_copied"), b + 1)
                hot3 = types_s[:, u * P:(u + 1) * P]
                for j, w in enumerate((Wk_s, Wv_s)):
                    o = bank[2 + u][:, j * P:(j + 1) * P]
                    for t in range(TYPES):
                        mm(o, w[:, t * P:(t + 1) * P], xmT[u][:, t * P:(t + 1) * P], start=(t == 0), stop=False)
                    mm(o, bias3[:, j * P:(j + 1) * P], hot3, start=False, stop=True)
                o = bank[2 + u][:, 2 * P:3 * P]
                for t in range(TYPES):
                    mm(o, xmT[u][:, t * P:(t + 1) * P], Wq_s[:, t * P:(t + 1) * P], start=(t == 0), stop=False)
                mm(o, hot3, bias3[:, 2 * P:3 * P], start=False, stop=True).then_inc(sem("qkv_made"), 1)

            def make_tab(b, u):
                pe.wait_ge(sem("tabv_copied"), b + 1)
                pe.wait_ge(sem("kvT_copied"), b + 1)
                mm(bank[4 + u], kvT[u][:, 0:P], relk, start=True, stop=True)
                mm(bank[6 + u], kvT[u][:, P:2 * P], relv, start=True, stop=True).then_inc(sem("tab_made"), 1)

            pe.wait_ge(sem("consts_loaded"), 16 * NCONST)
            pe.wait_ge(sem("masks_made"), 1)
            turn_xm(0, 0)
            turn_xm(1, 1)
            make_qkv(0, 0)
            with pe.Fori(0, NK // 2 - 1) as i:
                for u in range(2):
                    b = 2 * i + u
                    make_qkv(b + 1, 1 - u)
                    turn_xm(b + 2, u)
                    make_tab(b, u)
            make_qkv(NK - 1, 1)
            turn_xm(NK, 0)
            make_tab(NK - 2, 0)
            make_qkv(NK, 0)
            make_tab(NK - 1, 1)
            make_tab(NK, 0)

            pe.wait_ge(sem("arrays_made"), 1)
            pe.wait_ge(sem("tabk_copied"), NB)
            turn(bank[4][0:SG, 0:P], small[:, SG:2 * SG], ident).then_inc(sem("blk_turned"), 1)
            for g in range(SG):
                if g >= 2:
                    pe.wait_ge(sem("reca_copied"), g - 1)
                    pe.wait_ge(sem("recb_copied"), g - 1)
                for j, w in enumerate((7, 1, 2, 9)):
                    last = turn(bank[g % 2 * 2][:, j * P:(j + 1) * P], W(w)[:, g * P:(g + 1) * P], ident)
                last.then_inc(sem("reca_turned"), 1)
                for j, w in enumerate((3, 8, 6)):
                    last = turn(bank[g % 2 * 2 + 1][:, j * P:(j + 1) * P], W(w)[:, g * P:(g + 1) * P], ident)
                last.then_inc(sem("recb_turned"), 1)

            def turn_hot(k, par, half):
                pe.wait_ge(sem("hot_made"), 4 * k + 2 * half + 2)
                if half:
                    pe.wait_ge(sem("hotT_copied"), 2 * k + 1)
                for t in range(8):
                    last = turn(bank[3].bitcast(BF16)[:, t * P:(t + 1) * P],
                                hot_step_bf16(par, 8 * half + t), identb)
                last.then_inc(sem("hot_turned"), 1)

            def spread_q(k, q, regs):
                if q % 2 == 0:
                    pe.wait_ge(sem("hotT_copied"), 2 * k + q // 2 + 1)
                for j in range(4):
                    t = 4 * q + j
                    for part in range(3):
                        last = mm(bank[Q_BANK[q]][:, j * P:(j + 1) * P], hotT[:, t * P:(t + 1) * P],
                                  Qsplit[:, bass.ds(regs[t] * (3 * P) + part * P, P)],
                                  start=(part == 0), stop=(part == 2))
                last.then_inc(sem("q_spread"), 1)

            pe.wait_ge(sem("blk_loaded0"), 16)
            pe.wait_ge(sem("reca_copied"), SG)
            pe.wait_ge(sem("recb_copied"), SG)
            regs = load_regs(PE_, blk_slot[0][:, 0:12], NB - 1)
            for half in range(2):
                turn_hot(0, 0, half)
            for q in range(3):
                spread_q(0, q, regs)

            def sum_edges(k, u, ts):
                for t in ts:
                    if t % 2 == 0:
                        pe.wait_ge(sem("acc_done"), STEPS * k + t + 2)
                    mm(bank[5 + t % RING // 2][:, t % 2 * 256:t % 2 * 256 + SUMW], hot_step((u + 1) % 2, t),
                       rows3[:, t, 0:SUMW], start=True, stop=True).then_inc(sem("sum_made"), 1)
                    last = mm(bank[7][0:2 * STEPS, u % 2 * 256:u % 2 * 256 + ROWW],
                              ends[:, t * 2 * STEPS:(t + 1) * 2 * STEPS], rows3[:, t, :],
                              start=(t == 0), stop=(t == STEPS - 1))
                    if t == STEPS - 1:
                        last.then_inc(sem("ends_summed"), 1)

            with pe.Fori(0, ROUNDS // SLOTS) as i:
                for u in range(SLOTS):
                    k = SLOTS * i + u
                    pe.wait_ge(sem("msg_ready"), 4 * k + 1)
                    sum_edges(k, u, range(0, 2))
                    regs = [None] * 12 + list(load_regs(PE_, blk_slot[u][:, 12:16], NB - 1))
                    pe.wait_ge(sem("q_used"), 4 * k + 1)
                    spread_q(k, 3, regs)
                    sum_edges(k, u, range(2, 6))
                    pe.wait_ge(sem("att_made"), 4 * (k + 1))
                    turn(bank[2][:, 0:P], att, ident).then_inc(sem("att_turned"), 1)
                    sum_edges(k, u, range(6, 12))
                    pe.wait_ge(sem("shift_made"), k + 1)
                    turn(bank[2][:, P:2 * P], shifted, ident)
                    turn(bank[2][:, 2 * P:3 * P], seg, ident).then_inc(sem("shift_turned"), 1)
                    sum_edges(k, u, range(12, 14))
                    turn_hot(k + 1, (u + 1) % 2, 0)
                    sum_edges(k, u, range(14, 16))
                    pe.wait_ge(sem(f"blk_loaded{(u + 1) % SLOTS}"), 16 * (i + 1 + (u + 1) // SLOTS))
                    turn_hot(k + 1, (u + 1) % 2, 1)
                    regs = load_regs(PE_, blk_slot[(u + 1) % SLOTS][:, 0:12], NB - 1)
                    for q, used in ((0, 4), (1, 2), (2, 3)):
                        pe.wait_ge(sem("q_used"), 4 * k + used)
                        spread_q(k + 1, q, regs)
            pe.wait_ge(sem("msg_ready"), 4 * ROUNDS + 1)
            pe.wait_ge(sem("list_copied"), ROUNDS)
            sum_edges(ROUNDS, 0, range(STEPS))

            pe.wait_ge(sem("keys_made"), 1)
            pe.wait_ge(sem("list_copied"), ROUNDS + 1)
            nc4 = -(-LG // 4)
            for w, of in ((0, mval), (1, key8)):
                for c in range(nc4):
                    if w:
                        pe.wait_ge(sem("list_taken"), c + 1)
                    for g in range(4 * c, min(4 * c + 4, LG)):
                        last = turn(bank[c][0:HEADS, g % 4 * P:(g % 4 + 1) * P], of[:, g * HEADS:(g + 1) * HEADS], ident)
                    last.then_inc(sem("list_turned"), 1)
            pe.wait_ge(sem("keys_made"), 2)
            pe.wait_ge(sem("list_taken"), 2 * nc4)
            for g in range(LG):
                last = turn(bank[1][:, g * HEADS:(g + 1) * HEADS], keyT[:, g * P:(g + 1) * P], ident[0:HEADS, 0:HEADS])
            last.then_inc(sem("keys_back"), 1)
            pe.wait_ge(sem("mexp_done"), 1)
            for g in range(LG):
                last = turn(bank[0][:, g * HEADS:(g + 1) * HEADS], mT[:, g * P:(g + 1) * P], ident[0:HEADS, 0:HEADS])
            last.then_inc(sem("factors_back"), 1)
            pe.wait_ge(sem("mblk_made"), 1)
            mm(bank[4][:, 0:MS], ones1, mblk_f, start=True, stop=True).then_inc(sem("mbase_spread"), 1)
            with pe.Fori(0, MR) as i:
                regs = load_regs(PE_, mtile_i[:, bass.ds(i * MERGES, MERGES)], LG - 1)
                for j in range(MERGES):
                    pe.wait_ge(sem("mhot_made"), MERGES * i + j + 1)
                    mm(bank[2 + j // 3][:, j % 3 * AW:(j % 3 + 1) * AW], hot[:, j * P:(j + 1) * P],
                       plist[:, bass.ds(regs[j] * ROWW, AW)], start=True, stop=True).then_inc(sem("msum_made"), 1)

            with pe.Fori(0, NR) as i:
                pe.wait_ge(sem("hm_made"), i + 1)
                pe.wait_ge(sem("types_made"), i + 1)
                pe.wait_ge(sem("trans_used"), i + 1)
                for j in range(EC + 1):
                    if j < EC:
                        if j >= 2:
                            pe.wait_ge(sem("hmT_copied"), EC * i + j - 1)
                        for t in range(TYPES):
                            last = turn(bank[6 + j % 2][:, t * P:(t + 1) * P],
                                        hm[:, (t * EC + j) * P:(t * EC + j + 1) * P], ident)
                        last.then_inc(sem("hm_turned"), 1)
                    if j > 0:
                        pe.wait_ge(sem("hmT_copied"), EC * i + j)
                        o = bank[(j - 1) // 4][:, (j - 1) % 4 * P:((j - 1) % 4 + 1) * P]
                        for t in range(TYPES):
                            mm(o, hmT[:, ((j - 1) * TYPES + t) * P:((j - 1) * TYPES + t + 1) * P],
                               Wa_s[:, t * P:(t + 1) * P], start=(t == 0), stop=False)
                        last = mm(o, types_s[:, (j - 1) * P:j * P], bias3[:, 3 * P:4 * P], start=False, stop=True)
                last.then_inc(sem("trans_made"), 1)
                pe.wait_ge(sem("gains_used"), i + 1)
                for j in range(EC):
                    last = mm(bank[2 + j // 2][:, j % 2 * 256:j % 2 * 256 + 256], types_n[:, j * P:(j + 1) * P],
                              bias3[:, 4 * P:6 * P], start=True, stop=True)
                last.then_inc(sem("gains_made"), 1)

            pe.wait_ge(sem("x1_made"), NR)
            for c, (lo, hi) in enumerate(CH):
                if c >= 8:
                    pe.wait_ge(sem("agg_begun"), c - 7)
                for b in range(lo // P, hi // P):
                    last = turn(bank[c % 8][:, b * P - lo:b * P - lo + P], X[:, b * P:(b + 1) * P], ident)
                last.then_inc(sem("x1_turned"), 1)

            pe.wait_ge(sem("agg_begun"), len(CH))
            with pe.Fori(0, ROUNDS // SLOTS) as i:
                for u in range(SLOTS):
                    k = SLOTS * i + u
                    pe.wait_ge(sem(f"xg_loaded{u}"), 16 * STEPS * (i + 1))
                    for t in range(STEPS):
                        if t % 4 == 0:
                            pe.wait_ge(sem("hot2_made"), 4 * k + t // 4 + 1)
                            pe.wait_ge(sem("agg_done"), STEPS * k + t + 4)
                        mm(bank[t // 4][:, t % 4 * P:(t % 4 + 1) * P], xg_slot[u][:, t * P:(t + 1) * P],
                           hot_step(u % 2, t), start=True, stop=True).then_inc(sem("agg_made"), 1)

            pe.wait_ge(sem("agg_done"), STEPS * (ROUNDS + 1))
            for m, of in ((0, aggT), (1, y1)):
                if m:
                    pe.wait_ge(sem("relu_done"), len(CH))
                for c, (lo, hi) in enumerate(CH):
                    if m * len(CH) + c >= 8:
                        pe.wait_ge(sem("lin_copied"), m * len(CH) + c - 7)
                    mm(bank[c % 8][:, 0:hi - lo], W12[:, m * P:(m + 1) * P], of[:, lo:hi],
                       start=True, stop=True).then_inc(sem("lin_made"), 1)
            pe.wait_ge(sem("relu_done"), 2 * len(CH))
            for c in range(NB // EC):
                if c >= 4:
                    pe.wait_ge(sem("h2_used"), c - 3)
                for j in range(EC):
                    last = turn(bank[c % 4 * 2 + j // 4][:, j % 4 * P:(j % 4 + 1) * P],
                                y2[:, (c * EC + j) * P:(c * EC + j + 1) * P], ident)
                last.then_inc(sem("h2_turned"), 1)

        @block.vector
        def _(dve):
            v = nc.vector
            link = Chain(dve, sem("dve_chain"))
            then = link.then
            DVE_ = mybir.EngineType.DVE

            v.memset(tail_d, PADNODE).then_inc(sem("tails_set"), 1)
            v.memset(tail_z, 0).then_inc(sem("tails_set"), 1)
            v.memset(relk, 0.0)
            v.memset(relv, 0.0).then_inc(sem("zeroed"), 1)
            v.memset(X[:, NK * P:NB * P], 0.0)
            v.memset(ntype_i, 0)
            v.memset(types_i, 0).then_inc(sem("zeroed"), 1)
            v.memset(resets, 0.0).then_inc(sem("zeroed"), 1)
            v.memset(ones1, 1.0)
            dve.wait_ge(sem("patterns_made"), 3)
            v.tensor_copy(iota_f, iota_i)
            v.tensor_copy(step_f, misc_i[:, 0:SG])
            v.tensor_copy(tcol, misc_i[0:TYPES, SG:SG + 1])
            then(v.tensor_copy(pcol, misc_i[:, SG:SG + 1]))
            v.tensor_scalar(identb, iota_f, pcol, None, ALU.is_equal)
            then(v.tensor_scalar(ident, iota_f, pcol, None, ALU.is_equal))

            v.memset(ones_f, 1.0)
            dve.wait_ge(sem("order_loaded"), 48)
            then(v.tensor_tensor(descents[:, 0:NT - 1], order_a[:, 0:NT - 1], order_b[:, 0:NT - 1], ALU.is_gt))
            then(v.memset(descents[:, NT - 1:NT], 0.0))
            then(v.tensor_tensor(descents[0:P - 1, NT - 1:NT], order_a[0:P - 1, NT - 1:NT], order_b[0:P - 1, NT - 1:NT],
                                 ALU.is_gt))
            v.tensor_reduce(before_f[:, 0:1], descents, AX.X, ALU.add).then_inc(sem("descents_counted"), 1)
            dve.wait_ge(sem("descents_summed"), 1)
            v.tensor_copy(unsorted_i, bank[0][0:1, 0:1]).then_inc(sem("order_checked"), 1)
            dve.wait_ge(sem("order_checked"), 1)
            unsorted = dve.value_load(unsorted_i[:, :])
            srt_link = Chain(dve, sem("sort_chain"))
            then_s = srt_link.then

            def digit_hots():
                then_s(v.tensor_scalar(digits_i[:, 0:1], edge3[:, 0:1], P - 1, None, ALU.bitwise_and))
                then_s(v.tensor_scalar(digits_i[:, 1:2], edge3[:, 0:1], 7, None, ALU.arith_shift_right))
                then_s(v.tensor_copy(digits_f, digits_i))
                then_s(v.tensor_scalar(one_lo, iota_f, digits_f[:, 0:1], None, ALU.is_equal))
                then_s(v.tensor_scalar(one_hi, iota_f[:, 0:NB], digits_f[:, 1:2], None, ALU.is_equal))

            with dve.If(unsorted > 0):
                then_s(v.memset(counts, 0.0))
                then_s(v.tensor_scalar(later, iota_f, pcol, None, ALU.is_lt))
                then_s(v.tensor_scalar(earlier, iota_f, pcol, None, ALU.is_gt))
                dve.sem_inc(sem("tile_counted"), 1)
                with dve.Fori(0, NT) as t:
                    srt_link.enter(t, 6)
                    dve.wait_ge(sem("count_loaded"), 16 * (t + 1))
                    digit_hots()
                    dve.sem_inc(sem("digits_hot"), 1)
                    dve.wait_ge(sem("count_made"), t + 1)
                    then_s(v.tensor_tensor(counts, counts, bank[0][:, 0:NB], ALU.add))
                    dve.sem_inc(sem("tile_counted"), 1)
                srt_link.leave(NT)
                dve.sem_inc(sem("counts_made"), 1)
                dve.wait_ge(sem("prefix_made"), 1)
                then_s(v.tensor_copy(counts, bank[0][:, 128:128 + NB]))
                then_s(v.memset(before_f, 0.0))
                then_s(v.tensor_tensor_scan(nextp, counts, before_f, 0.0, ALU.add, ALU.add))
                then_s(v.tensor_tensor(nextp, nextp, counts, ALU.subtract))
                then_s(v.tensor_tensor(nextp, nextp, bank[0][:, 0:NB], ALU.add))
                dve.sem_inc(sem("tile_ranked"), 1)
                with dve.Fori(0, NT) as t:
                    srt_link.enter(t, 16)
                    dve.wait_ge(sem("place_loaded"), 64 * (t + 1))
                    digit_hots()
                    dve.sem_inc(sem("digits2_hot"), 1)
                    then_s(v.tensor_copy(row_f, row_i))
                    then_s(v.tensor_copy(dst_f, edge3[:, 0:1]))
                    then_s(v.tensor_scalar(row_f, row_f, dst_f, None, ALU.is_equal))
                    then_s(v.tensor_tensor(row_f, row_f, later, ALU.mult))
                    then_s(v.tensor_reduce(rank, row_f, AX.X, ALU.add))
                    dve.wait_ge(sem("lo_turned"), t + 1)
                    then_s(v.tensor_copy(one_loT, bank[1][:, 0:P]))
                    dve.sem_inc(sem("loT_copied"), 1)
                    dve.wait_ge(sem("base_made"), t + 1)
                    then_s(v.tensor_tensor(before_f, bank[0][:, 0:NB], one_hi, ALU.mult))
                    then_s(v.tensor_reduce(base_f, before_f, AX.X, ALU.add))
                    then_s(v.tensor_tensor(base_f, base_f, rank, ALU.add))
                    then_s(v.tensor_copy(place_i, base_f))
                    then_s(v.tensor_tensor(nextp, nextp, bank[0][:, 128:128 + NB], ALU.add))
                    dve.sem_inc(sem("tile_ranked"), 1)
                srt_link.leave(NT)

            dve.wait_ge(sem("last_loaded"), 16)
            then(v.tensor_scalar(last_b, last_i, 7, None, ALU.arith_shift_right))
            v.tensor_copy(last_row, last_b).then_inc(sem("last_made"), 1)
            for c in range(-(-NT // 512)):
                n = min(NT - c * 512, 512)
                dve.wait_ge(sem("last_spread"), c + 1)
                last = v.tensor_scalar(below[:, c * 512:c * 512 + n], bank[c][0:NB, 0:n], pcol[0:NB], None, ALU.is_lt)
            then(last)
            then(v.tensor_reduce(small[0:NB, 0:1], below[:, 0:NT - 1], AX.X, ALU.add))
            then(v.tensor_scalar(small[0:NB, 0:1], small[0:NB, 0:1], pcol[0:NB], None, ALU.add))
            v.tensor_scalar(diag, ident[0:NB, 0:NB], small[0:NB, 0:1], None, ALU.mult).then_inc(sem("starts_made"), 1)
            dve.wait_ge(sem("starts_spread"), 1)
            passed3 = passed.rearrange("p (g b) -> p g b", b=NB - 1)
            then(v.tensor_tensor(passed3, bank[4][:, 1:NB].unsqueeze(1).to_broadcast([P, SG, NB - 1]),
                                 spread(step_f, NB - 1), ALU.is_le))
            then(v.tensor_reduce(small[:, SG:2 * SG], passed3, AX.X, ALU.add))
            then(v.tensor_tensor(small[:, 0:SG], step_f, small[:, SG:2 * SG], ALU.subtract))
            then(v.tensor_scalar(small[:, 0:SG], small[:, 0:SG], float(NT - 1), None, ALU.min))
            v.tensor_copy(tile_i, small[:, 0:SG]).then_inc(sem("tiles_made"), 1)
            then(v.tensor_tensor(small[:, SG:2 * SG], step_f, small[:, 0:SG], ALU.subtract))
            then(v.tensor_scalar(small[:, 2 * SG:3 * SG], small[:, SG:2 * SG], float(P), None, ALU.mult))

            dve.wait_ge(sem("consts_loaded"), 16 * NCONST)
            then(v.tensor_copy(ntype_f, ntype_i))
            for t in range(TYPES):
                then(v.tensor_scalar(tmask[:, t * NB:(t + 1) * NB], ntype_f, float(t), None, ALU.is_equal))
            then(v.tensor_scalar(onehot3, types_i, tcol, None, ALU.is_equal))
            for r in range(RELS):
                v.tensor_scalar(relk[:, r * P:(r + 1) * P], relk[:, r * P:(r + 1) * P], pri[:, r:r + 1],
                                DK ** -0.5, ALU.mult, ALU.mult)
            then(v.tensor_scalar(cols[:, 7:8], cols[:, 6:7], 1.0, None, ALU.add))
            dve.sem_inc(sem("masks_made"), 1)
            dve.wait_ge(sem("skip_gated"), 1)
            then(v.tensor_scalar(gate, tmask[:, 0:NB], skip_s[:, 0:1], None, ALU.mult))
            for t in range(1, TYPES):
                then(v.scalar_tensor_tensor(gate, tmask[:, t * NB:(t + 1) * NB], skip_s[:, t:t + 1], gate,
                                            ALU.mult, ALU.add))
            then(v.tensor_scalar(ungate, gate, -1.0, 1.0, ALU.mult, ALU.add))

            def mask_type(b, u, t):
                ins = v.tensor_scalar(xm[u][:, t * P:(t + 1) * P], X[:, bass.ds(b * P, P)],
                                      tmask[:, bass.ds(t * NB + b, 1)], None, ALU.mult)
                if t == TYPES - 1:
                    ins.then_inc(sem("xm_made"), 1)

            def node_types(b, u):
                v.tensor_scalar(types_s[:, u * P:(u + 1) * P], onehot3[:, bass.ds(b * P, P)], 0.0, None, ALU.add)

            def split_q(b, u, ahead):
                dve.wait_ge(sem("kvT_copied"), b + 1)
                q = bank[2 + u][:, 2 * P:3 * P]
                parts = [Qsplit[:, bass.ds(b * (3 * P) + j * P, P)] for j in range(3)]
                link.mark(v.tensor_scalar(parts[0], q, 0.0, None, ALU.add))
                if ahead is not None:
                    node_types(ahead, u)
                link.reach()
                link.mark(v.tensor_tensor(rest, q, parts[0], ALU.subtract))
                if ahead is not None:
                    mask_type(ahead, u, 0)
                link.reach()
                link.mark(v.tensor_scalar(parts[1], rest, 0.0, None, ALU.add))
                if ahead is not None:
                    mask_type(ahead, u, 1)
                link.reach()
                link.mark(v.tensor_tensor(parts[2], rest, parts[1], ALU.subtract))
                if ahead is not None:
                    mask_type(ahead, u, 2)
                link.reach()
                dve.sem_inc(sem("q_split"), 1)

            def copy_tabv(b, u):
                dve.wait_ge(sem("tab_made"), b + 1)
                dve.wait_ge(sem("tab_free"), b + 1)
                v.tensor_copy(tab_s[u].rearrange("p (r c) -> p r c", r=RELS)[:, :, P:2 * P],
                              bank[6 + u].rearrange("p (r c) -> p r c", r=RELS)).then_inc(sem("tabv_copied"), 1)

            def ids_and_keys(g):
                w = [W(j)[:, bass.ds(g * P, P)] for j in range(10)]
                v.tensor_scalar(w[5], w[2].bitcast(I32), 0.0, None, ALU.add)
                v.tensor_scalar(w[6], w[3].bitcast(I32), 0.0, None, ALU.add)
                then(v.tensor_scalar(w[7], w[4].bitcast(I32), 0.0, None, ALU.add))
                then(v.scalar_tensor_tensor(w[8], w[6], float(RELS), w[7], ALU.mult, ALU.add))
                then(v.tensor_scalar(w[7], w[5], small[:, bass.ds(2 * SG + g, 1)], None, ALU.subtract))
                then(v.tensor_scalar(w[0], w[7], 0.0, None, ALU.is_ge))
                then(v.scalar_tensor_tensor(w[0], w[7], float(P - 1), w[0], ALU.is_le, ALU.mult))

            def heads_and_ends(g):
                w = [W(j)[:, bass.ds(g * P, P)] for j in range(10)]
                then(v.tensor_tensor(W(9)[:, bass.ds(g * P + 1, P - 1)], W(5)[:, bass.ds(g * P + 1, P - 1)],
                                     W(5)[:, bass.ds(g * P, P - 1)], ALU.not_equal))
                v.tensor_scalar(w[4], w[9], -BIG, None, ALU.mult)
                v.tensor_tensor(w[3], w[5], w[9], ALU.mult)
                v.tensor_scalar(w[1], w[5], W(5)[:, bass.ds(g * P, 1)], None, ALU.is_equal)
                then(v.tensor_scalar(w[2], w[5], W(5)[:, bass.ds(g * P + P - 1, 1)], None, ALU.is_equal))
                then(v.scalar_tensor_tensor(w[2], w[1], 0.0, w[2], ALU.is_equal, ALU.mult))
                v.tensor_tensor(w[2], w[2], w[0], ALU.mult)
                then(v.tensor_tensor(w[1], w[1], w[0], ALU.mult))

            def table_loop(first, count, arrays):
                with dve.Fori(0, count) as i:
                    link.enter(i, 8 + (9 if arrays else 0))
                    for u in range(2):
                        b = 2 * (i + first) + u
                        split_q(b + 1, 1 - u, b + 3)
                        copy_tabv(b, u)
                        if arrays:
                            (ids_and_keys, heads_and_ends)[u](i)
                link.leave(count)

            dve.sem_inc(sem("q_split"), 2)
            dve.sem_inc(sem("tabv_copied"), 2)
            for b in range(2):
                node_types(b, b)
                for t in range(TYPES):
                    mask_type(b, b, t)
            split_q(0, 0, 2)
            looped = NK // 2 - 1
            along = min(SG, looped)
            if looped > along:
                table_loop(0, looped - along, False)
            dve.wait_ge(sem("rows_gathered"), 16 * 3 * SG)
            then(v.memset(W(9).rearrange("s (g e) -> s g e", e=P)[:, :, 0:1], 1.0))
            table_loop(looped - along, along, True)
            split_q(NK - 1, 1, None)
            copy_tabv(NK - 2, 0)
            split_q(NK, 0, None)
            copy_tabv(NK - 1, 1)
            copy_tabv(NK, 0)
            for g in range(along, SG):
                ids_and_keys(g)
                heads_and_ends(g)
            dve.sem_inc(sem("arrays_made"), 1)
            then(v.memset(pad_s, -1.0))
            dve.sem_inc(sem("pad_set"), 1)
            dve.wait_ge(sem("blk_turned"), 1)
            v.tensor_scalar(blkT, bank[4][0:SG, 0:P], float(NB - 1), None, ALU.min).then_inc(sem("blk_made"), 1)
            v.memset(acc, 0.0).then_inc(sem("acc_done"), RING)
            for g in range(SG):
                dve.wait_ge(sem("recb_turned"), g + 1)
                dve.wait_ge(sem("recs_free"), g + 1)
                to = rec_s[g % RECS].rearrange("e (k c s) -> e c k s", c=7, s=STEPS)
                of = bank[g % 2 * 2 + 1][:, 0:3 * P].rearrange("e (c k s) -> e c k s", c=3, s=STEPS)
                v.tensor_copy(to[:, C_HEADKEY], of[:, 0])
                v.tensor_copy(to[:, C_KVROW].bitcast(I32), of[:, 1])
                v.tensor_copy(to[:, C_SRC].bitcast(I32), of[:, 2]).then_inc(sem("recb_copied"), 1)

            def one_hot_quad(par, u, q, made):
                key = rec_col(u, C_KEY)[:, 4 * q:4 * q + 4]
                v.tensor_tensor(hot[:, (par * STEPS + 4 * q) * P:(par * STEPS + 4 * q + 4) * P]
                                .rearrange("e (t n) -> e t n", n=P),
                                iota_f.unsqueeze(1).to_broadcast([P, 4, P]), spread(key, P),
                                ALU.is_equal).then_inc(made, 1)

            def one_hot(par, u, made):
                for q in range(4):
                    one_hot_quad(par, u, q, made)

            dve.wait_ge(sem("rec_loaded0"), 16)
            dve.wait_ge(sem("recs_free"), RECS + SG)
            dve.wait_ge(sem("acc_done"), RING)
            one_hot(0, 0, sem("hot_made"))
            v.memset(ends, 0.0)
            v.memset(hot[:, STEPS * P:2 * STEPS * P], 0.0)
            v.memset(rows, 0.0).then_inc(sem("msg_ready"), 1)

            def add_sums(k, ts, regs):
                for t in ts:
                    dve.wait_ge(sem("acc_done"), RING + STEPS * k + t)
                    if t % 2 == 0:
                        dve.wait_ge(sem("sum_made"), STEPS * k + t + 2)
                    a = acc[:, bass.ds(regs[t] * SUMW, SUMW)]
                    v.tensor_tensor(a, bank[5 + t % RING // 2][:, t % 2 * 256:t % 2 * 256 + SUMW], a,
                                    ALU.add).then_inc(sem("acc_done"), 1)

            dve.wait_ge(sem("blk_loaded3"), 16)
            with dve.Fori(0, ROUNDS // SLOTS) as i:
                for u in range(SLOTS):
                    k = SLOTS * i + u
                    regs = load_regs(DVE_, blk_slot[u - 1], NB - 1)
                    dve.wait_ge(sem(f"kv_loaded{u}"), 16 * STEPS * (i + 1))
                    kv3 = kv_slot[u].rearrange("e (t c) -> e t c", c=2 * P)
                    pr = [prod[:, q * 512:q * 512 + 512] for q in range(2)]

                    def product(q):
                        dve.wait_ge(sem("q_spread"), 4 * k + q + 1)
                        v.tensor_tensor(pr[q % 2].rearrange("e (t c) -> e t c", c=P), kv3[:, 4 * q:4 * q + 4, 0:P],
                                        bank[Q_BANK[q]].rearrange("e (t c) -> e t c", c=P),
                                        ALU.mult).then_inc(sem("q_used"), 1)

                    def head_sums(q):
                        dve.wait_ge(sem("q_used"), 4 * k + q + 1)
                        v.tensor_reduce(att[:, q * 32:q * 32 + 32], pr[q % 2].rearrange("e (a d) -> e a d", d=DK),
                                        AX.X, ALU.add).then_inc(sem("att_made"), 1)

                    product(0)
                    product(1)
                    head_sums(0)
                    head_sums(1)
                    dve.wait_ge(sem("att_made"), 4 * k + 1)
                    product(2)
                    add_sums(k, (0,), regs)
                    head_sums(2)
                    add_sums(k, (1,), regs)
                    dve.wait_ge(sem("att_made"), 4 * k + 2)
                    product(3)
                    add_sums(k, (2,), regs)
                    head_sums(3)
                    add_sums(k, (3, 4), regs)
                    dve.wait_ge(sem("att_turned"), k + 1)
                    dve.wait_ge(sem(f"reset_loaded{u}"), 16 * (i + 1))
                    rs = reset_slot[u]
                    v.tensor_tensor_scan(fwd, rs[:, 0:P], bank[2][:, 0:P], -BIG, ALU.add, ALU.max).then_inc(sem("scanned"), 1)
                    add_sums(k, (5, 6), regs)
                    dve.wait_ge(sem("scanned"), 2 * k + 1)
                    v.tensor_tensor_scan(seg[:, ::-1], rs[:, P:0:-1], fwd[:, ::-1], -BIG, ALU.add,
                                         ALU.max).then_inc(sem("scanned"), 1)
                    add_sums(k, (7, 8), regs)
                    dve.wait_ge(sem("scanned"), 2 * k + 2)
                    v.tensor_tensor(shifted, bank[2][:, 0:P], seg, ALU.subtract).then_inc(sem("shift_made"), 1)
                    if u + 1 < SLOTS:
                        dve.wait_ge(sem(f"rec_loaded{u + 1}"), 16 * (i + 1))
                    else:
                        dve.wait_ge(sem("rec_loaded0"), 16 * (i + 2))
                    add_sums(k, (9,), regs)
                    for q in range(4):
                        dve.wait_ge(sem("sum_made"), STEPS * k + 4 * q + 4)
                        one_hot_quad((u + 1) % 2, (u + 1) % SLOTS, q, sem("hot_made"))
                        add_sums(k, ((10,), (11,), (12,), ())[q], regs)
                    dve.wait_ge(sem("ends_summed"), k + 1)
                    v.tensor_copy(ends[:, 0:511:34], rec_col(u, C_FIRST))
                    v.tensor_copy(ends[:, 1:512:34], rec_col(u, C_LAST))
                    v.tensor_copy(rows3[:, :, M_KEY], rec_col(u, C_HEADKEY))
                    add_sums(k, (13,), regs)
                    dve.wait_ge(sem("exp_done"), k + 1)
                    w3 = weight.rearrange("e (t h) -> e t h", h=HEADS)
                    v.tensor_tensor(rows3[:, :, M_MAX:M_MAX + HEADS],
                                    bank[2][:, 2 * P:3 * P].rearrange("e (t h) -> e t h", h=HEADS),
                                    spread(rec_col(u, C_HEAD), HEADS), ALU.mult)
                    v.tensor_copy(rows3[:, :, M_EXP:M_EXP + HEADS], w3)
                    dve.wait_ge(sem(f"blk_loaded{u}"), 16 * (i + 1))
                    for q in range(4):
                        tt = slice(4 * q, 4 * q + 4)
                        v.tensor_tensor(rows3[:, tt, 0:P].rearrange("e t (h d) -> e t h d", d=DK),
                                        kv3[:, tt, P:2 * P].rearrange("e t (h d) -> e t h d", d=DK),
                                        w3[:, tt].unsqueeze(3).to_broadcast([P, 4, HEADS, DK]),
                                        ALU.mult).then_inc(sem("msg_ready"), 1)
                        add_sums(k, ((), (14,), (15,), ())[q], regs)
            add_sums(ROUNDS, range(STEPS), load_regs(DVE_, blk_slot[SLOTS - 1], NB - 1))

            dve.wait_ge(sem("list_loaded"), 16)
            g8 = lambda a: a.rearrange("p (g h) -> p g h", h=HEADS)
            den = pl[:, :, M_EXP:M_EXP + HEADS]
            v.tensor_copy(g8(key8), pl[:, :, M_KEY:M_KEY + 1].to_broadcast([P, LG, HEADS]))
            then(v.tensor_scalar(g8(mval), den, 0.0, -BIG, ALU.is_equal, ALU.mult))
            then(v.tensor_tensor(g8(mval), g8(mval), pl[:, :, M_MAX:M_MAX + HEADS], ALU.add))
            dve.sem_inc(sem("keys_made"), 1)
            v.tensor_scalar(pl[:, :, M_MAX:M_MAX + 1], pl[:, :, M_EXP:M_EXP + 1], 0.0, None, ALU.is_gt)
            dve.wait_ge(sem("list_taken"), 2 * -(-LG // 4))
            then(v.tensor_tensor_scan(keyT, keyT, keyT, 0.0, ALU.max, ALU.max))
            dve.sem_inc(sem("keys_made"), 1)
            v.memset(resets2[:, 0:1], 1.0)
            v.memset(resets2[:, ENTRIES:ENTRIES + 1], 0.0)
            then(v.tensor_tensor(resets2[:, 1:ENTRIES], keyT[:, 1:ENTRIES], keyT[:, 0:ENTRIES - 1], ALU.not_equal))
            then(v.tensor_scalar(resets2, resets2, -BIG, None, ALU.mult))
            then(v.tensor_tensor_scan(seg2, resets2[:, 0:ENTRIES], mT, -BIG, ALU.add, ALU.max))
            then(v.tensor_tensor_scan(seg2[:, ::-1], resets2[:, ENTRIES:0:-1], seg2[:, ::-1], -BIG, ALU.add, ALU.max))
            v.tensor_tensor(mT, mT, seg2, ALU.subtract).then_inc(sem("mshift_made"), 1)
            dve.wait_ge(sem("patterns_made"), 5)
            v.tensor_copy(mstep_f, mtile_i)
            then(v.tensor_copy(mstart_f, mlast_i))
            mkeys = keyT[0:1, P - 1:(LG - 1) * P:P]
            then(v.tensor_copy(mlast_i, mkeys))
            then(v.tensor_scalar(mlast_i, mlast_i, 7, None, ALU.arith_shift_right))
            mc = mcount.rearrange("o (s g) -> o s g", g=LG - 1)
            then(v.tensor_copy(mblk_f[:, 0:LG - 1], mlast_i))
            then(v.tensor_tensor(mstart_f, mstart_f, mblk_f[:, 0:LG - 1], ALU.add))
            then(v.tensor_tensor(mc, mstart_f.unsqueeze(1).to_broadcast([1, MS, LG - 1]), spread(mstep_f, LG - 1), ALU.is_le))
            then(v.tensor_reduce(mtile_f, mc, AX.X, ALU.add))
            v.tensor_copy(mtile_i, mtile_f)
            then(v.tensor_tensor(mblk_f, mstep_f, mtile_f, ALU.subtract))
            v.tensor_scalar(mblk_i, mblk_f, float(NB - 1), None, ALU.min)
            then(v.tensor_scalar(mblk_f, mblk_f, float(P), None, ALU.mult))
            dve.sem_inc(sem("mblk_made"), 1)
            dve.wait_ge(sem("keys_back"), 1)
            then(v.tensor_copy(keyf, bank[1][:, 0:G8:HEADS]))
            dve.wait_ge(sem("mbase_spread"), 1)
            then(v.tensor_copy(mbase, bank[4][:, 0:MS]))
            dve.wait_ge(sem("factors_back"), 1)
            dve.sem_inc(sem("keys_merged"), 1)
            then(v.tensor_copy(factor, bank[0][:, 0:G8]))
            v.tensor_tensor(pl[:, :, 0:P].rearrange("p g (h d) -> p g h d", d=DK),
                            pl[:, :, 0:P].rearrange("p g (h d) -> p g h d", d=DK),
                            g8(factor).unsqueeze(3).to_broadcast([P, LG, HEADS, DK]), ALU.mult)
            then(v.tensor_tensor(den, den, g8(factor), ALU.mult))
            then(v.memset(acc2, 0.0))
            dve.sem_inc(sem("macc_done"), 1)
            with dve.Fori(0, MR) as i:
                rt = load_regs(DVE_, mtile_i[:, bass.ds(i * MERGES, MERGES)], LG - 1)
                rb = load_regs(DVE_, mblk_i[:, bass.ds(i * MERGES, MERGES)], NB - 1)
                for j in range(MERGES):
                    v.tensor_scalar(hot[:, j * P:(j + 1) * P], iota_f, mbase[:, bass.ds(i * MERGES + j, 1)],
                                    keyf[:, bass.ds(rt[j], 1)], ALU.add, ALU.is_equal).then_inc(sem("mhot_made"), 1)
                for j in range(MERGES):
                    dve.wait_ge(sem("macc_done"), MERGES * i + j + 1)
                    dve.wait_ge(sem("msum_made"), MERGES * (i + 1))
                    a = acc2[:, bass.ds(rb[j] * AW, AW)]
                    v.tensor_tensor(a, bank[2 + j // 3][:, j % 3 * AW:(j % 3 + 1) * AW], a,
                                    ALU.add).then_inc(sem("macc_done"), 1)

            dve.wait_ge(sem("macc_done"), MS + 1)
            dve.wait_ge(sem("types_loaded"), 16)
            if NPAD > N:
                then(v.memset(types2_i[:, N:NPAD], 0))
            then(v.tensor_scalar(onehot3b, types2_i, tcol, None, ALU.is_equal))

            def layer_norm(to, a, count):
                for b in range(EC):
                    last = v.bn_stats(stat[:, 6 * b:6 * b + 6], a[:, b])
                then(last)
                dve.sem_inc(sem("taken"), 1)
                for b in range(EC):
                    last = v.bn_aggr(stat[:, 6 * EC + 2 * b:6 * EC + 2 * b + 2], stat[:, 6 * b:6 * b + 6])
                then(last)
                root = stat[:, 6 * EC + 1:8 * EC:2]
                v.tensor_scalar(root, root, LN_EPS, None, ALU.add).then_inc(sem("var_made"), 1)
                dve.wait_ge(sem("root_made"), count)
                then(v.reciprocal(root, root))
                for b in range(EC):
                    last = v.tensor_scalar(to[:, b], a[:, b], stat[:, 6 * EC + 2 * b:6 * EC + 2 * b + 1],
                                           stat[:, 6 * EC + 2 * b + 1:6 * EC + 2 * b + 2], ALU.subtract, ALU.mult)
                then(last)

            f3, a3, r3, k3, s3 = by_block(fin, SUMW), by_block(aggr), by_block(res), by_block(kept), by_block(shift)

            def aggregate(i):
                rd = stat[:, 8 * EC:8 * EC + EC * HEADS]
                rd3 = rd.rearrange("p (b h) -> p b h", h=HEADS)
                dve.wait_ge(sem("fin_made"), i + 1)
                then(v.tensor_scalar(rd3, f3[:, :, P:SUMW], 1e-16, None, ALU.add))
                then(v.reciprocal(rd, rd))
                then(v.tensor_tensor(a3.rearrange("p b (h d) -> p b h d", d=DK),
                                     f3[:, :, 0:P].rearrange("p b (h d) -> p b h d", d=DK),
                                     rd3.unsqueeze(3).to_broadcast([P, EC, HEADS, DK]), ALU.mult))
                dve.sem_inc(sem("aggr_made"), 1)
                dve.sem_inc(sem("fin_used"), 1)
                then(v.tensor_scalar(types_s, onehot3b[:, bass.ds(i * EW, EW)], 0.0, None, ALU.add))
                dve.sem_inc(sem("types_made"), 1)

            def gain_types(i):
                v.tensor_scalar(types_n, onehot3b[:, bass.ds(i * EW, EW)], 0.0, None, ALU.add).then_inc(sem("gains_used"), 1)

            def update(i, more):
                dve.wait_ge(sem("trans_made"), i + 1)
                for n in range(2):
                    m = min(4, EC - 4 * n)
                    last = v.tensor_tensor(r3[:, 4 * n:4 * n + m], bank[n][:, 0:m * P].rearrange("p (b c) -> p b c", c=P),
                                           spread(gate[:, bass.ds(i * EC + 4 * n, m)], P), ALU.mult)
                then(last)
                dve.sem_inc(sem("trans_used"), 1)
                dve.wait_ge(sem("kept_made"), i + 1)
                then(v.tensor_tensor(r3, r3, k3, ALU.add))
                dve.sem_inc(sem("kept_used"), 1)
                if more:
                    aggregate(i + 1)
                layer_norm(r3, r3, 2 * i + 1)
                dve.wait_ge(sem("gains_made"), i + 1)
                for n in range(4):
                    m = min(2, EC - 2 * n)
                    gains = bank[2 + n][:, 0:m * 256].rearrange("p (b c) -> p b c", c=256)
                    v.tensor_tensor(r3[:, 2 * n:2 * n + m], r3[:, 2 * n:2 * n + m], gains[:, :, 0:P], ALU.mult)
                    last = v.tensor_tensor(s3[:, 2 * n:2 * n + m], blocks(X, i)[:, 2 * n:2 * n + m], gains[:, :, P:2 * P], ALU.add)
                then(last)
                if more:
                    gain_types(i + 1)
                then(v.tensor_tensor(r3, r3, s3, ALU.add))
                layer_norm(blocks(X, i), r3, 2 * i + 2)
                dve.sem_inc(sem("x1_made"), 1)

            then(v.tensor_scalar(keep, acc2.rearrange("p (b c) -> p b c", c=AW)[:, :, SUMW], 0.0, None, ALU.is_equal))
            dve.sem_inc(sem("fin_used"), 1)
            dve.sem_inc(sem("kept_used"), 1)
            dve.sem_inc(sem("trans_used"), 1)
            gain_types(0)
            aggregate(0)
            if NR > 1:
                with dve.Fori(0, NR - 1) as i:
                    link.enter(i, 16)
                    update(i, True)
                link.leave(NR - 1)
            update(NR - 1, False)

            dve.wait_ge(sem("agg_begun"), len(CH))
            dve.sem_inc(sem("agg_done"), STEPS)
            dve.wait_ge(sem("rec2_loaded0"), 16)
            one_hot(0, 0, sem("hot2_made"))
            with dve.Fori(0, ROUNDS // SLOTS) as i:
                for u in range(SLOTS):
                    k = SLOTS * i + u
                    if u + 1 < SLOTS:
                        dve.wait_ge(sem(f"rec2_loaded{u + 1}"), 16 * (i + 1))
                    else:
                        dve.wait_ge(sem("rec2_loaded0"), 16 * (i + 2))
                    dve.wait_ge(sem(f"blk2_loaded{u}"), 16 * (i + 1))
                    one_hot((u + 1) % 2, (u + 1) % SLOTS, sem("hot2_made"))
                    regs = load_regs(DVE_, blk_slot[u], NB - 1)
                    for t in range(STEPS):
                        dve.wait_ge(sem("agg_done"), STEPS * (k + 1) + t)
                        if t % 4 == 0:
                            dve.wait_ge(sem("agg_made"), STEPS * k + t + 4)
                        a = aggT[:, bass.ds(regs[t] * P, P)]
                        v.tensor_tensor(a, bank[t // 4][:, t % 4 * P:(t % 4 + 1) * P], a,
                                        ALU.add).then_inc(sem("agg_done"), 1)

            for m, y in ((0, y1), (1, y2)):
                for c, (lo, hi) in enumerate(CH):
                    dve.wait_ge(sem("lin_copied"), m * len(CH) + c + 1)
                    last = v.bn_stats(stat[:, 8 + 6 * c:14 + 6 * c], y[:, lo:min(hi, N)])
                then(last)
                then(v.bn_aggr(stat[:, 4:6], stat[:, 8:8 + 6 * len(CH)]))
                v.tensor_scalar(stat[:, 1:2], stat[:, 5:6], BN_EPS, None, ALU.add).then_inc(sem("var_made"), 1)
                dve.wait_ge(sem("root_made"), 2 * NR + m + 1)
                then(v.reciprocal(stat[:, 0:1], stat[:, 0:1]))
                then(v.tensor_tensor(stat[:, 2:3], stat[:, 0:1], cols[:, 3 * m + 1:3 * m + 2], ALU.mult))
                then(v.tensor_tensor(stat[:, 6:7], stat[:, 4:5], stat[:, 2:3], ALU.mult))
                v.tensor_tensor(stat[:, 3:4], cols[:, 3 * m + 2:3 * m + 3], stat[:, 6:7],
                                ALU.subtract).then_inc(sem("bscale_made"), 1)
                dve.wait_ge(sem("relu_done"), (m + 1) * len(CH))
            for c in range(NB // EC):
                xc = blocks(X, c)
                dve.wait_ge(sem("h2_turned"), c + 1)
                for n in range(2):
                    m = min(4, EC - 4 * n)
                    then(v.tensor_tensor(r3[:, 4 * n:4 * n + m],
                                         bank[c % 4 * 2 + n][:, 0:m * P].rearrange("p (b c) -> p b c", c=P),
                                         xc[:, 4 * n:4 * n + m], ALU.add))
                dve.sem_inc(sem("h2_used"), 1)
                then(v.tensor_tensor(r3, r3, xc, ALU.add))
                layer_norm(xc, r3, 2 * NR + 2 + c + 1)
                dve.sem_inc(sem("out_made"), 1)


_INS = ["x", "src", "dst", "edge_type_4", "node_type_3"] + ["L0_gnn_" + n for n in (
    "Wk", "bk", "Wq", "bq", "Wv", "bv", "Wa", "ba", "rel_pri", "rel_att", "rel_msg", "skip", "ln_g", "ln_b")] + [
    "L1_gnn_" + n for n in ("eps", "W1", "b1", "g1", "be1", "W2", "b2", "g2", "be2")]


def kernel(**inputs):
    import numpy as np
    import concourse.bacc as bacc
    from concourse.bass_utils import run_bass_kernel_spmd as run

    nc = bacc.Bacc("TRN2", target_bir_lowering=False, num_devices=1)
    arrays, args = {}, []
    for name in _INS:
        a = np.ascontiguousarray(inputs[name])
        if a.ndim == 0:
            a = a.reshape(1)
        arrays[f"in_{name}"] = a
        args.append(nc.dram_tensor(f"in_{name}", a.shape, mybir.dt.from_np(a.dtype), kind="ExternalInput").ap())
    out = nc.dram_tensor("out_x", tuple(inputs["x"].shape), F32, kind="ExternalOutput").ap()
    gnn_kernel(nc, *args, out)
    r = run(nc, [arrays], core_ids=[0])
    return r.results[0]["out_x"]
```
